# Optimizing a Trainium2 kernel written in Bass

```python
import numpy as np
import jax
import jax.numpy as jnp

def _softmax(x, axis=-1):
    return jax.nn.softmax(x, axis=axis)

def _gelu(x):
    return jax.nn.gelu(x, approximate=True)

def _silu(x):
    return jax.nn.silu(x)

def _sigmoid(x):
    return jax.nn.sigmoid(x)

def _layernorm(x, axis=-1, eps=1e-05):
    m = jnp.mean(x, axis=axis, keepdims=True)
    v = jnp.var(x, axis=axis, keepdims=True)
    return (x - m) / jnp.sqrt(v + eps)

def _scatter_add(tgt, idx, src, axis=0):
    return tgt.at[idx].add(src)

def _segment_sum(src, seg, n):
    return jax.ops.segment_sum(src, seg, n)
kernel_name = 'mk_xattn_ffn_d4_seqx_r8_3b9916'

def setup_inputs(seed: int=0):
    np.random.seed(seed)
    _w = jnp.asarray

    def _rec_inputs():
        import jax
        import jax.numpy as jnp
        _rk = jax.random.key(seed)
        x = -0.0002928 + 1 * jax.random.normal(jax.random.fold_in(_rk, 1), (8, 128, 128), jnp.float32)
        _lenS = 128 - jax.random.randint(jax.random.fold_in(_rk, 7), (8,), 0, max(1, 128 // 4) + 1, jnp.int32)
        _lenS2 = 128 - jax.random.randint(jax.random.fold_in(_rk, 8), (8,), 0, max(1, 128 // 4) + 1, jnp.int32)
        _ctx_1024P = jax.random.normal(jax.random.fold_in(_rk, 11), (8, 16, 128), jnp.float32)
        _ctx_1024c = jax.random.dirichlet(jax.random.fold_in(_rk, 511), 0.3 * jnp.ones((16,), jnp.float32), (8, 128))
        _ctx_1024t = jnp.einsum('bsk,bkd->bsd', _ctx_1024c, _ctx_1024P)
        _ctx_1024t = _ctx_1024t * jax.lax.rsqrt(jnp.mean(jnp.square(_ctx_1024t)) + 1e-12) * 0.953939
        ctx_1024 = -1.39393e-06 + 0.999914 * (_ctx_1024t + 0.3 * jax.random.normal(jax.random.fold_in(_rk, 611), (8, 128, 128), jnp.float32))
        _validS = jnp.arange(128)[None, :] < _lenS[:, None]
        _validS2 = jnp.arange(128)[None, :] < _lenS2[:, None]
        _causal = jnp.tril(jnp.ones((128, 128), dtype=bool))
        mask_Bx1xSxS2_ik1 = jnp.where(jnp.broadcast_to(_validS2[:, None, None, :], (8, 1, 128, 128)), 1, 0).astype(jnp.int32)
        return (x, ctx_1024, mask_Bx1xSxS2_ik1)
    x, ctx_1024, mask_Bx1xSxS2_ik1 = _rec_inputs()

    def _L0_xattn_setup():
        import jax, jax.numpy as jnp
        import numpy as np
        D_MODEL = 128
        NUM_HEADS = 16
        B, S = (2, 256)
        key = jax.random.key(seed)
        ks = jax.random.split(key, 11)
        scale = 1.0 / np.sqrt(D_MODEL)
        inp = {'q': jax.random.normal(ks[0], (B, S, D_MODEL), jnp.float32), 'k': jax.random.normal(ks[1], (B, S, D_MODEL), jnp.float32), 'v': jax.random.normal(ks[2], (B, S, D_MODEL), jnp.float32), 'w_q': jax.random.normal(ks[3], (D_MODEL, D_MODEL), jnp.float32) * scale, 'b_q': jax.random.normal(ks[4], (D_MODEL,), jnp.float32) * 0.01, 'w_k': jax.random.normal(ks[5], (D_MODEL, D_MODEL), jnp.float32) * scale, 'b_k': jax.random.normal(ks[6], (D_MODEL,), jnp.float32) * 0.01, 'w_v': jax.random.normal(ks[7], (D_MODEL, D_MODEL), jnp.float32) * scale, 'b_v': jax.random.normal(ks[8], (D_MODEL,), jnp.float32) * 0.01, 'w_o': jax.random.normal(ks[9], (D_MODEL, D_MODEL), jnp.float32) * scale, 'b_o': jax.random.normal(ks[10], (D_MODEL,), jnp.float32) * 0.01}
        return inp
    _L0_xattn_all = _L0_xattn_setup()
    _L0_xattn_in = {k: v for k, v in _L0_xattn_all.items() if k in ('w_q', 'b_q', 'w_k', 'b_k', 'w_v', 'b_v', 'w_o', 'b_o')}
    del _L0_xattn_all

    def _L0_ffn_setup():
        import jax, jax.numpy as jnp
        import numpy as np
        H, I, E_ROUTED, TOP_K = (128, 352, 7, 2)
        B, S = (4, 256)

        def _expert(h, g, u, d):
            return jnp.einsum('...i,hi->...h', jax.nn.silu(h @ g.T) * (h @ u.T), d)
        key = jax.random.key(seed)
        ks = jax.random.split(key, 10)
        sc = 0.02
        return {'x': jax.random.normal(ks[0], (B, S, H), dtype=jnp.float32), 'sg': jax.random.normal(ks[1], (I, H), dtype=jnp.float32) * sc, 'su': jax.random.normal(ks[2], (I, H), dtype=jnp.float32) * sc, 'sd': jax.random.normal(ks[3], (H, I), dtype=jnp.float32) * sc, 'rg': jax.random.normal(ks[4], (E_ROUTED, I, H), dtype=jnp.float32) * sc, 'ru': jax.random.normal(ks[5], (E_ROUTED, I, H), dtype=jnp.float32) * sc, 'rd': jax.random.normal(ks[6], (E_ROUTED, H, I), dtype=jnp.float32) * sc, 'wr': jax.random.normal(ks[7], (E_ROUTED, H), dtype=jnp.float32) * sc, 'rb': jnp.zeros((E_ROUTED,), dtype=jnp.float32)}
    _L0_ffn_all = _L0_ffn_setup()
    _L0_ffn_in = {k: v for k, v in _L0_ffn_all.items() if k in ('sg', 'su', 'sd', 'rg', 'ru', 'rd', 'wr', 'rb')}
    del _L0_ffn_all

    def _L1_xattn_setup():
        import jax, jax.numpy as jnp
        import numpy as np
        HEADS = 16
        NEG_INF = -1e+20
        key = jax.random.key(seed)
        ks = jax.random.split(key, 10)
        N, S, E = (4, 256, 128)
        D = E // HEADS
        inp = {'values': jax.random.normal(ks[0], (N, S, E), dtype=jnp.float32), 'keys': jax.random.normal(ks[1], (N, S, E), dtype=jnp.float32), 'query': jax.random.normal(ks[2], (N, S, E), dtype=jnp.float32), 'mask': jax.random.randint(ks[3], (N, 1, S, S), 0, 2, dtype=jnp.int32), 'Wv': jax.random.normal(ks[4], (D, D), dtype=jnp.float32) / np.sqrt(D), 'Wk': jax.random.normal(ks[5], (D, D), dtype=jnp.float32) / np.sqrt(D), 'Wq': jax.random.normal(ks[6], (D, D), dtype=jnp.float32) / np.sqrt(D), 'Wo': jax.random.normal(ks[7], (E, E), dtype=jnp.float32) / np.sqrt(E), 'bo': jax.random.normal(ks[8], (E,), dtype=jnp.float32) * 0.01}
        return inp
    _L1_xattn_all = _L1_xattn_setup()
    _L1_xattn_in = {k: v for k, v in _L1_xattn_all.items() if k in ('Wv', 'Wk', 'Wq', 'Wo', 'bo')}
    del _L1_xattn_all

    def _L1_ffn_setup():
        import jax, jax.numpy as jnp
        import numpy as np
        D_MODEL = 128
        HIDDEN = 512
        NUM_EXPERTS = 8
        TOP_K = 2
        DEPTH = 12
        DEPTH_SCALE = 1.0 / np.sqrt(DEPTH)
        key = jax.random.key(seed)
        k_x, k_r, k_g, k_u, k_d = jax.random.split(key, 5)
        s_in = 1.0 / np.sqrt(D_MODEL)
        s_hid = 1.0 / np.sqrt(HIDDEN)
        return {'x': jax.random.normal(k_x, (2, 256, D_MODEL), dtype=jnp.float32), 'Wr': jax.random.normal(k_r, (D_MODEL, NUM_EXPERTS), dtype=jnp.float32) * s_in, 'Wg': jax.random.normal(k_g, (NUM_EXPERTS, D_MODEL, HIDDEN), dtype=jnp.float32) * s_in, 'Wu': jax.random.normal(k_u, (NUM_EXPERTS, D_MODEL, HIDDEN), dtype=jnp.float32) * s_in, 'Wd': jax.random.normal(k_d, (NUM_EXPERTS, HIDDEN, D_MODEL), dtype=jnp.float32) * s_hid}
    _L1_ffn_all = _L1_ffn_setup()
    _L1_ffn_in = {k: v for k, v in _L1_ffn_all.items() if k in ('Wr', 'Wg', 'Wu', 'Wd')}
    del _L1_ffn_all

    def _L2_xattn_setup():
        import jax, jax.numpy as jnp
        import numpy as np
        EMBED_PHI = 128
        EMBED_F = 128
        HIDDEN_F = 128
        N_HEADS = 16
        B, S = (2, 256)
        key = jax.random.key(seed)
        ks = jax.random.split(key, 9)
        sphi = 1.0 / np.sqrt(EMBED_PHI)
        sf = 1.0 / np.sqrt(EMBED_F)
        sh = 1.0 / np.sqrt(HIDDEN_F)
        return {'q': jax.random.normal(ks[0], (B, S, EMBED_PHI), jnp.float32), 'k': jax.random.normal(ks[1], (B, S, EMBED_PHI), jnp.float32), 'v': jax.random.normal(ks[2], (B, S, EMBED_F), jnp.float32), 'Wq': jax.random.normal(ks[3], (HIDDEN_F, EMBED_PHI), jnp.float32) * sphi, 'Wk': jax.random.normal(ks[4], (HIDDEN_F, EMBED_PHI), jnp.float32) * sphi, 'Wv': jax.random.normal(ks[5], (HIDDEN_F, EMBED_F), jnp.float32) * sf, 'bv': jax.random.normal(ks[6], (HIDDEN_F,), jnp.float32) * sf, 'Wo': jax.random.normal(ks[7], (EMBED_F, HIDDEN_F), jnp.float32) * sh, 'bo': jax.random.normal(ks[8], (EMBED_F,), jnp.float32) * sh}
    _L2_xattn_all = _L2_xattn_setup()
    _L2_xattn_in = {k: v for k, v in _L2_xattn_all.items() if k in ('Wq', 'Wk', 'Wv', 'bv', 'Wo', 'bo')}
    del _L2_xattn_all

    def _L2_ffn_setup():
        import jax, jax.numpy as jnp
        import numpy as np
        D = 128
        N_EXP = 8
        TOP_K = 1
        key = jax.random.key(seed)
        ks = jax.random.split(key, 7)
        s = 0.02
        return {'x': jax.random.normal(ks[0], (4, 256, D), jnp.float32), 'gate_w': jax.random.normal(ks[1], (D, N_EXP), jnp.float32) * s, 'gate_b': jnp.zeros((N_EXP,), jnp.float32), 'w1': jax.random.normal(ks[2], (N_EXP, D, 4 * D), jnp.float32) * s, 'b1': jnp.zeros((N_EXP, 4 * D), jnp.float32), 'w2': jax.random.normal(ks[3], (N_EXP, 4 * D, D), jnp.float32) * s, 'b2': jnp.zeros((N_EXP, D), jnp.float32)}
    _L2_ffn_all = _L2_ffn_setup()
    _L2_ffn_in = {k: v for k, v in _L2_ffn_all.items() if k in ('gate_w', 'gate_b', 'w1', 'b1', 'w2', 'b2')}
    del _L2_ffn_all

    def _L3_xattn_setup():
        import jax, jax.numpy as jnp
        import numpy as np
        B, NT, NM, C, H, FF = (8, 128, 256, 128, 8, 512)

        def _ln(x, g, b):
            m = x.mean(-1, keepdims=True)
            v = jnp.mean((x - m) ** 2, axis=-1, keepdims=True)
            return (x - m) / jnp.sqrt(v + 1e-05) * g + b
        key = jax.random.key(seed)
        ks = jax.random.split(key, 8)
        w = lambda k, shape, s=0.02: jax.random.normal(k, shape, dtype=jnp.float32) * s
        return {'tgt': jax.random.normal(ks[0], (B, NT, C), dtype=jnp.float32), 'memory': jax.random.normal(ks[1], (B, NM, C), dtype=jnp.float32), 'qkv_w': w(ks[2], (3 * C, C)), 'qkv_b': jnp.zeros((3 * C,), jnp.float32), 'sa_out_w': w(ks[3], (C, C)), 'sa_out_b': jnp.zeros((C,), jnp.float32), 'in_proj_w': w(ks[4], (3 * C, C)), 'in_proj_b': jnp.zeros((3 * C,), jnp.float32), 'mha_out_w': w(ks[5], (C, C)), 'mha_out_b': jnp.zeros((C,), jnp.float32), 'lin1_w': w(ks[6], (FF, C)), 'lin1_b': jnp.zeros((FF,), jnp.float32), 'lin2_w': w(ks[7], (C, FF)), 'lin2_b': jnp.zeros((C,), jnp.float32), 'ln1_g': jnp.ones((C,), jnp.float32), 'ln1_b': jnp.zeros((C,), jnp.float32), 'ln2_g': jnp.ones((C,), jnp.float32), 'ln2_b': jnp.zeros((C,), jnp.float32), 'ln3_g': jnp.ones((C,), jnp.float32), 'ln3_b': jnp.zeros((C,), jnp.float32)}
    _L3_xattn_all = _L3_xattn_setup()
    _L3_xattn_in = {k: v for k, v in _L3_xattn_all.items() if k in ('qkv_w', 'qkv_b', 'sa_out_w', 'sa_out_b', 'in_proj_w', 'in_proj_b', 'mha_out_w', 'mha_out_b', 'lin1_w', 'lin1_b', 'lin2_w', 'lin2_b', 'ln1_g', 'ln1_b', 'ln2_g', 'ln2_b', 'ln3_g', 'ln3_b')}
    del _L3_xattn_all

    def _L3_ffn_setup():
        import jax, jax.numpy as jnp
        import numpy as np
        HIDDEN = 128
        NUM_EXPERTS = 8
        TOP_K = 2
        key = jax.random.key(seed)
        k_x, k_r, k_w1, k_w2 = jax.random.split(key, 4)
        x = jax.random.normal(k_x, (4, 256, HIDDEN), dtype=jnp.float32)
        router_w = jax.random.normal(k_r, (NUM_EXPERTS, HIDDEN), dtype=jnp.float32) * HIDDEN ** (-0.5)
        w1 = jax.random.normal(k_w1, (NUM_EXPERTS, HIDDEN, 2 * HIDDEN), dtype=jnp.float32) * HIDDEN ** (-0.5)
        w2 = jax.random.normal(k_w2, (NUM_EXPERTS, 2 * HIDDEN, HIDDEN), dtype=jnp.float32) * (2 * HIDDEN) ** (-0.5)
        return {'x': x, 'router_w': router_w, 'w1': w1, 'w2': w2}
    _L3_ffn_all = _L3_ffn_setup()
    _L3_ffn_in = {k: v for k, v in _L3_ffn_all.items() if k in ('router_w', 'w1', 'w2')}
    del _L3_ffn_all
    return {'x': x, 'ctx_1024': ctx_1024, 'mask_Bx1xSxS2_ik1': mask_Bx1xSxS2_ik1, 'L0_xattn_w_q': _L0_xattn_in['w_q'], 'L0_xattn_b_q': _L0_xattn_in['b_q'], 'L0_xattn_w_k': _L0_xattn_in['w_k'], 'L0_xattn_b_k': _L0_xattn_in['b_k'], 'L0_xattn_w_v': _L0_xattn_in['w_v'], 'L0_xattn_b_v': _L0_xattn_in['b_v'], 'L0_xattn_w_o': _L0_xattn_in['w_o'], 'L0_xattn_b_o': _L0_xattn_in['b_o'], 'L0_ffn_sg': _L0_ffn_in['sg'], 'L0_ffn_su': _L0_ffn_in['su'], 'L0_ffn_sd': _L0_ffn_in['sd'], 'L0_ffn_rg': _L0_ffn_in['rg'], 'L0_ffn_ru': _L0_ffn_in['ru'], 'L0_ffn_rd': _L0_ffn_in['rd'], 'L0_ffn_wr': _L0_ffn_in['wr'], 'L0_ffn_rb': _L0_ffn_in['rb'], 'L1_xattn_Wv': _L1_xattn_in['Wv'], 'L1_xattn_Wk': _L1_xattn_in['Wk'], 'L1_xattn_Wq': _L1_xattn_in['Wq'], 'L1_xattn_Wo': _L1_xattn_in['Wo'], 'L1_xattn_bo': _L1_xattn_in['bo'], 'L1_ffn_Wr': _L1_ffn_in['Wr'], 'L1_ffn_Wg': _L1_ffn_in['Wg'], 'L1_ffn_Wu': _L1_ffn_in['Wu'], 'L1_ffn_Wd': _L1_ffn_in['Wd'], 'L2_xattn_Wq': _L2_xattn_in['Wq'], 'L2_xattn_Wk': _L2_xattn_in['Wk'], 'L2_xattn_Wv': _L2_xattn_in['Wv'], 'L2_xattn_bv': _L2_xattn_in['bv'], 'L2_xattn_Wo': _L2_xattn_in['Wo'], 'L2_xattn_bo': _L2_xattn_in['bo'], 'L2_ffn_gate_w': _L2_ffn_in['gate_w'], 'L2_ffn_gate_b': _L2_ffn_in['gate_b'], 'L2_ffn_w1': _L2_ffn_in['w1'], 'L2_ffn_b1': _L2_ffn_in['b1'], 'L2_ffn_w2': _L2_ffn_in['w2'], 'L2_ffn_b2': _L2_ffn_in['b2'], 'L3_xattn_qkv_w': _L3_xattn_in['qkv_w'], 'L3_xattn_qkv_b': _L3_xattn_in['qkv_b'], 'L3_xattn_sa_out_w': _L3_xattn_in['sa_out_w'], 'L3_xattn_sa_out_b': _L3_xattn_in['sa_out_b'], 'L3_xattn_in_proj_w': _L3_xattn_in['in_proj_w'], 'L3_xattn_in_proj_b': _L3_xattn_in['in_proj_b'], 'L3_xattn_mha_out_w': _L3_xattn_in['mha_out_w'], 'L3_xattn_mha_out_b': _L3_xattn_in['mha_out_b'], 'L3_xattn_lin1_w': _L3_xattn_in['lin1_w'], 'L3_xattn_lin1_b': _L3_xattn_in['lin1_b'], 'L3_xattn_lin2_w': _L3_xattn_in['lin2_w'], 'L3_xattn_lin2_b': _L3_xattn_in['lin2_b'], 'L3_xattn_ln1_g': _L3_xattn_in['ln1_g'], 'L3_xattn_ln1_b': _L3_xattn_in['ln1_b'], 'L3_xattn_ln2_g': _L3_xattn_in['ln2_g'], 'L3_xattn_ln2_b': _L3_xattn_in['ln2_b'], 'L3_xattn_ln3_g': _L3_xattn_in['ln3_g'], 'L3_xattn_ln3_b': _L3_xattn_in['ln3_b'], 'L3_ffn_router_w': _L3_ffn_in['router_w'], 'L3_ffn_w1': _L3_ffn_in['w1'], 'L3_ffn_w2': _L3_ffn_in['w2']}

def reference(x, ctx_1024, mask_Bx1xSxS2_ik1, L0_xattn_w_q, L0_xattn_b_q, L0_xattn_w_k, L0_xattn_b_k, L0_xattn_w_v, L0_xattn_b_v, L0_xattn_w_o, L0_xattn_b_o, L0_ffn_sg, L0_ffn_su, L0_ffn_sd, L0_ffn_rg, L0_ffn_ru, L0_ffn_rd, L0_ffn_wr, L0_ffn_rb, L1_xattn_Wv, L1_xattn_Wk, L1_xattn_Wq, L1_xattn_Wo, L1_xattn_bo, L1_ffn_Wr, L1_ffn_Wg, L1_ffn_Wu, L1_ffn_Wd, L2_xattn_Wq, L2_xattn_Wk, L2_xattn_Wv, L2_xattn_bv, L2_xattn_Wo, L2_xattn_bo, L2_ffn_gate_w, L2_ffn_gate_b, L2_ffn_w1, L2_ffn_b1, L2_ffn_w2, L2_ffn_b2, L3_xattn_qkv_w, L3_xattn_qkv_b, L3_xattn_sa_out_w, L3_xattn_sa_out_b, L3_xattn_in_proj_w, L3_xattn_in_proj_b, L3_xattn_mha_out_w, L3_xattn_mha_out_b, L3_xattn_lin1_w, L3_xattn_lin1_b, L3_xattn_lin2_w, L3_xattn_lin2_b, L3_xattn_ln1_g, L3_xattn_ln1_b, L3_xattn_ln2_g, L3_xattn_ln2_b, L3_xattn_ln3_g, L3_xattn_ln3_b, L3_ffn_router_w, L3_ffn_w1, L3_ffn_w2):
    import jax
    import jax.numpy as jnp

    def _L0_xattn_ref(q, k, v, w_q, b_q, w_k, b_k, w_v, b_v, w_o, b_o):
        import jax, jax.numpy as jnp
        import numpy as np
        D_MODEL = 128
        NUM_HEADS = 16
        B, S = (2, 256)
        Bq, Sq, D = q.shape
        H = NUM_HEADS
        dh = D // H
        query = q @ w_q + b_q
        key = k @ w_k + b_k
        value = v @ w_v + b_v
        query = query.reshape(Bq, Sq, H, dh).transpose(0, 2, 1, 3)
        key = key.reshape(Bq, -1, H, dh).transpose(0, 2, 1, 3)
        value = value.reshape(Bq, -1, H, dh).transpose(0, 2, 1, 3)
        scores = jnp.einsum('bhqd,bhkd->bhqk', query, key)
        causal_mask = jnp.triu(jnp.ones((Sq, Sq), dtype=bool), k=1)
        scores = jnp.where(causal_mask[None, None], -jnp.inf, scores)
        attn = jax.nn.softmax(scores, axis=-1)
        data = jnp.einsum('bhqk,bhkd->bhqd', attn, value)
        data = data.transpose(1, 0, 2, 3).reshape(Bq, Sq, -1)
        return data @ w_o + b_o

    def _L0_ffn_ref(x, sg, su, sd, rg, ru, rd, wr, rb):
        import jax, jax.numpy as jnp
        import numpy as np
        H, I, E_ROUTED, TOP_K = (128, 352, 7, 2)
        B, S = (4, 256)

        def _expert(h, g, u, d):
            return jnp.einsum('...i,hi->...h', jax.nn.silu(h @ g.T) * (h @ u.T), d)
        shared_out = _expert(x, sg, su, sd)
        logits = x @ wr.T + rb
        probs = jax.nn.softmax(logits, axis=-1)
        scores, idx = jax.lax.top_k(probs, TOP_K)
        scores = scores / scores.sum(axis=-1, keepdims=True)
        w = jnp.sum(scores[..., None] * jax.nn.one_hot(idx, E_ROUTED, dtype=x.dtype), axis=-2)
        out = shared_out
        for e in range(E_ROUTED):
            out = out + w[..., e:e + 1] * _expert(x, rg[e], ru[e], rd[e])
        return out

    def _L1_xattn_ref(values, keys, query, mask, Wv, Wk, Wq, Wo, bo):
        import jax, jax.numpy as jnp
        import numpy as np
        HEADS = 16
        NEG_INF = -1e+20
        N, S, E = query.shape
        H = HEADS
        D = E // H
        v = jnp.einsum('nshd,ed->nshe', values.reshape(N, S, H, D), Wv)
        k = jnp.einsum('nshd,ed->nshe', keys.reshape(N, S, H, D), Wk)
        q = jnp.einsum('nshd,ed->nshe', query.reshape(N, S, H, D), Wq)
        energy = jnp.einsum('nqhd,nkhd->nhqk', q, k)
        energy = jnp.where(mask == 0, jnp.float32(NEG_INF), energy)
        attn = jax.nn.softmax(energy / jnp.sqrt(jnp.float32(E)), axis=3)
        out = jnp.einsum('nhqk,nkhd->nqhd', attn, v).reshape(N, S, E)
        return out @ Wo.T + bo

    def _L1_ffn_ref(x, Wr, Wg, Wu, Wd):
        import jax, jax.numpy as jnp
        import numpy as np
        D_MODEL = 128
        HIDDEN = 512
        NUM_EXPERTS = 8
        TOP_K = 2
        DEPTH = 12
        DEPTH_SCALE = 1.0 / np.sqrt(DEPTH)
        B, T, C = x.shape
        flat_x = x.reshape(-1, C)
        logits = flat_x @ Wr
        top_vals, top_idx = jax.lax.top_k(logits, TOP_K)
        rw = jax.nn.softmax(top_vals.astype(jnp.float32), axis=-1).astype(x.dtype)
        combine = jnp.sum(rw[..., None] * jax.nn.one_hot(top_idx, NUM_EXPERTS, dtype=x.dtype), axis=1)
        g = jnp.einsum('nc,ech->neh', flat_x, Wg)
        u = jnp.einsum('nc,ech->neh', flat_x, Wu)
        h = jax.nn.silu(g) * u
        eo = jnp.einsum('neh,ehc->nec', h, Wd) * DEPTH_SCALE
        out = jnp.einsum('ne,nec->nc', combine, eo)
        return out.reshape(B, T, C)

    def _L2_xattn_ref(q, k, v, Wq, Wk, Wv, bv, Wo, bo):
        import jax, jax.numpy as jnp
        import numpy as np
        EMBED_PHI = 128
        EMBED_F = 128
        HIDDEN_F = 128
        N_HEADS = 16
        B, S = (2, 256)
        Bq, Sq, _ = q.shape
        hd = HIDDEN_F // N_HEADS
        scale = 1.0 / np.sqrt(hd)
        qh = (q @ Wq.T).reshape(Bq, Sq, N_HEADS, hd).transpose(0, 2, 1, 3)
        kh = (k @ Wk.T).reshape(Bq, Sq, N_HEADS, hd).transpose(0, 2, 1, 3)
        vh = (v @ Wv.T + bv).reshape(Bq, Sq, N_HEADS, hd).transpose(0, 2, 1, 3)
        scores = jnp.einsum('bhsd,bhtd->bhst', qh, kh) * scale
        mask = jnp.triu(jnp.ones((Sq, Sq), dtype=bool), k=0).at[0, 0].set(False)
        scores = jnp.where(mask, -jnp.inf, scores)
        probs = jax.nn.softmax(scores, axis=-1)
        out = jnp.einsum('bhst,bhtd->bhsd', probs, vh)
        out = out.transpose(0, 2, 1, 3).reshape(Bq, Sq, HIDDEN_F)
        return out @ Wo.T + bo

    def _L2_ffn_ref(x, gate_w, gate_b, w1, b1, w2, b2):
        import jax, jax.numpy as jnp
        import numpy as np
        D = 128
        N_EXP = 8
        TOP_K = 1
        b, s, d = x.shape
        xf = x.reshape(-1, d)
        logits = xf @ gate_w + gate_b
        pb = jax.nn.softmax(logits, axis=-1)
        _, idx = jax.lax.top_k(pb, TOP_K)
        sel = jnp.any(idx[:, :, None] == jnp.arange(N_EXP)[None, None, :], axis=1)
        weights = pb * sel

        def expert_step(acc, params):
            w1e, b1e, w2e, b2e, wgt = params
            h = jax.nn.gelu(xf @ w1e + b1e, approximate=False)
            y = h @ w2e + b2e
            return (acc + wgt[:, None] * y, None)
        out0 = jnp.zeros_like(xf)
        out, _ = jax.lax.scan(expert_step, out0, (w1, b1, w2, b2, weights.T))
        return out.reshape(b, s, d)

    def _L3_xattn_ref(tgt, memory, qkv_w, qkv_b, sa_out_w, sa_out_b, in_proj_w, in_proj_b, mha_out_w, mha_out_b, lin1_w, lin1_b, lin2_w, lin2_b, ln1_g, ln1_b, ln2_g, ln2_b, ln3_g, ln3_b):
        import jax, jax.numpy as jnp
        import numpy as np
        B, NT, NM, C, H, FF = (8, 128, 256, 128, 8, 512)

        def _ln(x, g, b):
            m = x.mean(-1, keepdims=True)
            v = jnp.mean((x - m) ** 2, axis=-1, keepdims=True)
            return (x - m) / jnp.sqrt(v + 1e-05) * g + b
        Bx, N, Cx = tgt.shape
        qkv = tgt @ qkv_w.T + qkv_b
        q, k, v = jnp.split(qkv, 3, axis=-1)
        scores = jnp.einsum('bnc,bmc->bnm', q, k) * jnp.sqrt(jnp.float32(Cx))
        diag = jnp.eye(N, dtype=bool)
        scores = jnp.where(diag[None, :, :], scores, -jnp.inf)
        attn = jax.nn.softmax(scores, axis=-1)
        sa = jnp.einsum('bnm,bmc->bnc', attn, v) @ sa_out_w.T + sa_out_b
        x = _ln(tgt + sa, ln1_g, ln1_b)
        d = Cx // H
        wq, wk, wv = jnp.split(in_proj_w, 3, axis=0)
        bq, bk, bv = jnp.split(in_proj_b, 3, axis=0)
        qh = (x @ wq.T + bq).reshape(Bx, N, H, d).transpose(0, 2, 1, 3)
        kh = (memory @ wk.T + bk).reshape(Bx, -1, H, d).transpose(0, 2, 1, 3)
        vh = (memory @ wv.T + bv).reshape(Bx, -1, H, d).transpose(0, 2, 1, 3)
        a = jax.nn.softmax(jnp.einsum('bhnd,bhmd->bhnm', qh, kh) / jnp.sqrt(jnp.float32(d)), axis=-1)
        ca = jnp.einsum('bhnm,bhmd->bhnd', a, vh).transpose(0, 2, 1, 3).reshape(Bx, N, Cx)
        ca = ca @ mha_out_w.T + mha_out_b
        x = _ln(x + ca, ln2_g, ln2_b)
        ff = jax.nn.relu(x @ lin1_w.T + lin1_b) @ lin2_w.T + lin2_b
        return _ln(x + ff, ln3_g, ln3_b)

    def _L3_ffn_ref(x, router_w, w1, w2):
        import jax, jax.numpy as jnp
        import numpy as np
        HIDDEN = 128
        NUM_EXPERTS = 8
        TOP_K = 2
        bsz, seq, hidden = x.shape
        tokens = x.reshape(-1, hidden)
        logits = tokens @ router_w.T
        topk_vals, topk_idx = jax.lax.top_k(logits, TOP_K)
        weights = jax.nn.softmax(topk_vals, axis=-1)
        h = jnp.einsum('td,edf->etf', tokens, w1)
        h = jax.nn.gelu(h, approximate=False)
        out_all = jnp.einsum('etf,efd->etd', h, w2)
        out_ted = jnp.transpose(out_all, (1, 0, 2))
        gathered = jnp.take_along_axis(out_ted, topk_idx[:, :, None], axis=1)
        output = jnp.sum(weights[:, :, None] * gathered, axis=1)
        return output.reshape(bsz, seq, hidden)
    x = x + _L0_xattn_ref(_layernorm(x, axis=-1), ctx_1024, ctx_1024, L0_xattn_w_q, L0_xattn_b_q, L0_xattn_w_k, L0_xattn_b_k, L0_xattn_w_v, L0_xattn_b_v, L0_xattn_w_o, L0_xattn_b_o)
    x = x + _L0_ffn_ref(_layernorm(x, axis=-1), L0_ffn_sg, L0_ffn_su, L0_ffn_sd, L0_ffn_rg, L0_ffn_ru, L0_ffn_rd, L0_ffn_wr, L0_ffn_rb)
    x = x + _L1_xattn_ref(ctx_1024, ctx_1024, _layernorm(x, axis=-1), mask_Bx1xSxS2_ik1, L1_xattn_Wv, L1_xattn_Wk, L1_xattn_Wq, L1_xattn_Wo, L1_xattn_bo)
    x = x + _L1_ffn_ref(_layernorm(x, axis=-1), L1_ffn_Wr, L1_ffn_Wg, L1_ffn_Wu, L1_ffn_Wd)
    x = x + _L2_xattn_ref(_layernorm(x, axis=-1), ctx_1024, ctx_1024, L2_xattn_Wq, L2_xattn_Wk, L2_xattn_Wv, L2_xattn_bv, L2_xattn_Wo, L2_xattn_bo)
    x = x + _L2_ffn_ref(_layernorm(x, axis=-1), L2_ffn_gate_w, L2_ffn_gate_b, L2_ffn_w1, L2_ffn_b1, L2_ffn_w2, L2_ffn_b2)
    x = x + _L3_xattn_ref(_layernorm(x, axis=-1), ctx_1024, L3_xattn_qkv_w, L3_xattn_qkv_b, L3_xattn_sa_out_w, L3_xattn_sa_out_b, L3_xattn_in_proj_w, L3_xattn_in_proj_b, L3_xattn_mha_out_w, L3_xattn_mha_out_b, L3_xattn_lin1_w, L3_xattn_lin1_b, L3_xattn_lin2_w, L3_xattn_lin2_b, L3_xattn_ln1_g, L3_xattn_ln1_b, L3_xattn_ln2_g, L3_xattn_ln2_b, L3_xattn_ln3_g, L3_xattn_ln3_b)
    x = x + _L3_ffn_ref(_layernorm(x, axis=-1), L3_ffn_router_w, L3_ffn_w1, L3_ffn_w2)
    return x

_drawn_inputs = setup_inputs


def setup_inputs(seed=0):
    import zlib

    import numpy as np

    out = dict(_drawn_inputs(seed))
    spreads = {'L0_ffn_rb': (0.0, 0.8),
     'L2_ffn_gate_b': (0.0, 0.414),
     'L2_ffn_b1': (0.0, 0.786),
     'L2_ffn_b2': (0.0, 0.336),
     'L3_xattn_qkv_b': (0.0, 0.535),
     'L3_xattn_sa_out_b': (0.0, 0.1),
     'L3_xattn_in_proj_b': (0.0, 0.562),
     'L3_xattn_mha_out_b': (0.0, 0.1),
     'L3_xattn_lin1_b': (0.0, 0.349),
     'L3_xattn_lin2_b': (0.0, 0.1),
     'L3_xattn_ln1_g': (1.0, 0.2),
     'L3_xattn_ln1_b': (0.0, 0.1),
     'L3_xattn_ln2_g': (1.0, 0.2),
     'L3_xattn_ln2_b': (0.0, 0.1),
     'L3_xattn_ln3_g': (1.0, 0.2),
     'L3_xattn_ln3_b': (0.0, 0.1)}
    factors = {'L0_xattn_b_q': 5.028,
     'L0_xattn_b_k': 64.0,
     'L0_xattn_b_v': 3.745,
     'L0_xattn_b_o': 3.701,
     'L0_ffn_sg': 3.813,
     'L0_ffn_su': 4.08,
     'L0_ffn_sd': 3.713,
     'L0_ffn_rg': 4.564,
     'L0_ffn_ru': 5.449,
     'L0_ffn_rd': 5.235,
     'L0_ffn_wr': 5.16,
     'L1_xattn_bo': 4.079,
     'L2_ffn_gate_w': 2.816,
     'L2_ffn_w1': 4.646,
     'L2_ffn_w2': 4.438,
     'L3_xattn_in_proj_w': 4.104,
     'L3_xattn_mha_out_w': 3.539,
     'L3_xattn_qkv_w': 2.757}
    for name, (base, spread) in spreads.items():
        noise = np.random.default_rng([zlib.crc32(name.encode()), seed]).standard_normal(out[name].shape)
        drawn = base * np.exp(spread * noise) if base else spread * noise
        out[name] = jnp.asarray(drawn.astype(out[name].dtype))
    for name, factor in factors.items():
        out[name] = (out[name] * factor).astype(out[name].dtype)
    return out
```

```python
import concourse.bass as bass
from concourse import mybir
from contextlib import ExitStack
import numpy as np

F32 = mybir.dt.float32
F32R = mybir.dt.float32r
BF16 = mybir.dt.bfloat16
I32 = mybir.dt.int32
U32 = mybir.dt.uint32
ALU = mybir.AluOpType
ACT = mybir.ActivationFunctionType
AX = mybir.AxisListType

B, S, D = 8, 128, 128
LAYERS = 4
HEAD_DIM = [8, 8, 8, 16]
SCORE_SCALE = [1.0, 128.0 ** -0.5, 8.0 ** -0.5, 16.0 ** -0.5]
SELF_SCALE = 128.0 ** 0.5
MOE_SCALE = [1.0, 12.0 ** -0.5, 1.0, 1.0]
TOP_K = [2, 2, 1, 2]
EXPERTS = 8
DENSE = "dense"
CHUNKS = {0: 3, 1: 4, 2: 4, DENSE: 4, 3: 2}
GATED = {0: True, 1: True, 2: False, DENSE: False, 3: False}
FUNCTION = {0: ACT.Silu, 1: ACT.Silu, 2: ACT.Gelu, DENSE: ACT.Relu, 3: ACT.Gelu}
OUT_BIAS = {2, DENSE}
N_EXPERTS = {0: 8, 1: 8, 2: 8, DENSE: 1, 3: 8}
MASKED = -1e30
FILL = -1e20
EPS = 1e-5
ARENA_BYTES = 40960

QC, KC, VC, OC, RC = 0, 512, 1024, 1152, 1280
QKVC, SOC = 1288, 1672
B2C, LIN2C = 1288, 1800
ATT_COLS = [1288, 1288, 1288, 1800]
BIAS_COLS = 2312
RAW_COLS = 1800
WEIGHT_PARTS = 4
IDENT, MASKS, SEL, LAM, IOTA, CONST_COLS = 0, 128, 384, 896, 901, 909
LAM_Q, LAM_K, LAM_Q3, LAM_K3, LAM_ROW = range(5)


def expert_cols(kind):
    return CHUNKS[kind] * 128 * (3 if GATED[kind] else 2)


EXPERT_LIST = [(kind, e) for kind in (0, 1, 2, DENSE, 3) for e in range(N_EXPERTS[kind])]


def build_schedule():
    project = [(-9, "key"), (-8.6, "key_split"), (-7, "value"), (-6.8, "value_copy")]
    enter = [(-7.5, "xT"), (-6, "xT_split"), (-5, "query"), (-3.5, "query_split")]
    first = [(-9.5, "pre_stats"), (-8, "pre_norm")]
    heads = [(-2, "scores0"), (-1.5, "max0"), (-1, "scores1"), (0, "max1"), (0.5, "max_split"),
             (1.8, "maxT"), (1.9, "maxT_copy"), (3.2, "expscores0"), (4, "exp0"),
             (4.2, "expscores1"), (5, "exp1"), (6.5, "mix"), (7.5, "mix_norm")]
    leave = [(9, "oT"), (10.1, "oT_split"), (12, "out"), (13.2, "residual")]
    last = [(14, "post_stats"), (15.5, "post_norm"), (17, "fT"), (18.1, "fT_split")]
    inner = [(-29, "pre_stats"), (-27.5, "pre_norm"), (-26, "tT"), (-25, "tT_split"),
             (-23, "self_qkv"), (-22.5, "self_copy"), (-21.8, "self_dot"), (-21, "self_exp"),
             (-20.5, "self_value"), (-18.2, "vT"), (-17.1, "vT_split"), (-15, "self_out"),
             (-14.2, "self_residual"), (-13.5, "mid_stats"), (-12, "mid_norm")]
    one = [s for s in heads if s[1] not in ("scores1", "max1", "expscores1", "exp1")]
    tables = {
        (0, "heads"): project + first + enter + heads + [(8, "shuffle_store")],
        (0, "leave"): [(7, "shuffle_load")] + leave + last,
        (1, "all"): project + first + enter + heads + leave + last,
        (2, "all"): project + first + enter + heads + leave + last,
        (3, "all"): project + inner + enter + one + leave
        + [(14, "cross_stats"), (15.5, "cross_norm"), (17, "yT"), (18.1, "yT_split")],
    }
    steps, items = [], []

    def weights(item):
        items.append(item)
        return [("weights", len(items) - 1, part) for part in range(WEIGHT_PARTS)]

    def attention(key, load=()):
        at = [(10 * b + t, kind, key[0], b) for b in range(B) for t, kind in tables[key]]
        loads = [step for item in load for step in weights(item)]
        at += [(1 + 2.5 * i, *step) for i, step in enumerate(loads)]
        steps.extend(tuple(s[1:]) for s in sorted(at, key=lambda s: s[0]))

    def finish_tiles(first_tile):
        table = [(0, "final_stats"), (2.5, "final_norm"), (4.5, "post_stats"), (7, "post_norm"),
                 (8, "fT"), (9, "fT_split")]
        at = [(2 * b + t, kind, 3, b) for b in range(first_tile, first_tile + 4) for t, kind in table]
        steps.extend(tuple(s[1:]) for s in sorted(at, key=lambda s: s[0]))

    def feed_forward(kind):
        units = [(e, n) for e in range(N_EXPERTS[kind]) for n in range(2)]
        before = None

        def down(e, n):
            steps.append(("down", kind, e, n))
            steps.append(("add_expert", kind, e, n))
            x = EXPERT_LIST.index((kind, e)) + 2
            if n == 1 and x < len(EXPERT_LIST) and EXPERT_LIST[x][0] in (kind, 3) and (kind != 2):
                steps.extend(weights(("expert", x)))
            elif n == 1 and kind == 2 and EXPERT_LIST[x][0] == 2:
                steps.extend(weights(("expert", x)))
            if kind == DENSE:
                finish_tiles(4 * n)
            if kind == 3 and e == EXPERTS - 1:
                steps.append(("store", n))

        for i, (e, n) in enumerate(units):
            for c in range(CHUNKS[kind]):
                steps.append(("up", kind, e, n, c))
                if before is not None:
                    steps.append(("hidden_split", kind, *before))
                before = (e, n, c)
                if c == 1 and i:
                    down(*units[i - 1])
            if i == 0 and kind != DENSE:
                steps.append(("route", kind))
        steps.append(("hidden_split", kind, *before))
        down(*units[-1])

    def experts(*which):
        return [("expert", EXPERT_LIST.index(x)) for x in which]

    steps.extend(weights(("attention", 0)))
    attention((0, "heads"), [("attention", 1), *experts((0, 0), (0, 1))])
    attention((0, "leave"))
    feed_forward(0)
    attention((1, "all"), [("attention", 2), *experts((1, 0), (1, 1))])
    feed_forward(1)
    attention((2, "all"), [("attention", 3), *experts((2, 0), (2, 1))])
    feed_forward(2)
    attention((3, "all"), experts((DENSE, 0), (3, 0)))
    feed_forward(DENSE)
    feed_forward(3)
    return steps, items


def fused_layers(nc, x_in, ctx_in, mask_in, att_w, expert_w, bias_in, hidden_bias_in, norm_in,
                 const_in, x_out):
    steps, items = build_schedule()
    ordinal, per_kind = {}, {}
    for step in steps:
        ordinal[step] = per_kind.get(step[0], 0)
        per_kind[step[0]] = ordinal[step] + 1

    TRANSPOSES = ("xT", "fT", "oT", "tT", "vT", "yT")
    SMALL = TRANSPOSES + ("query", "key", "value", "maxT", "mix", "out", "self_qkv", "self_out", "route")
    UNITS = ("scores0", "scores1", "expscores0", "expscores1")
    smalls = [s for s in steps if s[0] in SMALL]
    units = [s for s in steps if s[0] in UNITS]
    small_at = {s: i for i, s in enumerate(smalls)}
    unit_at = {s: i for i, s in enumerate(units)}
    READ = {"query": "query_split", "key": "key_split", "value": "value_copy", "maxT": "maxT_copy",
            "mix": "mix_norm", "out": "residual", "self_qkv": "self_copy", "self_out": "self_residual",
            "route": "logits", **{t: f"{t}_lo" for t in TRANSPOSES},
            "scores0": "max", "scores1": "max", "expscores0": "exp", "expscores1": "exp"}

    def read_count(step):
        kind = step[0]
        if kind in ("scores0", "scores1", "expscores0", "expscores1"):
            same = [u for u in units if u[0][:-1] == kind[:-1]]
            return same.index(step) + 1
        return ordinal[step] + 1

    dscratch = nc.dram_tensor("head_major_scratch", (16, B, S, 8), F32, kind="Internal").ap()

    with ExitStack() as stack:
        def sb(name, shape, dtype):
            return stack.enter_context(nc.sbuf_tensor(name, [shape[0], int(np.prod(shape[1:]))], dtype))[:, :]

        arena = {}

        def shared(name, shape, dtype, phase):
            at = arena.setdefault(phase, arena["base"])
            arena[phase] = at + 4 * shape[1]
            assert arena[phase] <= arena["base"] + ARENA_BYTES
            return nc.alloc_sbuf_tensor_at(name, shape, dtype, offset=at)[:, :]

        def split3(ap, a):
            return ap.rearrange("p (a c) -> p a c", a=a)

        sems = {}
        SEMAPHORES = (
            ["loads_x", "loads_ctx", "loads_const", "loads_mask", "loads_bias", "raw0", "raw1", "shuffled0",
             "shuffled1", "unshuffled0", "unshuffled1", "stored", "dve_own", "pool_own", "constants", "const_rows",
             "masks", "context_hi", "context_lo", "weights_split", "variance", "rstd", "pre_norm",
             "mid_norm", "cross_norm", "post_norm", "self_value", "self_copy", "self_dot", "self_exp",
             "self_residual", "query", "query_round", "query_split", "key", "key_round", "key_split",
             "value", "value_copy", "scores", "max", "max_split", "maxT", "maxT_copy", "expscores",
             "exp", "mix", "mix_norm", "out", "residual", "self_qkv", "self_out", "route", "logits",
             "route_diff", "route_exp", "gate_up", "plain_up", "activated", "hidden", "hidden_hi", "hidden_lo", "down",
             "add_expert", "final_sum"]
            + [f"{t}_{p}" for t in TRANSPOSES for p in ("ps", "hi", "lo")])
        for name in SEMAPHORES:
            sems[name] = stack.enter_context(nc.semaphore(name))

        arena["base"] = (nc.sbuf_base + 31) // 32 * 32
        sb("arena", [128, ARENA_BYTES // 4 + 8], F32)
        x = split3(sb("x", [128, B * D], F32), B)
        ctx = sb("ctx_hi", [128, B * S], F32R), sb("ctx_lo", [128, B * S], F32R)
        att = [(sb(f"att_hi{l}", [128, ATT_COLS[l]], F32R), sb(f"att_lo{l}", [128, ATT_COLS[l]], F32R))
               for l in range(LAYERS)]
        bias = sb("bias_rows", [128, BIAS_COLS], F32R)
        raw = [sb(f"raw{i}", [128, RAW_COLS], F32) for i in range(2)]
        exp_w = [(sb(f"expert_hi{i}", [128, 1536], F32R), sb(f"expert_lo{i}", [128, 1536], F32R))
                 for i in range(2)]
        const = sb("const", [128, CONST_COLS], F32)
        const16 = sb("const16", [128, 384], BF16)
        ident_r = sb("ident_r", [128, 128], F32R)
        sel = split3(sb("sel", [128, 512], F32R), 4)
        ones = sb("ones", [128, 128], F32R)
        minus_half = sb("minus_half", [128, 1], F32)
        hidden_bias = sb("hidden_bias", [128, 36], F32)
        norms = split3(sb("norms", [128, 6 * D], F32), 6)
        mask1 = split3(sb("mask1", [128, B * S], BF16), B)
        stats = [sb(f"stats{i}", [128, 6], F32) for i in range(4)]
        moments = [sb(f"moments{i}", [128, 2], F32) for i in range(4)]
        var_eps = [sb(f"var_eps{i}", [128, 1], F32) for i in range(4)]
        rstd = [sb(f"rstd{i}", [128, 1], F32) for i in range(4)]
        norm_x = [sb(f"norm_x{i}", [128, D], F32) for i in range(2)]
        norm_f = [sb(f"norm_f{i}", [128, D], F32) for i in range(2)]
        turned = {t: [(sb(f"{t}_hi{i}", [128, 128], F32R), sb(f"{t}_lo{i}", [128, 128], F32R))
                      for i in range(2)] for t in ("xT", "oT", "tT", "vT")}
        ffn_in = sb("ffn_in_hi", [128, B * S], F32R), sb("ffn_in_lo", [128, B * S], F32R)
        stacked = {w: [shared(f"{w}_stack{i}", [128, 512], F32R, "attention") for i in range(2)] for w in ("query", "key")}
        rounded = tuple(shared(f"rounded_{w}", [128, 512], F32R, "attention") for w in ("q", "k"))
        values = [sb(f"values{i}", [128, 16 * 9], F32) for i in range(2)]
        values3 = [sb(f"values_wide{i}", [128, 8 * 17], F32) for i in range(2)]
        neg_max = [sb(f"neg_max{i}", [128, 16], F32) for i in range(2)]
        max_parts = [sb(f"max_parts{i}", [128, 128], F32R) for i in range(2)]
        max_parts3 = [sb(f"max_parts_wide{i}", [128, 128], F32R) for i in range(2)]
        max_rows = [sb(f"max_rows{i}", [128, 128], F32R) for i in range(2)]
        recip = sb("recip", [128, 16], F32)
        mixed = [sb(f"mixed{i}", [128, D], F32) for i in range(2)]
        unshuffled = [sb(f"unshuffled_x{i}", [128, D], F32) for i in range(2)]
        hid_hi = [shared(f"hidden_hi{i}", [128, 2048], F32R, "ffn") for i in range(2)]
        hid_lo = [shared(f"hidden_lo{i}", [128, 2048], F32R, "ffn") for i in range(2)]
        probs = [shared(f"probs{i}", [128, 2048], F32, "attention") for i in range(2)]
        hid = [shared(f"hidden{i}", [128, 512], F32, "ffn") for i in range(2)]
        gate = [shared(f"gate{i}", [128, 512], F32, "ffn") for i in range(2)]
        tgt = split3(sb("tgt", [128, B * D], F32), B)
        x1 = split3(sb("x1", [128, B * D], F32), B)
        mask_raw = x1.rearrange("p b d -> p (b d)").bitcast(I32)
        x2 = tgt
        mid_sum = [sb(f"mid_sum{i}", [128, D], F32) for i in range(2)]
        cross_sum = [sb(f"cross_sum{i}", [128, D], F32) for i in range(2)]
        final_sum = split3(sb("final_sum_x", [128, 4 * D], F32), 4)
        final_norm = sb("final_norm_x", [128, D], F32)
        self_qkv = [sb(f"self_qkv_x{i}", [128, 384], F32) for i in range(2)]
        self_prod = sb("self_prod", [128, D], F32)
        self_s = [sb(f"self_s{i}", [128, 8], F32) for i in range(2)]
        self_v = [sb(f"self_v{i}", [128, D], F32) for i in range(2)]
        logits = split3(sb("logits_x", [128, B * EXPERTS], F32), B)
        top = split3(sb("top", [128, B * 8], F32), B)
        top_at = split3(sb("top_at", [128, B * 8], U32), B)
        top_atf = split3(sb("top_atf", [128, B * 8], F32), B)
        route_diff = split3(sb("route_diff_x", [128, B * 8], F32), B)
        route_exp = split3(sb("route_exp_x", [128, B * 8], F32), B)
        route_sum = sb("route_sum", [128, B], F32)
        route_r = sb("route_r", [128, B], F32)
        hot = split3(sb("hot", [128, B * 8], F32), B)
        share = split3(sb("share", [128, B * 8], F32), B)

        ident = const[:, IDENT:IDENT + 128]
        ident16 = const16[:, 0:128]
        mask0, mask2 = const16[:, 128:256], const16[:, 256:384]
        iota = const[:, IOTA:IOTA + 8]

        def lam(i):
            return const[:, LAM + i:LAM + i + 1]

        psum = [stack.enter_context(nc.psum_tensor(f"pair{i}", [128, 1024], F32))[:, :] for i in range(3)]
        small = [stack.enter_context(nc.psum_tensor(f"small{i}", [128, 512], F32))[:, :] for i in range(2)]

        def small_of(step):
            return small[small_at[step] % 2]

        def unit_of(step):
            return psum[unit_at[step] % 3]

        def bank(i):
            return psum[i // 2][:, 512 * (i % 2):512 * (i % 2) + 512]

        def attn_ordinal(l, b):
            return l * B + b

        def par(l, b):
            return (l * B + b) % 2

        def n_attn(l):
            return sum(B * (1 if m == 3 else 2) for m in range(l))

        def source(t, l, b):
            k = ordinal[(t, l, b)]
            if t == "xT":
                if l < 3:
                    return norm_x[k % 2], "pre_norm", ordinal[("pre_norm", l, b)] + 1
                return x1[:, b, :], "mid_norm", b + 1
            if t == "tT":
                return tgt[:, b, :], "pre_norm", ordinal[("pre_norm", l, b)] + 1
            if t == "vT":
                return self_v[b % 2], "self_value", b + 1
            if t == "oT":
                if l == 0:
                    return unshuffled[b % 2], f"unshuffled{b % 2}", 16 * (b // 2 + 1)
                return mixed[par(l, b)], "mix_norm", ordinal[("mix_norm", l, b)] + 1
            if t == "yT":
                return x2[:, b, :], "cross_norm", b + 1
            return norm_f[k % 2], "post_norm", k + 1

        def target(t, l, b):
            if t in ("fT", "yT"):
                return tuple(a[:, S * b:S * b + S] for a in ffn_in)
            return turned[t][ordinal[(t, l, b)] % 2]

        def chunk_ordinal(kind, e, n, c):
            return ordinal[("up", kind, e, n, c)]

        def plain_before(kind):
            order = (0, 1, 2, DENSE, 3)
            return sum(CHUNKS[m] * N_EXPERTS[m] * 2 for m in order[:order.index(kind)])

        def local_chunk(kind, e, n, c):
            return chunk_ordinal(kind, e, n, c) - plain_before(kind)

        def columns(item):
            return ATT_COLS[item[1]] if item[0] == "attention" else expert_cols(EXPERT_LIST[item[1]][0])

        def part_of(item, part):
            cols = columns(item)
            edge = [(cols * i // WEIGHT_PARTS + 7) // 8 * 8 for i in range(WEIGHT_PARTS)] + [cols]
            return edge[part], edge[part + 1]

        def parts(item):
            return att[item[1]] if item[0] == "attention" else exp_w[item[1] % 2]

        def split_count(item):
            return WEIGHT_PARTS * (items.index(item) + 1)

        block = stack.enter_context(nc.Block())

        @block.sync
        def _(sp):
            def load_item(i):
                kind, which = items[i]
                cols = columns(items[i])
                if i >= 2:
                    sp.wait_ge(sems["weights_split"], WEIGHT_PARTS * (i - 1))
                if kind == "attention":
                    src = att_w[which]
                else:
                    k, e = EXPERT_LIST[which]
                    src = expert_w[k][e]
                sp.dma_start(raw[i % 2][:, 0:cols], src).then_inc(sems[f"raw{i % 2}"], 16)

            sp.dma_start(const, const_in).then_inc(sems["loads_const"], 16)
            sp.dma_start(x.rearrange("p b d -> p (b d)"), x_in).then_inc(sems["loads_x"], 16)
            load_item(0)
            sp.dma_start(probs[1][:, 0:B * S], ctx_in).then_inc(sems["loads_ctx"], 16)
            load_item(1)
            for step in steps:
                what = step[0]
                if what == "weights" and step[2] == WEIGHT_PARTS - 1 and step[1] + 2 < len(items):
                    load_item(step[1] + 2)
                if what == "shuffle_store":
                    _, l, b = step
                    sp.wait_ge(sems["mix_norm"], b + 1)
                    sp.dma_start(dscratch[:, b, :, :].rearrange("h q d -> q h d"),
                                 split3(mixed[b % 2], 16)).then_inc(sems[f"shuffled{b % 2}"], 16)
                if what == "shuffle_load":
                    _, l, b = step
                    if b == 0:
                        sp.wait_ge(sems["shuffled0"], 16 * (B // 2))
                        sp.wait_ge(sems["shuffled1"], 16 * (B // 2))
                    if b >= 2:
                        sp.wait_ge(sems["oT_ps"], b - 1)
                    flat = dscratch.rearrange("h b q d -> (h b q d)").rearrange("(t s c) -> t s c", s=S, c=D)
                    sp.dma_start(unshuffled[b % 2], flat[b]).then_inc(sems[f"unshuffled{b % 2}"], 16)
                if what == "store":
                    n = step[1]
                    sp.wait_ge(sems["add_expert"], ordinal[("add_expert", 3, EXPERTS - 1, n)] + 1)
                    sp.dma_start(x_out[:, 512 * n:512 * n + 512],
                                 x[:, 4 * n:4 * n + 4, :].rearrange("p b d -> p (b d)")).then_inc(sems["stored"], 16)
            sp.wait_ge(sems["stored"], 32)

        @block.gpsimd
        def _(pool):
            own = [0]

            def chain(instruction):
                own[0] += 1
                instruction.then_inc(sems["pool_own"], 1)
                pool.wait_ge(sems["pool_own"], own[0])

            pool.dma_start(mask_raw, mask_in).then_inc(sems["loads_mask"], 16)
            pool.dma_start(probs[0][:, 0:2048], bias_in[:, 0:2048]).then_inc(sems["loads_bias"], 16)
            pool.dma_start(probs[1][:, 1024:1024 + BIAS_COLS - 2048], bias_in[:, 2048:BIAS_COLS]).then_inc(sems["loads_bias"], 16)
            pool.dma_start(hidden_bias, hidden_bias_in).then_inc(sems["loads_mask"], 16)
            pool.dma_start(norms.rearrange("p a c -> p (a c)"), norm_in).then_inc(sems["loads_mask"], 16)
            pool.memset(minus_half, -0.5).then_inc(sems["pool_own"], 1)
            own[0] += 1
            count = 0
            for step in steps:
                what = step[0]
                if what == "weights":
                    _, i, part = step
                    item = items[i]
                    hi, lo = parts(item)
                    a, z = part_of(item, part)
                    if part == 0:
                        pool.wait_ge(sems[f"raw{i % 2}"], 16 * (i // 2 + 1))
                        if item[0] == "expert" and item[1] >= 2:
                            pool.wait_ge(sems["down"], 2 * (item[1] - 1))
                    w = raw[i % 2][:, a:z]
                    chain(pool.tensor_scalar(hi[:, a:z], w, 1.0, 1.0, ALU.mult, ALU.mult))
                    pool.tensor_tensor(lo[:, a:z], w, hi[:, a:z].bitcast(F32), ALU.subtract).then_inc(
                        sems["weights_split"], 1)
                    if i == 0 and part == WEIGHT_PARTS - 1:
                        pool.wait_ge(sems["loads_mask"], 48)
                        pool.tensor_scalar(mask1.rearrange("p b k -> p (b k)"), mask_raw, 0.0, FILL,
                                           ALU.is_equal, ALU.mult).then_inc(sems["masks"], 1)
                if what.endswith("_stats"):
                    i = count % 4
                    count += 1
                    pool.wait_ge(sems["variance"], count)
                    if count == 1:
                        pool.wait_ge(sems["pool_own"], 1)
                    pool.tensor_tensor(rstd[i], var_eps[i], minus_half, ALU.pow).then_inc(sems["rstd"], 1)

        @block.scalar
        def _(act):
            act.wait_ge(sems["loads_ctx"], 16)
            act.activation(ctx[0], probs[1][:, 0:B * S], ACT.Copy).then_inc(sems["context_hi"], 1)
            act.wait_ge(sems["loads_bias"], 32)
            act.activation(bias[:, 0:2048], probs[0], ACT.Copy).then_inc(sems["const_rows"], 1)
            act.activation(bias[:, 2048:BIAS_COLS], probs[1][:, 1024:1024 + BIAS_COLS - 2048],
                           ACT.Copy).then_inc(sems["const_rows"], 1)
            for step in steps:
                what = step[0]
                if what.endswith("_split") and what[:-6] in TRANSPOSES:
                    t, l, b = what[:-6], step[1], step[2]
                    k = ordinal[(t, l, b)]
                    hi, _ = target(t, l, b)
                    act.wait_ge(sems[f"{t}_ps"], k + 1)
                    if t in ("xT", "tT", "vT", "oT") and k >= 2:
                        user = {"xT": "query", "tT": "self_qkv", "vT": "self_out", "oT": "out"}[t]
                        act.wait_ge(sems[user], k - 1)
                    act.activation(hi, small_of((t, l, b))[:, 0:128], ACT.Copy).then_inc(sems[f"{t}_hi"], 1)
                elif what in ("query_split", "key_split"):
                    w = what[:-6]
                    k = ordinal[(w, *step[1:])]
                    act.wait_ge(sems[w], k + 1)
                    if k >= 1:
                        act.wait_ge(sems[what], k)
                    act.activation(rounded[w == "key"], small_of((w, *step[1:])), ACT.Copy).then_inc(
                        sems[f"{w}_round"], 1)
                elif what == "value_copy":
                    _, l, b = step
                    k = ordinal[step]
                    act.wait_ge(sems["value"], k + 1)
                    if k == 0:
                        act.wait_ge(sems["constants"], 4)
                    if k >= 2:
                        act.wait_ge(sems["mix"], k - 1)
                    d = HEAD_DIM[l]
                    to = split3((values3 if l == 3 else values)[par(l, b)], 128 // d)[:, :, 0:d]
                    act.activation(to, split3(small_of(("value", l, b))[:, 0:128], 128 // d),
                                   ACT.Copy).then_inc(sems["value_copy"], 1)
                elif what == "maxT_copy":
                    _, l, b = step
                    k = ordinal[step]
                    act.wait_ge(sems["maxT"], k + 1)
                    if k >= 2:
                        l2, b2 = divmod(k - 2, B)
                        act.wait_ge(sems["expscores"], n_attn(l2) + (b2 + 1) * (1 if l2 == 3 else 2))
                    act.activation(max_rows[k % 2], small_of(("maxT", l, b))[:, 0:128], ACT.Copy).then_inc(
                        sems["maxT_copy"], 1)
                elif what in ("exp0", "exp1"):
                    _, l, b = step
                    half = int(what[-1])
                    unit = (f"expscores{half}", l, b)
                    act.wait_ge(sems["expscores"], read_count(unit))
                    k = attn_ordinal(l, b)
                    if k >= 2 and half == 0:
                        act.wait_ge(sems["mix"], k - 1)
                    act.activation(probs[k % 2][:, 1024 * half:1024 * half + 1024], unit_of(unit), ACT.Exp,
                                   scale=SCORE_SCALE[l]).then_inc(sems["exp"], 1)
                elif what == "self_copy":
                    _, l, b = step
                    act.wait_ge(sems["self_qkv"], b + 1)
                    if b >= 2:
                        act.wait_ge(sems["self_value"], b - 1)
                    act.activation(self_qkv[b % 2], small_of(("self_qkv", l, b))[:, 0:384], ACT.Copy).then_inc(
                        sems["self_copy"], 1)
                elif what == "self_exp":
                    _, l, b = step
                    act.wait_ge(sems["self_dot"], b + 1)
                    s = self_s[b % 2]
                    act.activation(s[:, 3:4], s[:, 1:2], ACT.Exp, bias=s[:, 2:3]).then_inc(sems["self_exp"], 1)
                elif what == "route":
                    k = ordinal[step]
                    act.wait_ge(sems["route_diff"], k + 1)
                    width = 8 if TOP_K[step[1]] == 1 else 2
                    act.activation(route_exp[:, :, 0:width], route_diff[:, :, 0:width], ACT.Exp).then_inc(
                        sems["route_exp"], 1)
                elif what == "up":
                    _, kind, e, n, c = step
                    k, j = ordinal[step], local_chunk(kind, e, n, c)
                    act.wait_ge(sems["gate_up"], k + 1)
                    if GATED[kind]:
                        if j >= 2:
                            act.wait_ge(sems["hidden"], k - 1)
                        act.activation(gate[j % 2], bank(2 * j % 4), FUNCTION[kind]).then_inc(sems["activated"], 1)
                    else:
                        if j >= 2:
                            act.wait_ge(sems["hidden_lo"], k - 1)
                        col = 4 * e + c if kind == 2 else 32 + c
                        extra = dict(bias=hidden_bias[:, col:col + 1]) if kind in (2, DENSE) else {}
                        act.activation(hid[j % 2], bank(j % 4), FUNCTION[kind], **extra).then_inc(
                            sems["activated"], 1)
                elif what == "hidden_split":
                    _, kind, e, n, c = step
                    k, j = chunk_ordinal(kind, e, n, c), local_chunk(kind, e, n, c)
                    if GATED[kind]:
                        y = ordinal[("down", kind, e, n)]
                        act.wait_ge(sems["hidden"], k + 1)
                        if c == 0 and y >= 2:
                            act.wait_ge(sems["down"], y - 1)
                        act.activation(hid_hi[y % 2][:, 512 * c:512 * c + 512], hid[j % 2], ACT.Copy).then_inc(
                            sems["hidden_hi"], 1)

        @block.vector
        def _(dve):
            own = [0]

            def chain(instruction):
                own[0] += 1
                instruction.then_inc(sems["dve_own"], 1)
                dve.wait_ge(sems["dve_own"], own[0])

            norm_count = [0]
            pending = {}

            def statistics(key, src):
                i = norm_count[0] % 4
                norm_count[0] += 1
                pending[key] = i, norm_count[0]
                chain(dve.bn_stats(stats[i], src))
                chain(dve.bn_aggr(moments[i], stats[i]))
                dve.tensor_scalar(var_eps[i], moments[i][:, 1:2], EPS, None, ALU.add).then_inc(sems["variance"], 1)

            def normalize(key, out, src):
                i, count = pending.pop(key)
                dve.wait_ge(sems["rstd"], count)
                return dve.tensor_scalar(out, src, moments[i][:, 0:1], rstd[i], ALU.subtract, ALU.mult)

            def affine(out, which):
                chain(dve.tensor_tensor(out, out, norms[:, 2 * which, :], ALU.mult))
                return dve.tensor_tensor(out, out, norms[:, 2 * which + 1, :], ALU.add)

            def x_ready(l, b):
                if l == 0:
                    dve.wait_ge(sems["loads_x"], 16)
                else:
                    n = b // 4
                    dve.wait_ge(sems["add_expert"], ordinal[("add_expert", l - 1, EXPERTS - 1, n)] + 1)

            for i in range(2):
                dve.memset(max_parts[i].bitcast(F32), 0.0)
                dve.memset(max_parts3[i].bitcast(F32), 0.0)
                dve.memset(values[i], 1.0).then_inc(sems["constants"], 1)
                dve.memset(values3[i], 1.0).then_inc(sems["constants"], 1)
            dve.wait_ge(sems["loads_const"], 16)
            dve.tensor_copy(ident_r, ident)
            dve.tensor_copy(const16, const[:, IDENT:IDENT + 384])
            dve.tensor_copy(sel.rearrange("p s k -> p (s k)"), const[:, SEL:SEL + 512])
            dve.memset(ones.bitcast(F32), 1.0).then_inc(sems["constants"], 1)
            dve.wait_ge(sems["context_hi"], 1)
            dve.tensor_tensor(ctx[1], probs[1][:, 0:B * S], ctx[0].bitcast(F32), ALU.subtract).then_inc(
                sems["context_lo"], 1)
            dve.wait_ge(sems["const_rows"], 2)
            dve.scalar_tensor_tensor(bias[:, 0:2048], bias[:, 0:2048].bitcast(F32), lam(LAM_ROW), probs[0],
                                     ALU.mult, ALU.add).then_inc(sems["const_rows"], 1)
            dve.scalar_tensor_tensor(bias[:, 2048:BIAS_COLS], bias[:, 2048:BIAS_COLS].bitcast(F32), lam(LAM_ROW),
                                     probs[1][:, 1024:1024 + BIAS_COLS - 2048],
                                     ALU.mult, ALU.add).then_inc(sems["const_rows"], 1)
            dve.wait_ge(sems["loads_mask"], 48)

            for step in steps:
                what = step[0]
                if what.endswith("_split") and what[:-6] in TRANSPOSES:
                    t, l, b = what[:-6], step[1], step[2]
                    k = ordinal[(t, l, b)]
                    hi, lo = target(t, l, b)
                    dve.wait_ge(sems[f"{t}_hi"], k + 1)
                    dve.tensor_tensor(lo, small_of((t, l, b))[:, 0:128], hi.bitcast(F32), ALU.subtract).then_inc(
                        sems[f"{t}_lo"], 1)
                elif what in ("query_split", "key_split"):
                    w, l, b = what[:-6], step[1], step[2]
                    k = ordinal[(w, l, b)]
                    dve.wait_ge(sems[f"{w}_round"], k + 1)
                    if k >= 2:
                        l2, b2 = divmod(k - 2, B)
                        dve.wait_ge(sems["expscores"], n_attn(l2) + (b2 + 1) * (1 if l2 == 3 else 2))
                    column = lam((LAM_Q if w == "query" else LAM_K) + (2 if l == 3 else 0))
                    dve.scalar_tensor_tensor(stacked[w][k % 2], rounded[w == "key"].bitcast(F32), column,
                                             small_of((w, l, b)), ALU.mult, ALU.add).then_inc(sems[what], 1)
                elif what == "pre_stats":
                    _, l, b = step
                    x_ready(l, b)
                    statistics(step[1:], x[:, b, :])
                elif what == "pre_norm":
                    _, l, b = step
                    k = ordinal[step]
                    if l == 3:
                        out = tgt[:, b, :]
                    else:
                        out = norm_x[k % 2]
                        if k >= 2:
                            dve.wait_ge(sems["xT_ps"], k - 1)
                    normalize(step[1:], out, x[:, b, :]).then_inc(sems["pre_norm"], 1)
                elif what in ("max0", "max1"):
                    _, l, b = step
                    half = int(what[-1])
                    unit = (f"scores{half}", l, b)
                    dve.wait_ge(sems["scores"], read_count(unit))
                    dve.tensor_reduce(neg_max[par(l, b)][:, 8 * half:8 * half + 8], split3(unit_of(unit), 8),
                                      AX.X, ALU.max, negate=True).then_inc(sems["max"], 1)
                elif what == "max_split":
                    _, l, b = step
                    k = attn_ordinal(l, b)
                    dve.wait_ge(sems["max"], n_attn(l) + (b + 1) * (1 if l == 3 else 2))
                    if k >= 2:
                        dve.wait_ge(sems["maxT"], k - 1)
                    if l == 3:
                        m = split3(neg_max[k % 2][:, 0:8], 2)
                        to = split3(max_parts3[k % 2], 2)
                    else:
                        m = split3(neg_max[k % 2], 4)
                        to = split3(max_parts[k % 2], 4)
                    chain(dve.tensor_copy(to[:, :, 0:4], m))
                    dve.tensor_tensor(to[:, :, 4:8], m, to[:, :, 0:4].bitcast(F32), ALU.subtract).then_inc(
                        sems["max_split"], 1)
                elif what == "mix_norm":
                    _, l, b = step
                    k = attn_ordinal(l, b)
                    d = HEAD_DIM[l]
                    heads = 128 // d
                    got = split3(small_of(("mix", l, b))[:, 0:heads * (d + 1)], heads)
                    dve.wait_ge(sems["mix"], k + 1)
                    chain(dve.reciprocal(recip[:, 0:heads].unsqueeze(2), got[:, :, d:d + 1]))
                    if l == 0 and b >= 2:
                        dve.wait_ge(sems[f"shuffled{b % 2}"], 16 * (b // 2))
                    elif l == 1 and b < 2:
                        dve.wait_ge(sems[f"shuffled{b % 2}"], 16 * (B // 2))
                    elif l > 0:
                        dve.wait_ge(sems["oT_ps"], k - 1)
                    dve.tensor_tensor(split3(mixed[k % 2], heads), got[:, :, 0:d],
                                      recip[:, 0:heads].unsqueeze(2).to_broadcast([128, heads, d]),
                                      ALU.mult).then_inc(sems["mix_norm"], 1)
                elif what == "residual":
                    _, l, b = step
                    k = ordinal[step]
                    dve.wait_ge(sems["out"], k + 1)
                    got = small_of(("out", l, b))[:, 0:128]
                    if l < 3:
                        dve.tensor_tensor(x[:, b, :], x[:, b, :], got, ALU.add).then_inc(sems["residual"], 1)
                    else:
                        dve.tensor_tensor(cross_sum[b % 2], x1[:, b, :], got, ALU.add).then_inc(sems["residual"], 1)
                elif what == "cross_stats":
                    _, l, b = step
                    dve.wait_ge(sems["residual"], ordinal[("residual", l, b)] + 1)
                    statistics(("cross", b), cross_sum[b % 2])
                elif what == "cross_norm":
                    _, l, b = step
                    chain(normalize(("cross", b), x2[:, b, :], cross_sum[b % 2]))
                    affine(x2[:, b, :], 1).then_inc(sems["cross_norm"], 1)
                elif what == "self_dot":
                    _, l, b = step
                    s = self_s[b % 2]
                    dve.wait_ge(sems["self_copy"], b + 1)
                    qkv = self_qkv[b % 2]
                    chain(dve.tensor_tensor(self_prod, qkv[:, 0:128], qkv[:, 128:256], ALU.mult))
                    chain(dve.tensor_reduce(s[:, 0:1], self_prod, AX.X, ALU.add))
                    chain(dve.tensor_scalar(s[:, 1:2], s[:, 0:1], SELF_SCALE, None, ALU.mult))
                    dve.tensor_scalar(s[:, 2:3], s[:, 1:2], -1.0, None, ALU.mult).then_inc(sems["self_dot"], 1)
                elif what == "self_value":
                    _, l, b = step
                    s = self_s[b % 2]
                    dve.wait_ge(sems["self_exp"], b + 1)
                    chain(dve.reciprocal(s[:, 4:5], s[:, 3:4]))
                    if b >= 2:
                        dve.wait_ge(sems["vT_ps"], b - 1)
                    dve.tensor_scalar(self_v[b % 2], self_qkv[b % 2][:, 256:384], s[:, 3:4], s[:, 4:5],
                                      ALU.mult, ALU.mult).then_inc(sems["self_value"], 1)
                elif what == "mid_stats":
                    _, l, b = step
                    dve.wait_ge(sems["self_out"], b + 1)
                    dve.tensor_tensor(mid_sum[b % 2], tgt[:, b, :], small_of(("self_out", l, b))[:, 0:128],
                                      ALU.add).then_inc(sems["self_residual"], 1)
                    dve.wait_ge(sems["self_residual"], b + 1)
                    statistics(("mid", b), mid_sum[b % 2])
                elif what == "mid_norm":
                    _, l, b = step
                    chain(normalize(("mid", b), x1[:, b, :], mid_sum[b % 2]))
                    affine(x1[:, b, :], 0).then_inc(sems["mid_norm"], 1)
                elif what == "final_stats":
                    _, l, b = step
                    dve.wait_ge(sems["add_expert"], ordinal[("add_expert", DENSE, 0, b // 4)] + 1)
                    statistics(("final", b), final_sum[:, b % 4, :])
                elif what == "final_norm":
                    _, l, b = step
                    chain(normalize(("final", b), final_norm, final_sum[:, b % 4, :]))
                    chain(affine(final_norm, 2))
                    dve.tensor_tensor(x[:, b, :], x[:, b, :], final_norm, ALU.add).then_inc(sems["final_sum"], 1)
                elif what == "post_stats":
                    _, l, b = step
                    if l < 3:
                        dve.wait_ge(sems["residual"], ordinal[("residual", l, b)] + 1)
                    else:
                        dve.wait_ge(sems["final_sum"], b + 1)
                    statistics(("post", l, b), x[:, b, :])
                elif what == "post_norm":
                    _, l, b = step
                    k = ordinal[step]
                    if k >= 2:
                        dve.wait_ge(sems["fT_ps"], k - 1)
                    normalize(("post", l, b), norm_f[k % 2], x[:, b, :]).then_inc(sems["post_norm"], 1)
                elif what == "route":
                    l = step[1]
                    k = ordinal[step]
                    dve.wait_ge(sems["route"], k + 1)
                    dve.tensor_copy(logits, split3(small_of(step)[:, 0:64], B)).then_inc(sems["logits"], 1)
                    dve.wait_ge(sems["logits"], k + 1)
                    for b in range(B):
                        last = dve.max(top[:, b, :], logits[:, b, :])
                    chain(last)
                    for b in range(B):
                        last = dve.max_index(top_at[:, b, :], top[:, b, :], logits[:, b, :])
                    chain(last)
                    chain(dve.tensor_copy(top_atf, top_at))
                    width = 8 if TOP_K[l] == 1 else 2
                    scores = logits if width == 8 else top
                    dve.tensor_tensor(route_diff[:, :, 0:width], scores[:, :, 0:width],
                                      top[:, :, 0:1].to_broadcast([128, B, width]), ALU.subtract).then_inc(
                        sems["route_diff"], 1)
                    dve.wait_ge(sems["route_exp"], k + 1)
                    chain(dve.tensor_reduce(route_sum, route_exp[:, :, 0:width], AX.X, ALU.add))
                    if MOE_SCALE[l] != 1.0:
                        chain(dve.tensor_scalar(route_sum, route_sum, 1.0 / MOE_SCALE[l], None, ALU.mult))
                    chain(dve.reciprocal(route_r, route_sum))
                    for i in range(TOP_K[l]):
                        chain(dve.tensor_tensor(hot, iota.unsqueeze(1).to_broadcast([128, B, 8]),
                                                top_atf[:, :, i:i + 1].to_broadcast([128, B, 8]), ALU.is_equal))
                        to = share if i == 0 else hot
                        if TOP_K[l] == 1:
                            chain(dve.tensor_tensor(to, hot, route_r.unsqueeze(2).to_broadcast([128, B, 8]),
                                                    ALU.mult))
                            continue
                        chain(dve.tensor_tensor(hot, hot, route_exp[:, :, i:i + 1].to_broadcast([128, B, 8]),
                                                ALU.mult))
                        chain(dve.tensor_tensor(to, hot, route_r.unsqueeze(2).to_broadcast([128, B, 8]), ALU.mult))
                        if i:
                            chain(dve.tensor_tensor(share, share, hot, ALU.add))
                    if l == 0:
                        chain(dve.memset(share[:, :, 7:8], 1.0))
                elif what == "up":
                    _, kind, e, n, c = step
                    k, j = ordinal[step], local_chunk(kind, e, n, c)
                    if GATED[kind]:
                        dve.wait_ge(sems["plain_up"], k + 1)
                        dve.wait_ge(sems["activated"], k + 1)
                        if j >= 2:
                            dve.wait_ge(sems["hidden_lo"], k - 1)
                        dve.tensor_tensor(hid[j % 2], gate[j % 2], bank((2 * j + 1) % 4), ALU.mult).then_inc(
                            sems["hidden"], 1)
                elif what == "hidden_split":
                    _, kind, e, n, c = step
                    k, j = chunk_ordinal(kind, e, n, c), local_chunk(kind, e, n, c)
                    y = ordinal[("down", kind, e, n)]
                    hi = hid_hi[y % 2][:, 512 * c:512 * c + 512]
                    if GATED[kind]:
                        dve.wait_ge(sems["hidden_hi"], k + 1)
                    else:
                        dve.wait_ge(sems["activated"], k + 1)
                        if c == 0 and y >= 2:
                            dve.wait_ge(sems["down"], y - 1)
                        dve.tensor_copy(hi, hid[j % 2]).then_inc(sems["hidden_hi"], 1)
                        dve.wait_ge(sems["hidden_hi"], k + 1)
                    if c == 0 and y >= 2:
                        dve.wait_ge(sems["down"], y - 1)
                    dve.tensor_tensor(hid_lo[y % 2][:, 512 * c:512 * c + 512], hid[j % 2], hi.bitcast(F32),
                                      ALU.subtract).then_inc(sems["hidden_lo"], 1)
                elif what == "add_expert":
                    _, kind, e, n = step
                    y = ordinal[step]
                    dve.wait_ge(sems["down"], y + 1)
                    if y >= 2:
                        dve.wait_ge(sems["add_expert"], y - 1)
                    got = split3(bank(4 + y % 2), 4)
                    for i in range(4):
                        b = 4 * n + i
                        if kind == DENSE:
                            last = dve.tensor_tensor(final_sum[:, i, :], x2[:, b, :], got[:, i, :], ALU.add)
                        else:
                            last = dve.scalar_tensor_tensor(x[:, b, :], got[:, i, :], share[:, b, e:e + 1],
                                                            x[:, b, :], ALU.mult, ALU.add)
                    last.then_inc(sems["add_expert"], 1)

        @block.tensor
        def _(pe):
            def product(out, left, right, row=None, start=True):
                (lh, ll), (rh, rl) = left, right
                if row is not None:
                    pe.matmul(out, *row, start=start, stop=False, skip_group_check=True)
                    start = False
                pe.matmul(out, lh, rh, start=start, stop=False, skip_group_check=True)
                pe.matmul(out, lh, rl, start=False, stop=False, skip_group_check=True)
                return pe.matmul(out, ll, rh, start=False, stop=True, skip_group_check=True)

            def cut(pair, a, z):
                return pair[0][:, a:z], pair[1][:, a:z]

            def free_small(step):
                i = small_at[step]
                if i >= 2:
                    before = smalls[i - 2]
                    pe.wait_ge(sems[READ[before[0]]], read_count(before))

            def free_unit(step):
                i = unit_at[step]
                if i >= 3:
                    before = units[i - 3]
                    pe.wait_ge(sems[READ[before[0]]], read_count(before))

            def bias_rows(l, a, z):
                return bias[32 * l:32 * l + 2, a:z]

            def ones_rows(l):
                return ones[32 * l:32 * l + 2, :]

            def token_row(l, a, z):
                return ones_rows(l), bias_rows(l, a, z)

            def mask_of(l, b):
                return {0: mask0, 1: mask1[:, b, :], 2: mask2}[l]

            def rows(l, j):
                size = 32 if l < 3 else 64
                return slice(size * j, size * j + size)

            pe.wait_ge(sems["constants"], 5)
            pe.wait_ge(sems["context_lo"], 1)
            pe.wait_ge(sems["const_rows"], 4)
            pe.wait_ge(sems["loads_mask"], 48)
            pe.wait_ge(sems["loads_const"], 16)
            for step in steps:
                what = step[0]
                if what in TRANSPOSES:
                    _, l, b = step
                    src, sem, value = source(*step)
                    pe.wait_ge(sems[sem], value)
                    free_small(step)
                    pe.transpose(small_of(step)[:, 0:128], src, ident).then_inc(sems[f"{what}_ps"], 1)
                elif what in ("query", "key"):
                    _, l, b = step
                    if what == "key" and b == 0:
                        pe.wait_ge(sems["weights_split"], split_count(("attention", l)))
                        if l > 0:
                            pe.wait_ge(sems["add_expert"], ordinal[("add_expert", l - 1, EXPERTS - 1, 1)] + 1)
                    if what == "query":
                        pe.wait_ge(sems["xT_lo"], ordinal[("xT", l, b)] + 1)
                        right = turned["xT"][ordinal[("xT", l, b)] % 2]
                    else:
                        right = cut(ctx, S * b, S * b + S)
                    free_small(step)
                    base = QC if what == "query" else KC
                    to = split3(small_of(step), 4)
                    for s in range(4):
                        a, z = base + 128 * s, base + 128 * s + 128
                        row = (bias_rows(l, a, z), ones_rows(l)) if l in (0, 3) else None
                        last = product(to[:, s, :], cut(att[l], a, z), right, row)
                    last.then_inc(sems[what], 1)
                elif what == "value":
                    _, l, b = step
                    free_small(step)
                    product(small_of(step)[:, 0:128], cut(ctx, S * b, S * b + S), cut(att[l], VC, VC + 128),
                            token_row(l, VC, VC + 128) if l != 1 else None).then_inc(sems["value"], 1)
                elif what in ("scores0", "scores1"):
                    _, l, b = step
                    half = int(what[-1])
                    p = par(l, b)
                    q, k = split3(stacked["query"][p], 4), split3(stacked["key"][p], 4)
                    pe.wait_ge(sems["query_split"], attn_ordinal(l, b) + 1)
                    pe.wait_ge(sems["key_split"], attn_ordinal(l, b) + 1)
                    if l == 1 and b == 0:
                        pe.wait_ge(sems["masks"], 1)
                    free_unit(step)
                    to = unit_of(step).rearrange("p (j s k) -> p j s k", j=2, s=4)
                    if l < 3:
                        for jj in range(2):
                            pe.matmul(to[:, jj], ident16, mask_of(l, b).unsqueeze(1).to_broadcast([128, 4, 128]),
                                      start=True, stop=False, skip_group_check=True)
                    for s in range(4):
                        for jj in range(2):
                            r = rows(l, 2 * half + jj)
                            last = pe.matmul(to[:, jj, s, :], q[r, s, :], k[r, s, :], start=(l == 3), stop=True,
                                             skip_group_check=True)
                    last.then_inc(sems["scores"], 1)
                elif what == "maxT":
                    _, l, b = step
                    k = attn_ordinal(l, b)
                    pe.wait_ge(sems["max_split"], k + 1)
                    free_small(step)
                    pe.matmul(small_of(step)[:, 0:128], (max_parts3 if l == 3 else max_parts)[k % 2], ident_r,
                              start=True, stop=True).then_inc(sems["maxT"], 1)
                elif what in ("expscores0", "expscores1"):
                    _, l, b = step
                    half = int(what[-1])
                    p = par(l, b)
                    q, k = split3(stacked["query"][p], 4), split3(stacked["key"][p], 4)
                    pe.wait_ge(sems["maxT_copy"], attn_ordinal(l, b) + 1)
                    free_unit(step)
                    to = unit_of(step).rearrange("p (j s q) -> p j s q", j=2, s=4)
                    if l < 3:
                        for jj in range(2):
                            pe.matmul(to[:, jj], mask_of(l, b), ident16.unsqueeze(1).to_broadcast([128, 4, 128]),
                                      start=True, stop=False, skip_group_check=True)
                    for s in range(4):
                        for jj in range(2):
                            r = rows(l, 2 * half + jj)
                            low = slice(r.start, r.start + 32)
                            pe.matmul(to[:, jj, s, :], k[r, s, :], q[r, s, :], start=(l == 3), stop=False,
                                      skip_group_check=True)
                            last = pe.matmul(to[:, jj, s, :], sel[low, s, :], max_rows[p][low, :], start=False,
                                             stop=True, skip_group_check=True)
                    last.then_inc(sems["expscores"], 1)
                elif what == "mix":
                    _, l, b = step
                    k = attn_ordinal(l, b)
                    d = HEAD_DIM[l]
                    heads = 128 // d
                    pe.wait_ge(sems["exp"], n_attn(l) + (b + 1) * (1 if l == 3 else 2))
                    pe.wait_ge(sems["value_copy"], k + 1)
                    free_small(step)
                    p = split3(probs[k % 2], 16)
                    v = split3((values3 if l == 3 else values)[k % 2], heads)
                    to = split3(small_of(step)[:, 0:heads * (d + 1)], heads)
                    for h in range(heads):
                        last = pe.matmul(to[:, h, :], p[:, h, :], v[:, h, :], start=True, stop=True)
                    last.then_inc(sems["mix"], 1)
                elif what == "out":
                    _, l, b = step
                    k = ordinal[("oT", l, b)]
                    pe.wait_ge(sems["oT_lo"], k + 1)
                    free_small(step)
                    product(small_of(step)[:, 0:128], turned["oT"][k % 2], cut(att[l], OC, OC + 128),
                            token_row(l, OC, OC + 128)).then_inc(sems["out"], 1)
                elif what == "self_qkv":
                    _, l, b = step
                    pe.wait_ge(sems["tT_lo"], b + 1)
                    free_small(step)
                    product(small_of(step)[:, 0:384], turned["tT"][b % 2], cut(att[3], QKVC, QKVC + 384),
                            token_row(3, QKVC, QKVC + 384)).then_inc(sems["self_qkv"], 1)
                elif what == "self_out":
                    _, l, b = step
                    pe.wait_ge(sems["vT_lo"], b + 1)
                    free_small(step)
                    product(small_of(step)[:, 0:128], turned["vT"][b % 2], cut(att[3], SOC, SOC + 128),
                            token_row(3, SOC, SOC + 128)).then_inc(sems["self_out"], 1)
                elif what == "route":
                    l = step[1]
                    pe.wait_ge(sems["fT_lo"], B * (l + 1))
                    free_small(step)
                    to = split3(small_of(step)[:, 0:64], B)
                    for b in range(B):
                        last = product(to[:, b, :], cut(ffn_in, S * b, S * b + S), cut(att[l], RC, RC + 8),
                                       token_row(l, RC, RC + 8))
                    last.then_inc(sems["route"], 1)
                elif what == "up":
                    _, kind, e, n, c = step
                    k, j = ordinal[step], local_chunk(kind, e, n, c)
                    hi, lo = exp_w[EXPERT_LIST.index((kind, e)) % 2]
                    if n == 0 and c == 0:
                        pe.wait_ge(sems["weights_split"], split_count(("expert", EXPERT_LIST.index((kind, e)))))
                    if e == 0 and c == 0:
                        if kind == DENSE:
                            pe.wait_ge(sems["yT_lo"], 4 * n + 4)
                        else:
                            pe.wait_ge(sems["fT_lo"], B * kind + 4 * n + 4)
                    if j == 0:
                        if kind == 3:
                            pe.wait_ge(sems["add_expert"], ordinal[("add_expert", DENSE, 0, 1)] + 1)
                        else:
                            l = 3 if kind == DENSE else kind
                            pe.wait_ge(sems["exp"], n_attn(l) + B * (1 if l == 3 else 2))
                    tokens = cut(ffn_in, 512 * n, 512 * n + 512)
                    width = 128 * CHUNKS[kind]
                    if GATED[kind]:
                        if j >= 2:
                            pe.wait_ge(sems["activated"], k - 1)
                        product(bank(2 * j % 4), cut((hi, lo), 128 * c, 128 * c + 128), tokens).then_inc(
                            sems["gate_up"], 1)
                        if j >= 2:
                            pe.wait_ge(sems["hidden"], k - 1)
                        product(bank((2 * j + 1) % 4), cut((hi, lo), width + 128 * c, width + 128 * c + 128),
                                tokens).then_inc(sems["plain_up"], 1)
                    else:
                        if j >= 4:
                            pe.wait_ge(sems["activated"], k - 3)
                        product(bank(j % 4), cut((hi, lo), 128 * c, 128 * c + 128), tokens).then_inc(
                            sems["gate_up"], 1)
                elif what == "down":
                    _, kind, e, n = step
                    y = ordinal[step]
                    hi, lo = exp_w[EXPERT_LIST.index((kind, e)) % 2]
                    base = 128 * CHUNKS[kind] * (2 if GATED[kind] else 1)
                    pe.wait_ge(sems["hidden_lo"], chunk_ordinal(kind, e, n, CHUNKS[kind] - 1) + 1)
                    if y >= 2:
                        pe.wait_ge(sems["add_expert"], y - 1)
                    to = split3(bank(4 + y % 2), 4)
                    if kind in OUT_BIAS:
                        l, a = (2, B2C + 128 * e) if kind == 2 else (3, LIN2C)
                        pe.matmul(to, ones_rows(l), bias_rows(l, a, a + 128).unsqueeze(1).to_broadcast([2, 4, 128]),
                                  start=True, stop=False, skip_group_check=True)
                    for i in range(4):
                        for c in range(CHUNKS[kind]):
                            a = 512 * c + 128 * i
                            last = product(to[:, i, :], (hid_hi[y % 2][:, a:a + 128], hid_lo[y % 2][:, a:a + 128]),
                                           cut((hi, lo), base + 128 * c, base + 128 * c + 128),
                                           start=(c == 0 and kind not in OUT_BIAS))
                    last.then_inc(sems["down"], 1)


def _stack_columns(w, d):
    j = 32 // d
    w = w.reshape(*w.shape[:-1], j, 4, d)
    w = np.moveaxis(w, -2, -3)[..., None, :]
    w = np.broadcast_to(w, (*w.shape[:-2], 4, d))
    return w.reshape(*w.shape[:-4], 512)


def _constants():
    const = np.zeros((128, CONST_COLS), np.float32)
    const[:, IDENT:IDENT + 128] = np.eye(128)
    for s in range(4):
        for j in range(4):
            const[32 * j + s, SEL + 128 * s:SEL + 128 * s + 128] = 1
            const[32 * j + 4 + s, SEL + 128 * s:SEL + 128 * s + 128] = 1
    r = np.arange(128)
    const[:, LAM + LAM_Q] = np.where((r // 8) % 4 >= 2, -1.0, 0.0)
    const[:, LAM + LAM_K] = np.where((r // 8) % 2 == 1, -1.0, 0.0)
    const[:, LAM + LAM_Q3] = np.where((r // 16) % 4 >= 2, -1.0, 0.0)
    const[:, LAM + LAM_K3] = np.where((r // 16) % 2 == 1, -1.0, 0.0)
    const[:, LAM + LAM_ROW] = np.where(r % 32 == 1, -1.0, 0.0)
    const[:, IOTA:IOTA + 8] = np.arange(8)
    q, k = r[:, None], r[None, :]
    const[:, MASKS:MASKS + 128] = np.where(k <= q, 0, MASKED)
    strict = k < q
    strict[0, 0] = True
    const[:, MASKS + 128:MASKS + 256] = np.where(strict, 0, MASKED)
    return const


def _down_rows(w):
    return w.reshape(-1, 128, 128).transpose(1, 0, 2).reshape(128, -1)


def kernel(**inputs):
    import concourse.bacc as _bacc
    from concourse.bass_utils import run_bass_kernel_spmd as _run

    g = {k: np.asarray(v) for k, v in inputs.items()}
    x = g["x"].transpose(1, 0, 2).reshape(128, B * D)
    ctx = g["ctx_1024"].transpose(2, 0, 1).reshape(128, B * S)
    mask = g["mask_Bx1xSxS2_ik1"][:, 0].transpose(1, 0, 2).reshape(128, B * S)

    def diagonal(w):
        out = np.zeros((128, 128), np.float32)
        for h in range(16):
            out[8 * h:8 * h + 8, 8 * h:8 * h + 8] = w.T
        return out

    def router(w):
        out = np.zeros((128, 8), np.float32)
        out[:, :w.shape[1]] = w
        return out

    wq3, wk3, wv3 = np.split(g["L3_xattn_in_proj_w"], 3, axis=0)
    bq3, bk3, bv3 = np.split(g["L3_xattn_in_proj_b"], 3)
    att_parts = [
        [(g["L0_xattn_w_q"]), (g["L0_xattn_w_k"]), g["L0_xattn_w_v"], g["L0_xattn_w_o"], router(g["L0_ffn_wr"].T)],
        [diagonal(g["L1_xattn_Wq"]), diagonal(g["L1_xattn_Wk"]), diagonal(g["L1_xattn_Wv"]), g["L1_xattn_Wo"].T,
         router(g["L1_ffn_Wr"])],
        [g["L2_xattn_Wq"].T, g["L2_xattn_Wk"].T, g["L2_xattn_Wv"].T, g["L2_xattn_Wo"].T, router(g["L2_ffn_gate_w"])],
        [wq3.T, wk3.T, wv3.T, g["L3_xattn_mha_out_w"].T, router(g["L3_ffn_router_w"].T), g["L3_xattn_qkv_w"].T,
         g["L3_xattn_sa_out_w"].T],
    ]
    arrays = {}
    for l, p in enumerate(att_parts):
        p = [_stack_columns(p[0], HEAD_DIM[l]), _stack_columns(p[1], HEAD_DIM[l]), *p[2:]]
        arrays[f"att{l}"] = np.ascontiguousarray(np.concatenate(p, axis=1))
    bias = np.zeros((128, BIAS_COLS), np.float32)
    for r in range(2):
        bias[r, QC:QC + 512] = _stack_columns(g["L0_xattn_b_q"], 8)
        bias[r, KC:KC + 512] = _stack_columns(g["L0_xattn_b_k"], 8)
        bias[r, VC:VC + 128] = g["L0_xattn_b_v"]
        bias[r, OC:OC + 128] = g["L0_xattn_b_o"]
        bias[r, RC:RC + 7] = g["L0_ffn_rb"]
        bias[r, RC + 7] = MASKED
        bias[32 + r, OC:OC + 128] = g["L1_xattn_bo"]
        bias[64 + r, VC:VC + 128] = g["L2_xattn_bv"]
        bias[64 + r, OC:OC + 128] = g["L2_xattn_bo"]
        bias[64 + r, RC:RC + 8] = g["L2_ffn_gate_b"]
        bias[64 + r, B2C:B2C + 1024] = g["L2_ffn_b2"].reshape(-1)
        bias[96 + r, QC:QC + 512] = _stack_columns(bq3, 16)
        bias[96 + r, KC:KC + 512] = _stack_columns(bk3, 16)
        bias[96 + r, VC:VC + 128] = bv3
        bias[96 + r, OC:OC + 128] = g["L3_xattn_mha_out_b"]
        bias[96 + r, QKVC:QKVC + 384] = g["L3_xattn_qkv_b"]
        bias[96 + r, SOC:SOC + 128] = g["L3_xattn_sa_out_b"]
        bias[96 + r, LIN2C:LIN2C + 128] = g["L3_xattn_lin2_b"]
    hidden_bias = np.concatenate([g["L2_ffn_b1"].reshape(32, 128).T, g["L3_xattn_lin1_b"].reshape(4, 128).T], axis=1)
    norm = np.stack([g[f"L3_xattn_ln{i}_{p}"] for i in (1, 2, 3) for p in "gb"])
    norm = np.broadcast_to(norm[None], (128, 6, 128)).reshape(128, 768)

    def swiglu(gate, up, down):
        out = np.zeros((128, 3, 384), np.float32)
        out[:, 0, :gate.shape[0]] = gate.T
        out[:, 1, :up.shape[0]] = up.T
        rows = np.zeros((384, 128), np.float32)
        rows[:down.shape[1]] = down.T
        out[:, 2] = _down_rows(rows)
        return out.reshape(128, 1152)

    e0 = [swiglu(g["L0_ffn_rg"][e], g["L0_ffn_ru"][e], g["L0_ffn_rd"][e]) for e in range(7)]
    e0.append(swiglu(g["L0_ffn_sg"], g["L0_ffn_su"], g["L0_ffn_sd"]))
    arrays["exp0"] = np.stack(e0)
    arrays["exp1"] = np.stack([np.concatenate([g["L1_ffn_Wg"][e], g["L1_ffn_Wu"][e], _down_rows(g["L1_ffn_Wd"][e])],
                                              axis=1) for e in range(8)])
    arrays["exp2"] = np.stack([np.concatenate([g["L2_ffn_w1"][e], _down_rows(g["L2_ffn_w2"][e])], axis=1)
                               for e in range(8)])
    arrays["expdense"] = np.concatenate([g["L3_xattn_lin1_w"].T, _down_rows(g["L3_xattn_lin2_w"].T)], axis=1)[None]
    arrays["exp3"] = np.stack([np.concatenate([g["L3_ffn_w1"][e], _down_rows(g["L3_ffn_w2"][e])], axis=1)
                               for e in range(8)])
    const = _constants()
    arrays.update(x_in=x, ctx_in=ctx, mask_in=mask, bias_in=bias, hidden_bias_in=hidden_bias, norm_in=norm,
                  const_in=const)

    nc = _bacc.Bacc("TRN2", target_bir_lowering=False, num_devices=1)
    arrays = {k: np.ascontiguousarray(v) for k, v in arrays.items()}
    dram = {k: nc.dram_tensor(k, v.shape, mybir.dt.from_np(v.dtype), kind="ExternalInput").ap()
            for k, v in arrays.items()}
    out = nc.dram_tensor("x_out", (128, B * D), F32, kind="ExternalOutput").ap()
    fused_layers(nc, dram["x_in"], dram["ctx_in"], dram["mask_in"], [dram[f"att{l}"] for l in range(LAYERS)],
                 {k: dram[f"exp{k}"] for k in (0, 1, 2, DENSE, 3)}, dram["bias_in"], dram["hidden_bias_in"],
                 dram["norm_in"], dram["const_in"], out)
    r = _run(nc, [arrays], core_ids=[0])
    return np.ascontiguousarray(r.results[0]["x_out"].reshape(128, B, D).transpose(1, 0, 2))
```

```python
import concourse.bass as bass
from concourse import mybir
from contextlib import ExitStack
import numpy as np

F32 = mybir.dt.float32
F32R = mybir.dt.float32r
BF16 = mybir.dt.bfloat16
I32 = mybir.dt.int32
U32 = mybir.dt.uint32
ALU = mybir.AluOpType
ACT = mybir.ActivationFunctionType
AX = mybir.AxisListType

B, S, D = 8, 128, 128
LAYERS = 4
HEAD_DIM = [8, 8, 8, 16]
SCORE_SCALE = [1.0, 128.0 ** -0.5, 8.0 ** -0.5, 16.0 ** -0.5]
SELF_SCALE = 128.0 ** 0.5
MOE_SCALE = [1.0, 12.0 ** -0.5, 1.0, 1.0]
TOP_K = [2, 2, 1, 2]
EXPERTS = 8
DENSE = "dense"
CHUNKS = {0: 3, 1: 4, 2: 4, DENSE: 4, 3: 2}
GATED = {0: True, 1: True, 2: False, DENSE: False, 3: False}
FUNCTION = {0: ACT.Silu, 1: ACT.Silu, 2: ACT.Gelu, DENSE: ACT.Relu, 3: ACT.Gelu}
N_EXPERTS = {0: 8, 1: 8, 2: 8, DENSE: 1, 3: 8}
MASKED = -1e30
FILL = -1e20
EPS = 1e-5
ARENA_BYTES = 58368

QC, KC, VC, OC, RC = 0, 512, 1024, 1152, 1280
QKVC, SOC = 1288, 1672
ATT_COLS = [1288, 1288, 1288, 1800]
BIAS_COLS = 1800
RAW_COLS = 1800
WEIGHT_PARTS = 4
IDENT, MASKS, LAM, IOTA, PICK, TILE, CONST_COLS = 0, 128, 384, 389, 397, 405, 413
LAM_Q, LAM_K, LAM_Q3, LAM_K3, LAM_ROW = range(5)


def expert_cols(kind):
    return CHUNKS[kind] * 128 * (3 if GATED[kind] else 2)


def up_parts(item):
    return 3 if item[0] == "expert" and GATED[EXPERT_LIST[item[1]][0]] else 2


EXPERT_LIST = [(kind, e) for kind in (0, 1, 2, DENSE, 3) for e in range(N_EXPERTS[kind])]


def build_schedule():
    PERIOD = {0: 12.0, 1: 12.0, 2: 12.0, 3: 9.0}
    enter = [(-34, "pre_stats"), (-32.5, "pre_norm"), (-29.4, "xT"), (-28.4, "xT_split")]
    heads = [(-10, "scores0"), (-9, "max0"), (-8.7, "scores1"), (-7.8, "max1"), (-6.5, "max_split"),
             (-4.6, "maxT"), (-4, "max_merge"), (-6.9 + 10, "expscores0"), (4, "exp0"), (4.2, "expscores1"),
             (5, "exp1"), (6.4, "value"), (6.8, "value_copy"), (11.9, "mix"), (14.9, "mix_copy"),
             (16.5, "mixT"), (17, "mix_norm")]
    leave = [(20.6, "oT"), (21.6, "oT_split"), (23.6, "out"), (24.4, "residual")]
    last = [(25, "post_stats"), (26.6, "post_norm"), (28.6, "fT"), (29.5, "fT_split"), (31, "logits")]
    inner = [(-55, "pre_stats"), (-53.5, "pre_norm"), (-52, "tT"), (-51, "tT_split"),
             (-49, "self_qkv"), (-48.5, "self_copy"), (-47.8, "self_dot"), (-46.5, "self_exp"),
             (-45, "self_value"), (-43, "vT"), (-42, "vT_split"), (-40, "self_out"),
             (-39.2, "self_residual"), (-38.5, "mid_stats"), (-36, "mid_norm"), (-29.4, "xT"), (-28.4, "xT_split")]
    one = [s for s in heads if s[1] not in ("scores1", "max1", "expscores1", "exp1")]
    tables = {0: enter + heads + [(18.3, "shuffle_store")],
              1: enter + heads + leave + last,
              2: enter + heads + leave + last,
              3: inner + one + leave + [(25, "cross_stats"), (26.6, "cross_norm"), (28.6, "yT"), (29.5, "yT_split")]}
    at, items = [], []

    def add(time, *step):
        at.append((time, step))

    def weights(time, item, spread=0.0, down_time=None):
        items.append(item)
        up = up_parts(item)
        for part in range(WEIGHT_PARTS):
            at_part = time if down_time is None or part < up else down_time
            add(at_part + part * (spread + 1e-4), "weights", len(items) - 1, part)

    def attention(l, keys, half_ready, all_ready, start, load=()):
        unit = PERIOD[l] / 10
        before = start - 1.5
        if l == 3:
            startup = {kind: 0.5 * (t - inner[0][0]) for t, kind in inner}
            start = max(start, half_ready + startup["xT_split"] + 5.5)
        else:
            startup = {"pre_stats": 0, "pre_norm": 1.3, "xT": 2.2, "xT_split": 2.8}
        zero = start + 10 * unit
        for b in range(B):
            for t, kind in tables[l]:
                at_end = 10 * (B - 1) + 5
                t += 10 * b
                if b == B - 1 and t > at_end + 5:
                    t -= 5
                time = zero + unit * (min(t, at_end) + 0.6 * max(t - at_end, 0))
                ready = half_ready if b < B // 2 else all_ready
                if kind in startup:
                    time = max(time, ready + 0.1 + startup[kind] + (2.6 if l == 3 else 0.7) * (b % 4))
                add(time, kind, l, b)
        for pair in range(B // 2):
            for part in range(2):
                time = zero + unit * (20 * pair - 17.2 + 0.6 * part)
                time = max(time, start - 1.9 + 0.6 * part)
                add(time, "query", l, pair, part)
                add(time + 0.7, "query_split", l, pair, part)
        for s in range(4):
            add(keys + 0.02 + 0.9 * s, "key", l, s, 0)
            add(keys + 0.02 + 0.9 * s + 0.85, "key_split", l, s, 0)
            second = zero + unit * (10 * s - 3.7) if l < 3 else before + 0.9 * s
            add(second, "key", l, s, 1)
            add(second + unit, "key_split", l, s, 1)
        for i, item in enumerate(load):
            weights(zero + 12 * i, item, 3)
        end = max(time for time, step in at if step[0] in ("logits", "fT_split", "yT_split", "shuffle_store"))
        scores_end = max(time for time, step in at if step[0] in ("expscores0", "expscores1"))
        return scores_end, end

    def leave_first(start):
        at_tile = [(0, "oT"), (1, "oT_split"), (3, "out"), (4, "residual"), (4.5, "post_stats"),
                   (6.5, "post_norm"), (8, "fT"), (9, "fT_split"), (11, "logits")]
        add(start, "shuffle_load", 0, 0)
        add(start + 0.1, "shuffle_load", 0, 1)
        for b in range(B):
            for t, kind in at_tile:
                add(start + 3 + 2 * b + t, kind, 0, b)
        return start + 3 + 2 * (B - 1) + 11

    def finish_tiles(start, first_tile):
        table = [(0, "final_stats"), (2.5, "final_norm"), (4.5, "post_stats"), (7, "post_norm"),
                 (8, "fT"), (9, "fT_split"), (11, "logits")]
        for i in range(4):
            for t, kind in table:
                add(start + 1.2 * (2 * i + t), kind, 3, first_tile + i)
        return start + 1.2 * 17

    def feed_forward(kind, start, all_ready):
        units = [(e, n) for e in range(N_EXPERTS[kind]) for n in range(2)]
        if len(units) > 2:
            units[1], units[2] = units[2], units[1]
        up_time = 1.28 if GATED[kind] else 0.64
        before, t, merged = None, start, []

        def down(t, c, e, n):
            if c < CHUNKS[kind] - 1:
                add(t, "down_part", kind, e, n, c)
                return t + 0.64
            add(t, "down", kind, e, n)
            return t + 0.64

        def next_weights(t, e, n):
            x = EXPERT_LIST.index((kind, e)) + 2
            if n == 1 and x < len(EXPERT_LIST) and EXPERT_LIST[x][0] in ((kind,) if kind == 2 else (kind, 3)):
                unit_time = (up_time + 0.64) * CHUNKS[kind]
                weights(t + 0.01, ("expert", x), down_time=t + unit_time + 0.26)

        def finish(t, e, n):
            if kind != DENSE:
                add(t, "weigh", kind, e, n)
            add(t + 0.02, "add_expert", kind, e, n)
            if e == N_EXPERTS[kind] - 1:
                merge = t + (3.8 if kind != DENSE else 0.03)
                add(merge, "merge", kind, n)
                merged.append(merge + 0.02)
                if kind == 3:
                    add(merge + 0.01, "store", n)
            return t + (0.25 if kind != DENSE else 0)

        for i, (e, n) in enumerate(units):
            if i == (2 if kind != DENSE else 1):
                t = max(t, all_ready + 0.1)
                if kind != DENSE:
                    add(t, "route", kind)
            for c in range(CHUNKS[kind]):
                add(t, "up", kind, e, n, c)
                t += up_time
                if before is not None:
                    add(t - 0.01, "hidden_split", kind, *before)
                before = (e, n, c)
                if c == (0 if i > 3 else CHUNKS[kind] - 1) and i >= 3:
                    t = finish(t, *units[i - 2])
                if i:
                    if i == 3 and c == 0:
                        add(t - 0.005, "shareT", kind)
                        t = finish(t, *units[0])
                    t = down(t, c, *units[i - 1])
            next_weights(t, e, n)
        add(t + 0.01, "hidden_split", kind, *before)
        keys = t = finish(t + 0.02, *units[-2])
        t += 4
        for c in range(CHUNKS[kind]):
            t = down(t, c, *units[-1])
        t = finish(t + 0.5, *units[-1])
        return keys, merged[0], t, merged[-1]

    weights(-100, ("attention", 0))
    _, end = attention(0, -10, -60, -60, 0, [("attention", 1), ("expert", 0), ("expert", 1)])
    end_first = leave_first(end + 0.1)
    keys, half, done, merged = feed_forward(0, end + 3 + 15 + 0.5, end_first)
    for l in (1, 2, 3):
        kind = DENSE if l == 3 else l
        first = EXPERT_LIST.index((kind, 0))
        loads = [("expert", first), ("expert", first + 1)]
        if l < 3:
            loads.insert(0, ("attention", l + 1))
        scores_end, end = attention(l, keys, half, merged, done + 2, loads)
        keys, half, done, merged = feed_forward(kind, scores_end + 1, end)
    middle = finish_tiles(half + 0.1, 0)
    end = finish_tiles(max(merged + 0.1, middle - 1.2 * 7), 4)
    feed_forward(3, middle + 0.1, end)
    return [step for _, step in sorted(at, key=lambda s: s[0])], items


def fused_layers(nc, x_in, ctx_in, mask_in, att_w, expert_w, bias_in, hidden_bias_in, norm_in,
                 const_in, x_out):
    steps, items = build_schedule()
    ordinal, per_kind = {}, {}
    for step in steps:
        ordinal[step] = per_kind.get(step[0], 0)
        per_kind[step[0]] = ordinal[step] + 1

    TRANSPOSES = ("xT", "fT", "oT", "tT", "vT", "yT")
    SMALL = TRANSPOSES + ("query", "key", "value", "logits", "maxT", "mix", "mixT", "out", "self_qkv", "self_out",
                          "shareT", "weigh", "merge", "down")
    UNITS = ("scores0", "scores1", "expscores0", "expscores1")
    units = [s for s in steps if s[0] in UNITS]
    unit_at = {s: i for i, s in enumerate(units)}
    small_bank, small_before, held, turn, feeding = {}, {}, {}, [0, 0, 0], False
    rounded_turn, rounded_before = {}, {}
    for s in steps:
        feeding = s[0] == "up" or (feeding and not (s[0] == "add_expert" and s[2:] == (N_EXPERTS[s[1]] - 1, 1)))
        if s[0] in ("query", "key"):
            i = len(rounded_turn)
            rounded_turn[s] = i % 2
            rounded_before[s] = list(rounded_turn)[i - 2] if i >= 2 else None
        if s[0] in ("down", "down_part"):
            s = ("down", *s[1:4])
        if s[0] not in SMALL or s in small_bank:
            continue
        if s[0] == "down":
            bank_number = 2 + turn[0] % 2
            turn[0] += 1
        elif feeding:
            bank_number = turn[1] % 2
            turn[1] += 1
        else:
            bank_number = turn[2] % 4
            turn[2] += 1
        small_bank[s], small_before[s] = bank_number, held.get(bank_number)
        held[bank_number] = s
    READ = {"query": "query_split", "key": "key_split", "value": "value_copy", "maxT": "max_merge",
            "mix": "mix_copy", "mixT": "mix_norm", "out": "residual", "self_qkv": "self_copy", "self_out": "self_residual",
            "logits": "logits_copy", "shareT": "share_rows", "weigh": "weigh_copy", "merge": "merged",
            "down": "add_expert", **{t: f"{t}_lo" for t in TRANSPOSES},
            "scores0": "max", "scores1": "max", "expscores0": "exp", "expscores1": "exp"}

    def read_count(step):
        kind = step[0]
        if kind in ("scores0", "scores1", "expscores0", "expscores1"):
            same = [u for u in units if u[0][:-1] == kind[:-1]]
            return same.index(step) + 1
        return ordinal[step] + 1

    dscratch = nc.dram_tensor("head_major_scratch", (16, B, S, 8), F32, kind="Internal").ap()

    with ExitStack() as stack:
        def sb(name, shape, dtype):
            return stack.enter_context(nc.sbuf_tensor(name, [shape[0], int(np.prod(shape[1:]))], dtype))[:, :]

        arena = {}

        def shared(name, shape, dtype, phase):
            at = arena.setdefault(phase, arena["base"])
            arena[phase] = at + 4 * shape[1]
            assert arena[phase] <= arena["base"] + ARENA_BYTES
            return nc.alloc_sbuf_tensor_at(name, shape, dtype, offset=at)[:, :]

        def split3(ap, a):
            return ap.rearrange("p (a c) -> p a c", a=a)

        sems = {}
        SEMAPHORES = (
            ["loads_x", "loads_ctx", "loads_const", "loads_mask", "loads_bias", "raw0", "raw1", "shuffled0",
             "shuffled1", "unshuffled0", "unshuffled1", "stored", "dve_own", "pool_own", "constants", "const_rows",
             "masks", "context_hi", "context_lo", "weights_split", "variance", "rstd", "pre_norm",
             "mid_norm", "cross_norm", "post_norm", "self_value", "self_copy", "self_dot", "self_exp",
             "self_residual", "query", "query_round", "query_split", "key", "key_round", "key_split",
             "value", "value_copy", "scores", "max", "max_split", "maxT", "max_merge", "share_parts", "shareT",
             "share_rows", "weigh", "weigh_copy", "merge", "merged", "summed", "expscores",
             "exp", "mix", "mix_copy", "mixT", "mix_norm", "out", "residual", "self_qkv", "self_out", "logits", "logits_copy",
             "route_diff", "route_exp", "gate_up", "plain_up", "activated", "hidden", "hidden_hi", "hidden_lo", "down",
             "add_expert", "final_sum"]
            + [f"{t}_{p}" for t in TRANSPOSES for p in ("ps", "hi", "lo")])
        for name in SEMAPHORES:
            sems[name] = stack.enter_context(nc.semaphore(name))

        arena["base"] = (nc.sbuf_base + 31) // 32 * 32
        sb("arena", [128, ARENA_BYTES // 4 + 8], F32)
        x = split3(sb("x", [128, B * D], F32), B)
        ctx = sb("ctx_hi", [128, B * S], F32R), sb("ctx_lo", [128, B * S], F32R)
        att_ring = [(sb(f"att_hi{i}", [128, ATT_COLS[2 + i]], F32R), sb(f"att_lo{i}", [128, ATT_COLS[2 + i]], F32R))
                    for i in range(2)]
        att = [att_ring[l % 2] for l in range(LAYERS)]
        bias = sb("bias_rows", [128, BIAS_COLS], F32R)
        raw = [sb(f"raw{i}", [128, RAW_COLS], F32) for i in range(2)]
        exp_w = [(sb(f"expert_hi{i}", [128, 1536], F32R), sb(f"expert_lo{i}", [128, 1536], F32R))
                 for i in range(2)]
        const = sb("const", [128, CONST_COLS], F32)
        const16 = sb("const16", [128, 384], BF16)
        ident_r = sb("ident_r", [128, 128], F32R)
        pick = sb("pick", [128, 8], F32R)
        ones = sb("ones", [128, 256], F32R)
        minus_half = sb("minus_half", [128, 1], F32)
        hidden_bias = sb("hidden_bias", [128, 36 + 9], F32)
        out_bias = hidden_bias[:, 36:45]
        norms = split3(sb("norms", [128, 6 * D], F32), 6)
        mask1_at = (nc.sbuf_base + 31) // 32 * 32
        mask1 = split3(sb("mask1", [128, B * S], BF16), B)
        stats = [sb(f"stats{i}", [128, 6], F32) for i in range(4)]
        moments = [sb(f"moments{i}", [128, 2], F32) for i in range(4)]
        var_eps = [sb(f"var_eps{i}", [128, 1], F32) for i in range(4)]
        rstd = [sb(f"rstd{i}", [128, 1], F32) for i in range(4)]
        norm_x = [sb(f"norm_x{i}", [128, D], F32) for i in range(2)]
        norm_f = [sb(f"norm_f{i}", [128, D], F32) for i in range(2)]
        turned = {t: [(sb(f"{t}_hi{i}", [128, 128], F32R), sb(f"{t}_lo{i}", [128, 128], F32R))
                      for i in range(2)] for t in ("oT", "tT", "vT")}
        turned["xT"] = [(sb(f"xT_hi{i}", [128, 256], F32R), sb(f"xT_lo{i}", [128, 256], F32R)) for i in range(2)]
        ffn_in = sb("ffn_in_hi", [128, B * S], F32R), sb("ffn_in_lo", [128, B * S], F32R)
        key_stack = split3(shared("key_stack", [128, 4 * B * S], F32R, "attention"), 4)
        query_stack = [split3(shared(f"query_stack{i}", [128, 1024], F32R, "attention"), 4) for i in range(2)]
        query_max = [split3(shared(f"query_max{i}", [128, 512], F32R, "attention"), 4) for i in range(2)]
        rounded = [sb(f"rounded{i}", [128, 512], F32R) for i in range(2)]
        values = [sb(f"values{i}", [128, 16 * 32], F32) for i in range(2)]
        values3 = [nc.alloc_sbuf_tensor_at(f"values_wide{i}", [128, 8 * 32], F32, offset=mask1_at + 1024 * i)[:, :]
                   for i in range(2)]
        mix_rows = sb("mix_rows", [128, 512], F32)
        neg_max = [sb(f"neg_max{i}", [128, 16], F32) for i in range(2)]
        max_parts = [sb(f"max_parts{i}", [128, 512], F32R) for i in range(2)]
        recip = [sb(f"recip{i}", [128, 16], F32) for i in range(2)]
        mixed = [sb(f"mixed{i}", [128, D], F32) for i in range(2)]
        hid_hi, hid_lo = [[], []]
        hid_hi.append(shared("hidden_hi0", [128, 2048], F32R, "ffn"))
        hid_lo.append(shared("hidden_lo0", [128, 2048], F32R, "ffn"))
        hid = [shared(f"hidden{i}", [128, 512], F32, "ffn") for i in range(3)]
        gate = [shared(f"gate{i}", [128, 512], F32, "ffn") for i in range(3)]
        hid_hi.append(shared("hidden_hi1", [128, 2048], F32R, "ffn"))
        hid_lo.append(shared("hidden_lo1", [128, 2048], F32R, "ffn"))
        probs = [shared(f"probs{i}", [128, 2048], F32, "attention") for i in range(2)]
        weight = [shared(f"weight{i}", [128, 512], F32, "ffn") for i in range(2)]
        weighed = [shared(f"weighed{i}", [128, 512], F32, "ffn") for i in range(2)]
        share_rows = shared("share_rows_x", [128, B * 128], F32R, "ffn")
        expert_sum = sb("expert_sum", [128, B * 128], F32)
        tgt = split3(sb("tgt", [128, B * D], F32), B)
        x1 = split3(sb("x1", [128, B * D], F32), B)
        mask_raw = x1.rearrange("p b d -> p (b d)").bitcast(I32)
        unshuffled = tgt
        x2 = tgt
        mid_sum = [sb(f"mid_sum{i}", [128, D], F32) for i in range(2)]
        cross_sum = [sb(f"cross_sum{i}", [128, D], F32) for i in range(2)]
        final_sum = x1
        final_norm = sb("final_norm_x", [128, D], F32)
        self_qkv = [sb(f"self_qkv_x{i}", [128, 384], F32) for i in range(2)]
        self_prod = sb("self_prod", [128, D], F32)
        self_s = [sb(f"self_s{i}", [128, 8], F32) for i in range(2)]
        self_v = [sb(f"self_v{i}", [128, D], F32) for i in range(2)]
        logits = split3(sb("logits_x", [128, B * EXPERTS], F32), B)
        top = split3(sb("top", [128, B * 8], F32), B)
        top_at = split3(sb("top_at", [128, B * 8], U32), B)
        top_atf = split3(sb("top_atf", [128, B * 8], F32), B)
        route_diff = split3(sb("route_diff_x", [128, B * 8], F32), B)
        route_exp = split3(sb("route_exp_x", [128, B * 8], F32), B)
        route_sum = sb("route_sum", [128, B], F32)
        route_r = sb("route_r", [128, B], F32)
        hot = split3(sb("hot", [128, B * 8], F32), B)
        share = split3(sb("share", [128, B * 8], F32), B)
        share_parts = split3(sb("share_parts_x", [128, B * 16], F32R), B)

        ident = const[:, IDENT:IDENT + 128]
        ident16 = const16[:, 0:128]
        mask0, mask2 = const16[:, 128:256], const16[:, 256:384]
        iota = const[:, IOTA:IOTA + 8]

        def lam(i):
            return const[:, LAM + i:LAM + i + 1]

        psum = [stack.enter_context(nc.psum_tensor(f"pair{i}", [128, 1024], F32))[:, :] for i in range(2)]
        small = [stack.enter_context(nc.psum_tensor(f"small{i}", [128, 512], F32))[:, :] for i in range(4)]

        def small_of(step):
            return small[small_bank[step]]

        def unit_of(step):
            return psum[unit_at[step] % 2]

        def bank(i):
            return psum[i // 2][:, 512 * (i % 2):512 * (i % 2) + 512]

        def queries(l, b):
            return query_stack[(l * (B // 2) + b // 2) % 2][:, :, S * (b % 2):S * (b % 2) + S]

        def attn_ordinal(l, b):
            return l * B + b

        def par(l, b):
            return (l * B + b) % 2

        summed = [s for s in steps if s[0] == "add_expert" and s[1] != DENSE and s[2] > 0]

        def sum_count(step):
            return summed.index(step) + 1

        weighs = [s for s in steps if s[0] == "weigh"]

        def n_attn(l):
            return sum(B * (1 if m == 3 else 2) for m in range(l))

        def source(t, l, b):
            k = ordinal[(t, l, b)]
            if t == "xT":
                if l < 3:
                    return norm_x[k % 2], "pre_norm", ordinal[("pre_norm", l, b)] + 1
                return x1[:, b, :], "mid_norm", b + 1
            if t == "tT":
                return tgt[:, b, :], "pre_norm", ordinal[("pre_norm", l, b)] + 1
            if t == "vT":
                return self_v[b % 2], "self_value", b + 1
            if t == "oT":
                if l == 0:
                    return unshuffled[:, b, :], f"unshuffled{b // 4}", 16
                return mixed[par(l, b)], "mix_norm", ordinal[("mix_norm", l, b)] + 1
            if t == "yT":
                return x2[:, b, :], "cross_norm", b + 1
            return norm_f[k % 2], "post_norm", k + 1

        def target(t, l, b):
            if t in ("fT", "yT"):
                return tuple(a[:, S * b:S * b + S] for a in ffn_in)
            if t == "xT":
                return tuple(a[:, S * (b % 2):S * (b % 2) + S] for a in turned["xT"][b // 2 % 2])
            return turned[t][ordinal[(t, l, b)] % 2]

        def chunk_ordinal(kind, e, n, c):
            return ordinal[("up", kind, e, n, c)]

        def plain_before(kind):
            order = (0, 1, 2, DENSE, 3)
            return sum(CHUNKS[m] * N_EXPERTS[m] * 2 for m in order[:order.index(kind)])

        def local_chunk(kind, e, n, c):
            return chunk_ordinal(kind, e, n, c) - plain_before(kind)

        def columns(item):
            return ATT_COLS[item[1]] if item[0] == "attention" else expert_cols(EXPERT_LIST[item[1]][0])

        def part_of(item, part):
            cols = columns(item)
            if item[0] == "attention":
                edge = [(cols * i // WEIGHT_PARTS + 7) // 8 * 8 for i in range(WEIGHT_PARTS)] + [cols]
            else:
                n, width = up_parts(item), 128 * CHUNKS[EXPERT_LIST[item[1]][0]]
                up, down = cols - width, WEIGHT_PARTS - n
                edge = [up * i // n for i in range(n)] + [up + width * i // down for i in range(down)] + [cols]
            return edge[part], edge[part + 1]

        def parts(item):
            return att[item[1]] if item[0] == "attention" else exp_w[item[1] % 2]

        def first_down(x):
            kind = EXPERT_LIST[x][0]
            return expert_cols(kind) - 128 * CHUNKS[kind]

        weight_steps = [s for s in steps if s[0] == "weights"]

        def split_count(item, part=WEIGHT_PARTS - 1):
            return max(weight_steps.index(("weights", items.index(item), p)) for p in range(part + 1)) + 1

        def last_mix(kind, e, n):
            y, l = ordinal[("down", kind, e, n)], 3 if kind == DENSE else kind
            first = [ordinal[s] for s in steps if s[0] == "down" and s[1] == kind][1]
            return B * (l + 1) if y == first and kind != 3 else None

        def on_act(step):
            return GATED[step[1]] or step[4] % 2 == 1

        act_highs = [s for s in steps if s[0] == "hidden_split" and on_act(s)]

        block = stack.enter_context(nc.Block())

        @block.sync
        def _(sp):
            def load_item(i):
                kind, which = items[i]
                cols = columns(items[i])
                if i >= 2:
                    sp.wait_ge(sems["weights_split"], split_count(items[i - 2]))
                if kind == "attention":
                    src = att_w[which]
                else:
                    k, e = EXPERT_LIST[which]
                    src = expert_w[k][e]
                sp.dma_start(raw[i % 2][:, 0:cols], src).then_inc(sems[f"raw{i % 2}"], 16)

            sp.dma_start(const, const_in).then_inc(sems["loads_const"], 16)
            sp.dma_start(x.rearrange("p b d -> p (b d)"), x_in).then_inc(sems["loads_x"], 16)
            load_item(0)
            sp.dma_start(probs[1][:, 0:B * S], ctx_in).then_inc(sems["loads_ctx"], 16)
            load_item(1)
            for step in steps:
                what = step[0]
                if what == "weights" and step[2] == WEIGHT_PARTS - 1 and step[1] + 2 < len(items):
                    load_item(step[1] + 2)
                if what == "shuffle_store":
                    _, l, b = step
                    sp.wait_ge(sems["mix_norm"], b + 1)
                    sp.dma_start(dscratch[:, b, :, :].rearrange("h q d -> q h d"),
                                 split3(mixed[b % 2], 16)).then_inc(sems[f"shuffled{b % 2}"], 16)
                if what == "shuffle_load":
                    n = step[2]
                    if n == 0:
                        sp.wait_ge(sems["shuffled0"], 16 * (B // 2))
                        sp.wait_ge(sems["shuffled1"], 16 * (B // 2))
                    flat = dscratch.rearrange("h b q d -> (h b q d)").rearrange("(t s c) -> s t c", s=S, c=D)
                    sp.dma_start(unshuffled[:, 4 * n:4 * n + 4, :], flat[:, 4 * n:4 * n + 4, :]).then_inc(
                        sems[f"unshuffled{n}"], 16)
                if what == "store":
                    n = step[1]
                    sp.wait_ge(sems["merged"], ordinal[("merge", 3, n)] + 1)
                    sp.dma_start(x_out[:, 512 * n:512 * n + 512],
                                 x[:, 4 * n:4 * n + 4, :].rearrange("p b d -> p (b d)")).then_inc(sems["stored"], 16)
            sp.wait_ge(sems["stored"], 32)

        @block.gpsimd
        def _(pool):
            own = [0]

            def chain(instruction):
                own[0] += 1
                instruction.then_inc(sems["pool_own"], 1)
                pool.wait_ge(sems["pool_own"], own[0])

            pool.dma_start(mask_raw, mask_in).then_inc(sems["loads_mask"], 16)
            pool.dma_start(probs[0][:, 0:BIAS_COLS], bias_in).then_inc(sems["loads_bias"], 16)
            pool.dma_start(hidden_bias, hidden_bias_in).then_inc(sems["loads_mask"], 16)
            pool.dma_start(norms.rearrange("p a c -> p (a c)"), norm_in).then_inc(sems["loads_mask"], 16)
            pool.memset(minus_half, -0.5).then_inc(sems["pool_own"], 1)
            own[0] += 1
            count = 0
            for step in steps:
                what = step[0]
                if what == "weights":
                    _, i, part = step
                    item = items[i]
                    hi, lo = parts(item)
                    a, z = part_of(item, part)
                    if part == 0:
                        pool.wait_ge(sems[f"raw{i % 2}"], 16 * (i // 2 + 1))
                        if item[0] == "attention" and item[1] >= 2:
                            pool.wait_ge(sems["logits"], B * (item[1] - 1))
                        if item[0] == "expert" and item[1] >= 2:
                            kind, e = EXPERT_LIST[item[1] - 2]
                            last_up = ordinal[("up", kind, e, 1, CHUNKS[kind] - 1)] + 1
                            pool.wait_ge(sems["gate_up"], last_up)
                            if GATED[kind]:
                                pool.wait_ge(sems["plain_up"], last_up)
                    if item[0] == "expert" and item[1] >= 2 and z > first_down(item[1] - 2):
                        pool.wait_ge(sems["down"], ordinal[("down", *EXPERT_LIST[item[1] - 2], 1)] + 1)
                    w = raw[i % 2][:, a:z]
                    chain(pool.tensor_scalar(hi[:, a:z], w, 1.0, 1.0, ALU.mult, ALU.mult))
                    pool.tensor_tensor(lo[:, a:z], w, hi[:, a:z].bitcast(F32), ALU.subtract).then_inc(
                        sems["weights_split"], 1)
                    if i == 0 and part == WEIGHT_PARTS - 1:
                        pool.wait_ge(sems["loads_mask"], 48)
                        pool.tensor_scalar(mask1.rearrange("p b k -> p (b k)"), mask_raw, 0.0, FILL,
                                           ALU.is_equal, ALU.mult).then_inc(sems["masks"], 1)
                if what == "add_expert" and step in summed:
                    _, kind, e, n = step
                    y = ordinal[step]
                    total = expert_sum[:, 512 * n:512 * n + 512]
                    pool.wait_ge(sems["add_expert"], y + 1)
                    if sum_count(step) > 2:
                        pool.wait_ge(sems["summed"], sum_count(step) - 2)
                    pool.tensor_tensor(total, total, weighed[sum_count(step) % 2], ALU.add).then_inc(sems["summed"], 1)
                if what.endswith("_stats"):
                    i = count % 4
                    count += 1
                    pool.wait_ge(sems["variance"], count)
                    if count == 1:
                        pool.wait_ge(sems["pool_own"], 1)
                    pool.tensor_tensor(rstd[i], var_eps[i], minus_half, ALU.pow).then_inc(sems["rstd"], 1)

        @block.scalar
        def _(act):
            act.wait_ge(sems["loads_ctx"], 16)
            act.activation(ctx[0], probs[1][:, 0:B * S], ACT.Copy).then_inc(sems["context_hi"], 1)
            act.wait_ge(sems["loads_bias"], 16)
            act.activation(bias, probs[0][:, 0:BIAS_COLS], ACT.Copy).then_inc(sems["const_rows"], 1)
            for step in steps:
                what = step[0]
                if what.endswith("_split") and what[:-6] in TRANSPOSES:
                    t, l, b = what[:-6], step[1], step[2]
                    k = ordinal[(t, l, b)]
                    hi, _ = target(t, l, b)
                    act.wait_ge(sems[f"{t}_ps"], k + 1)
                    if t == "xT" and (l, b) >= (0, 4):
                        act.wait_ge(sems["query"], 2 * (l * (B // 2) + b // 2 - 1))
                    if t in ("tT", "vT", "oT") and k >= 2:
                        user = {"tT": "self_qkv", "vT": "self_out", "oT": "out"}[t]
                        act.wait_ge(sems[user], k - 1)
                    act.activation(hi, small_of((t, l, b))[:, 0:128], ACT.Copy).then_inc(sems[f"{t}_hi"], 1)
                elif what in ("query_split", "key_split"):
                    w = what[:-6]
                    k = ordinal[(w, *step[1:])]
                    act.wait_ge(sems[w], k + 1)
                    before = rounded_before[(w, *step[1:])]
                    if before is not None:
                        act.wait_ge(sems[READ[before[0]]], read_count(before))
                    act.activation(rounded[rounded_turn[(w, *step[1:])]], small_of((w, *step[1:])), ACT.Copy).then_inc(
                        sems[f"{w}_round"], 1)
                elif what == "value_copy":
                    _, l, b = step
                    k = ordinal[step]
                    act.wait_ge(sems["value"], k + 1)
                    if b == 0:
                        act.wait_ge(sems["constants"], 3 if l == 3 else 1)
                    if k >= 2:
                        act.wait_ge(sems["mix"], k - 1)
                    d = HEAD_DIM[l]
                    to = split3((values3 if l == 3 else values)[par(l, b)], 128 // d)[:, :, 0:d]
                    act.activation(to, split3(small_of(("value", l, b))[:, 0:128], 128 // d),
                                   ACT.Copy).then_inc(sems["value_copy"], 1)
                elif what == "mix_copy":
                    _, l, b = step
                    k = attn_ordinal(l, b)
                    act.wait_ge(sems["mix"], k + 1)
                    if k:
                        act.wait_ge(sems["mixT"], k)
                    r = 128 if l < 3 else 64
                    act.activation(mix_rows[0:r, :], small_of(("mix", l, b))[0:r, :], ACT.Copy).then_inc(
                        sems["mix_copy"], 1)
                elif what in ("exp0", "exp1"):
                    _, l, b = step
                    half = int(what[-1])
                    unit = (f"expscores{half}", l, b)
                    act.wait_ge(sems["expscores"], read_count(unit))
                    k = attn_ordinal(l, b)
                    if k >= 2 and half == 0:
                        act.wait_ge(sems["mix"], k - 1)
                    act.activation(probs[k % 2][:, 1024 * half:1024 * half + 1024], unit_of(unit), ACT.Exp,
                                   scale=SCORE_SCALE[l]).then_inc(sems["exp"], 1)
                elif what == "self_copy":
                    _, l, b = step
                    act.wait_ge(sems["self_qkv"], b + 1)
                    if b >= 2:
                        act.wait_ge(sems["self_value"], b - 1)
                    act.activation(self_qkv[b % 2], small_of(("self_qkv", l, b))[:, 0:384], ACT.Copy).then_inc(
                        sems["self_copy"], 1)
                elif what == "self_exp":
                    _, l, b = step
                    act.wait_ge(sems["self_dot"], b + 1)
                    s = self_s[b % 2]
                    act.activation(s[:, 3:4], s[:, 1:2], ACT.Exp, bias=s[:, 2:3]).then_inc(sems["self_exp"], 1)
                elif what == "route":
                    k = ordinal[step]
                    act.wait_ge(sems["route_diff"], k + 1)
                    width = 8 if TOP_K[step[1]] == 1 else 2
                    act.activation(route_exp[:, :, 0:width], route_diff[:, :, 0:width], ACT.Exp).then_inc(
                        sems["route_exp"], 1)
                elif what == "weigh":
                    k = ordinal[step]
                    act.wait_ge(sems["weigh"], k + 1)
                    if k >= 2:
                        act.wait_ge(sems["add_expert"], ordinal[("down", *weighs[k - 2][1:])] + 1)
                    act.activation(weight[k % 2], small_of(step), ACT.Copy).then_inc(sems["weigh_copy"], 1)
                elif what == "up":
                    _, kind, e, n, c = step
                    k, j = ordinal[step], local_chunk(kind, e, n, c)
                    act.wait_ge(sems["gate_up"], k + 1)
                    if GATED[kind]:
                        if j >= 3:
                            act.wait_ge(sems["hidden"], k - 2)
                        act.activation(gate[j % 3], bank(2 * j % 4), FUNCTION[kind]).then_inc(sems["activated"], 1)
                    else:
                        if j >= 3:
                            act.wait_ge(sems["hidden_lo"], k - 2)
                        col = 4 * e + c if kind == 2 else 32 + c
                        extra = dict(bias=hidden_bias[:, col:col + 1]) if kind in (2, DENSE) else {}
                        act.activation(hid[j % 3], bank(j % 4), FUNCTION[kind], **extra).then_inc(
                            sems["activated"], 1)
                elif what == "hidden_split":
                    _, kind, e, n, c = step
                    k, j = chunk_ordinal(kind, e, n, c), local_chunk(kind, e, n, c)
                    if on_act(step):
                        y = ordinal[("down", kind, e, n)]
                        if GATED[kind]:
                            act.wait_ge(sems["hidden"], k + 1)
                        else:
                            act.wait_ge(sems["activated"], k + 1)
                        if y >= 2:
                            act.wait_ge(sems["down"], y - 1)
                        if last_mix(kind, e, n) is not None:
                            act.wait_ge(sems["mix"], last_mix(kind, e, n))
                        act.activation(hid_hi[y % 2][:, 512 * c:512 * c + 512], hid[j % 3], ACT.Copy).then_inc(
                            sems["hidden_hi"], 1)

        @block.vector
        def _(dve):
            own = [0]

            def chain(instruction):
                own[0] += 1
                instruction.then_inc(sems["dve_own"], 1)
                dve.wait_ge(sems["dve_own"], own[0])

            norm_count = [0]
            pending = {}

            def statistics(key, src):
                i = norm_count[0] % 4
                norm_count[0] += 1
                pending[key] = i, norm_count[0]
                chain(dve.bn_stats(stats[i], src))
                chain(dve.bn_aggr(moments[i], stats[i]))
                dve.tensor_scalar(var_eps[i], moments[i][:, 1:2], EPS, None, ALU.add).then_inc(sems["variance"], 1)

            def normalize(key, out, src):
                i, count = pending.pop(key)
                dve.wait_ge(sems["rstd"], count)
                return dve.tensor_scalar(out, src, moments[i][:, 0:1], rstd[i], ALU.subtract, ALU.mult)

            def affine(out, which):
                chain(dve.tensor_tensor(out, out, norms[:, 2 * which, :], ALU.mult))
                return dve.tensor_tensor(out, out, norms[:, 2 * which + 1, :], ALU.add)

            def x_ready(l, b):
                if l == 0:
                    dve.wait_ge(sems["loads_x"], 16)
                else:
                    n = b // 4
                    dve.wait_ge(sems["merged"], ordinal[("merge", l - 1, n)] + 1)

            for i in range(2):
                dve.memset(max_parts[i].bitcast(F32), 0.0)
                chain(dve.memset(values[i], 0.0))
                last = dve.memset(split3(values[i], 16)[:, :, 8:9], 1.0)
            last.then_inc(sems["constants"], 1)
            dve.wait_ge(sems["loads_const"], 16)
            dve.tensor_copy(ident_r, ident)
            dve.tensor_copy(const16, const[:, IDENT:IDENT + 384])
            dve.tensor_copy(pick, const[:, PICK:PICK + 8])
            dve.memset(ones.bitcast(F32), 1.0).then_inc(sems["constants"], 1)
            dve.wait_ge(sems["context_hi"], 1)
            dve.tensor_tensor(ctx[1], probs[1][:, 0:B * S], ctx[0].bitcast(F32), ALU.subtract).then_inc(
                sems["context_lo"], 1)
            dve.wait_ge(sems["const_rows"], 1)
            dve.scalar_tensor_tensor(bias, bias.bitcast(F32), lam(LAM_ROW), probs[0][:, 0:BIAS_COLS],
                                     ALU.mult, ALU.add).then_inc(sems["const_rows"], 1)
            dve.wait_ge(sems["loads_mask"], 48)

            for step in steps:
                what = step[0]
                if what.endswith("_split") and what[:-6] in TRANSPOSES:
                    t, l, b = what[:-6], step[1], step[2]
                    k = ordinal[(t, l, b)]
                    hi, lo = target(t, l, b)
                    dve.wait_ge(sems[f"{t}_hi"], k + 1)
                    dve.tensor_tensor(lo, small_of((t, l, b))[:, 0:128], hi.bitcast(F32), ALU.subtract).then_inc(
                        sems[f"{t}_lo"], 1)
                elif what in ("query_split", "key_split"):
                    w, l, which, part = what[:-6], *step[1:]
                    k = ordinal[(w, *step[1:])]
                    dve.wait_ge(sems[f"{w}_round"], k + 1)
                    got, temp = small_of((w, *step[1:])), rounded[rounded_turn[(w, *step[1:])]]
                    column = lam((LAM_Q if w == "query" else LAM_K) + (2 if l == 3 else 0))
                    if w == "query":
                        pair = l * (B // 2) + which
                        if pair >= 2 and part == 0:
                            dve.wait_ge(sems["max_merge"], 2 * (pair - 1))
                            dve.wait_ge(sems["maxT"], 2 * (pair - 1))
                        to = query_stack[pair % 2][:, 2 * part:2 * part + 2, :]
                        got, temp = split3(got, 2), split3(temp, 2)
                    else:
                        to = key_stack[:, which, 512 * part:512 * part + 512]
                    dve.scalar_tensor_tensor(to, temp.bitcast(F32), column, got, ALU.mult, ALU.add).then_inc(
                        sems[what], 1)
                elif what == "pre_stats":
                    _, l, b = step
                    if l == 3 and b == 0:
                        for i in range(2):
                            chain(dve.memset(values3[i], 0.0))
                            last = dve.memset(split3(values3[i], 8)[:, :, 16:17], 1.0)
                        last.then_inc(sems["constants"], 1)
                    x_ready(l, b)
                    statistics(step[1:], x[:, b, :])
                elif what == "pre_norm":
                    _, l, b = step
                    k = ordinal[step]
                    if l == 3:
                        out = tgt[:, b, :]
                    else:
                        out = norm_x[k % 2]
                        if k >= 2:
                            dve.wait_ge(sems["xT_ps"], k - 1)
                    normalize(step[1:], out, x[:, b, :]).then_inc(sems["pre_norm"], 1)
                elif what in ("max0", "max1"):
                    _, l, b = step
                    half = int(what[-1])
                    unit = (f"scores{half}", l, b)
                    dve.wait_ge(sems["scores"], read_count(unit))
                    dve.tensor_reduce(neg_max[par(l, b)][:, 8 * half:8 * half + 8], split3(unit_of(unit), 8),
                                      AX.X, ALU.max, negate=True).then_inc(sems["max"], 1)
                elif what == "max_split":
                    _, l, b = step
                    k = attn_ordinal(l, b)
                    dve.wait_ge(sems["max"], n_attn(l) + (b + 1) * (1 if l == 3 else 2))
                    if k >= 2:
                        dve.wait_ge(sems["maxT"], k - 1)
                    heads = 128 // HEAD_DIM[l] // 4
                    m = split3(neg_max[k % 2][:, 0:4 * heads], heads)
                    to = max_parts[k % 2].rearrange("p (s j r) -> p j s r", s=4, j=heads)
                    r = 3 * (128 // heads) // 4
                    if l == 3 and b < 2:
                        chain(dve.memset(max_parts[k % 2].bitcast(F32), 0.0))
                    chain(dve.tensor_copy(to[:, :, :, r], m))
                    dve.tensor_tensor(to[:, :, :, r + 1], m, to[:, :, :, r].bitcast(F32), ALU.subtract).then_inc(
                        sems["max_split"], 1)
                elif what == "max_merge":
                    _, l, b = step
                    k = attn_ordinal(l, b)
                    dve.wait_ge(sems["maxT"], k + 1)
                    if k >= 2:
                        l2, b2 = divmod(k - 2, B)
                        dve.wait_ge(sems["expscores"], n_attn(l2) + (b2 + 1) * (1 if l2 == 3 else 2))
                    dve.tensor_tensor(query_max[k % 2], queries(l, b).bitcast(F32),
                                      split3(small_of(("maxT", l, b)), 4), ALU.add).then_inc(sems["max_merge"], 1)
                elif what == "mix_norm":
                    _, l, b = step
                    k = attn_ordinal(l, b)
                    d = HEAD_DIM[l]
                    heads = 128 // d
                    got = small_of(("mixT", l, b))[:, 0:4 * 32 * (heads // 4)].rearrange(
                        "p (s j r) -> p j s r", s=4, r=32)
                    dve.wait_ge(sems["mixT"], k + 1)
                    if k >= 2:
                        dve.wait_ge(sems["mix_norm"], k - 1)
                    r4 = recip[k % 2][:, 0:heads].rearrange("p (j s) -> p j s", s=4)
                    chain(dve.reciprocal(r4, got[:, :, :, d]))
                    if l == 0 and b >= 2:
                        dve.wait_ge(sems[f"shuffled{b % 2}"], 16 * (b // 2))
                    elif l == 1 and b < 2:
                        dve.wait_ge(sems[f"shuffled{b % 2}"], 16 * (B // 2))
                    elif l > 0:
                        dve.wait_ge(sems["oT_ps"], k - 1)
                    dve.tensor_tensor(mixed[k % 2].rearrange("p (j s d) -> p j s d", s=4, d=d), got[:, :, :, 0:d],
                                      r4.unsqueeze(3).to_broadcast([128, heads // 4, 4, d]),
                                      ALU.mult).then_inc(sems["mix_norm"], 1)
                elif what == "residual":
                    _, l, b = step
                    k = ordinal[step]
                    dve.wait_ge(sems["out"], k + 1)
                    got = small_of(("out", l, b))[:, 0:128]
                    if l < 3:
                        dve.tensor_tensor(x[:, b, :], x[:, b, :], got, ALU.add).then_inc(sems["residual"], 1)
                    else:
                        dve.tensor_tensor(cross_sum[b % 2], x1[:, b, :], got, ALU.add).then_inc(sems["residual"], 1)
                elif what == "cross_stats":
                    _, l, b = step
                    dve.wait_ge(sems["residual"], ordinal[("residual", l, b)] + 1)
                    statistics(("cross", b), cross_sum[b % 2])
                elif what == "cross_norm":
                    _, l, b = step
                    chain(normalize(("cross", b), x2[:, b, :], cross_sum[b % 2]))
                    affine(x2[:, b, :], 1).then_inc(sems["cross_norm"], 1)
                elif what == "self_dot":
                    _, l, b = step
                    s = self_s[b % 2]
                    dve.wait_ge(sems["self_copy"], b + 1)
                    qkv = self_qkv[b % 2]
                    chain(dve.tensor_tensor(self_prod, qkv[:, 0:128], qkv[:, 128:256], ALU.mult))
                    chain(dve.tensor_reduce(s[:, 0:1], self_prod, AX.X, ALU.add))
                    chain(dve.tensor_scalar(s[:, 1:2], s[:, 0:1], SELF_SCALE, None, ALU.mult))
                    dve.tensor_scalar(s[:, 2:3], s[:, 1:2], -1.0, None, ALU.mult).then_inc(sems["self_dot"], 1)
                elif what == "self_value":
                    _, l, b = step
                    s = self_s[b % 2]
                    dve.wait_ge(sems["self_exp"], b + 1)
                    chain(dve.reciprocal(s[:, 4:5], s[:, 3:4]))
                    if b >= 2:
                        dve.wait_ge(sems["vT_ps"], b - 1)
                    dve.tensor_scalar(self_v[b % 2], self_qkv[b % 2][:, 256:384], s[:, 3:4], s[:, 4:5],
                                      ALU.mult, ALU.mult).then_inc(sems["self_value"], 1)
                elif what == "mid_stats":
                    _, l, b = step
                    dve.wait_ge(sems["self_out"], b + 1)
                    dve.tensor_tensor(mid_sum[b % 2], tgt[:, b, :], small_of(("self_out", l, b))[:, 0:128],
                                      ALU.add).then_inc(sems["self_residual"], 1)
                    dve.wait_ge(sems["self_residual"], b + 1)
                    statistics(("mid", b), mid_sum[b % 2])
                elif what == "mid_norm":
                    _, l, b = step
                    chain(normalize(("mid", b), x1[:, b, :], mid_sum[b % 2]))
                    affine(x1[:, b, :], 0).then_inc(sems["mid_norm"], 1)
                elif what == "final_stats":
                    _, l, b = step
                    dve.wait_ge(sems["merged"], ordinal[("merge", DENSE, b // 4)] + 1)
                    statistics(("final", b), final_sum[:, b, :])
                elif what == "final_norm":
                    _, l, b = step
                    chain(normalize(("final", b), final_norm, final_sum[:, b, :]))
                    chain(affine(final_norm, 2))
                    dve.tensor_tensor(x[:, b, :], x[:, b, :], final_norm, ALU.add).then_inc(sems["final_sum"], 1)
                elif what == "post_stats":
                    _, l, b = step
                    if l < 3:
                        dve.wait_ge(sems["residual"], ordinal[("residual", l, b)] + 1)
                    else:
                        dve.wait_ge(sems["final_sum"], b + 1)
                    statistics(("post", l, b), x[:, b, :])
                elif what == "post_norm":
                    _, l, b = step
                    k = ordinal[step]
                    if k >= 2:
                        dve.wait_ge(sems["fT_ps"], k - 1)
                    normalize(("post", l, b), norm_f[k % 2], x[:, b, :]).then_inc(sems["post_norm"], 1)
                elif what == "logits":
                    _, l, b = step
                    dve.wait_ge(sems["logits"], ordinal[step] + 1)
                    dve.tensor_copy(logits[:, b, :], small_of(step)[:, 0:8]).then_inc(sems["logits_copy"], 1)
                elif what == "route":
                    l = step[1]
                    k = ordinal[step]
                    dve.wait_ge(sems["logits_copy"], B * (k + 1))
                    for b in range(B):
                        last = dve.max(top[:, b, :], logits[:, b, :])
                    chain(last)
                    for b in range(B):
                        last = dve.max_index(top_at[:, b, :], top[:, b, :], logits[:, b, :])
                    chain(last)
                    chain(dve.tensor_copy(top_atf, top_at))
                    width = 8 if TOP_K[l] == 1 else 2
                    scores = logits if width == 8 else top
                    dve.tensor_tensor(route_diff[:, :, 0:width], scores[:, :, 0:width],
                                      top[:, :, 0:1].to_broadcast([128, B, width]), ALU.subtract).then_inc(
                        sems["route_diff"], 1)
                    dve.wait_ge(sems["route_exp"], k + 1)
                    chain(dve.tensor_reduce(route_sum, route_exp[:, :, 0:width], AX.X, ALU.add))
                    if MOE_SCALE[l] != 1.0:
                        chain(dve.tensor_scalar(route_sum, route_sum, 1.0 / MOE_SCALE[l], None, ALU.mult))
                    chain(dve.reciprocal(route_r, route_sum))
                    for i in range(TOP_K[l]):
                        chain(dve.tensor_tensor(hot, iota.unsqueeze(1).to_broadcast([128, B, 8]),
                                                top_atf[:, :, i:i + 1].to_broadcast([128, B, 8]), ALU.is_equal))
                        to = share if i == 0 else hot
                        if TOP_K[l] == 1:
                            chain(dve.tensor_tensor(to, hot, route_r.unsqueeze(2).to_broadcast([128, B, 8]),
                                                    ALU.mult))
                            continue
                        chain(dve.tensor_tensor(hot, hot, route_exp[:, :, i:i + 1].to_broadcast([128, B, 8]),
                                                ALU.mult))
                        chain(dve.tensor_tensor(to, hot, route_r.unsqueeze(2).to_broadcast([128, B, 8]), ALU.mult))
                        if i:
                            chain(dve.tensor_tensor(share, share, hot, ALU.add))
                    if l == 0:
                        chain(dve.memset(share[:, :, 7:8], 1.0))
                    if k:
                        dve.wait_ge(sems["shareT"], k)
                    chain(dve.tensor_copy(share_parts[:, :, 0:8], share))
                    dve.tensor_tensor(share_parts[:, :, 8:16], share, share_parts[:, :, 0:8].bitcast(F32),
                                      ALU.subtract).then_inc(sems["share_parts"], 1)
                elif what == "shareT":
                    k = ordinal[step]
                    dve.wait_ge(sems["shareT"], k + 1)
                    dve.tensor_tensor(split3(share_rows, B),
                                      small_of(step)[:, 0:128].unsqueeze(1).to_broadcast([128, B, 128]),
                                      const[:, TILE:TILE + 8].unsqueeze(2).to_broadcast([128, B, 128]),
                                      ALU.mult).then_inc(sems["share_rows"], 1)
                elif what == "up":
                    _, kind, e, n, c = step
                    k, j = ordinal[step], local_chunk(kind, e, n, c)
                    if GATED[kind]:
                        dve.wait_ge(sems["plain_up"], k + 1)
                        dve.wait_ge(sems["activated"], k + 1)
                        if j >= 3:
                            dve.wait_ge(sems["hidden_lo"], k - 2)
                        dve.tensor_tensor(hid[j % 3], gate[j % 3], bank((2 * j + 1) % 4), ALU.mult).then_inc(
                            sems["hidden"], 1)
                elif what == "hidden_split":
                    _, kind, e, n, c = step
                    k, j = chunk_ordinal(kind, e, n, c), local_chunk(kind, e, n, c)
                    y = ordinal[("down", kind, e, n)]
                    hi = hid_hi[y % 2][:, 512 * c:512 * c + 512]
                    if y >= 2:
                        dve.wait_ge(sems["down"], y - 1)
                    if last_mix(kind, e, n) is not None:
                        dve.wait_ge(sems["mix"], last_mix(kind, e, n))
                    if on_act(step):
                        dve.wait_ge(sems["hidden_hi"], act_highs.index(step) + 1)
                    else:
                        dve.wait_ge(sems["activated"], k + 1)
                        chain(dve.tensor_copy(hi, hid[j % 3]))
                    dve.tensor_tensor(hid_lo[y % 2][:, 512 * c:512 * c + 512], hid[j % 3], hi.bitcast(F32),
                                      ALU.subtract).then_inc(sems["hidden_lo"], 1)
                elif what == "add_expert":
                    _, kind, e, n = step
                    y = ordinal[step]
                    dve.wait_ge(sems["down"], y + 1)
                    got = small_of(("down", *step[1:]))
                    total = expert_sum[:, 512 * n:512 * n + 512]
                    if e == 0 and (kind != 0):
                        order = (0, 1, 2, DENSE, 3)
                        dve.wait_ge(sems["merge"], ordinal[("merge", order[order.index(kind) - 1], n)] + 1)
                    if kind == DENSE:
                        dve.tensor_scalar(total, got, out_bias[:, 8:9], None, ALU.add).then_inc(
                            sems["add_expert"], 1)
                        continue
                    k = ordinal[("weigh", *step[1:])]
                    dve.wait_ge(sems["weigh_copy"], k + 1)
                    if e == 0:
                        to = total
                    else:
                        to = weighed[sum_count(step) % 2]
                        if sum_count(step) > 2:
                            dve.wait_ge(sems["summed"], sum_count(step) - 2)
                    if kind == 2:
                        dve.scalar_tensor_tensor(to, got, out_bias[:, e:e + 1], weight[k % 2], ALU.add,
                                                 ALU.mult).then_inc(sems["add_expert"], 1)
                    else:
                        dve.tensor_tensor(to, weight[k % 2], got, ALU.mult).then_inc(sems["add_expert"], 1)
                elif what == "merge":
                    _, kind, n = step
                    dve.wait_ge(sems["merge"], ordinal[step] + 1)
                    got = split3(small_of(step), 4)
                    if kind == DENSE:
                        dve.tensor_tensor(final_sum[:, 4 * n:4 * n + 4, :], x2[:, 4 * n:4 * n + 4, :], got, ALU.add).then_inc(
                            sems["merged"], 1)
                    else:
                        tiles = x[:, 4 * n:4 * n + 4, :]
                        dve.tensor_tensor(tiles, tiles, got, ALU.add).then_inc(sems["merged"], 1)

        @block.tensor
        def _(pe):
            def product(out, left, right, row=None, start=True, stop=True):
                (lh, ll), (rh, rl) = left, right
                if row is not None:
                    pe.matmul(out, *row, start=start, stop=False, skip_group_check=True)
                    start = False
                pe.matmul(out, lh, rh, start=start, stop=False, skip_group_check=True)
                pe.matmul(out, lh, rl, start=False, stop=False, skip_group_check=True)
                return pe.matmul(out, ll, rh, start=False, stop=stop, skip_group_check=True)

            def cut(pair, a, z):
                return pair[0][:, a:z], pair[1][:, a:z]

            def free_small(step):
                before = small_before[step]
                if before is not None:
                    pe.wait_ge(sems[READ[before[0]]], read_count(before))

            def free_unit(step):
                i = unit_at[step]
                if i >= 2:
                    before = units[i - 2]
                    pe.wait_ge(sems[READ[before[0]]], read_count(before))

            def bias_rows(l, a, z):
                return bias[32 * l:32 * l + 2, a:z]

            def ones_rows(l):
                return ones[32 * l:32 * l + 2, 0:128]

            def token_row(l, a, z):
                return ones_rows(l), bias_rows(l, a, z)

            def mask_of(l, b):
                return {0: mask0, 1: mask1[:, b, :], 2: mask2}[l]

            def rows(l, j):
                size = 32 if l < 3 else 64
                return slice(size * j, size * j + size)

            pe.wait_ge(sems["constants"], 2)
            pe.wait_ge(sems["context_lo"], 1)
            pe.wait_ge(sems["const_rows"], 2)
            pe.wait_ge(sems["loads_mask"], 48)
            pe.wait_ge(sems["loads_const"], 16)
            for step in steps:
                what = step[0]
                if what in TRANSPOSES:
                    _, l, b = step
                    src, sem, value = source(*step)
                    pe.wait_ge(sems[sem], value)
                    free_small(step)
                    pe.transpose(small_of(step)[:, 0:128], src, ident).then_inc(sems[f"{what}_ps"], 1)
                elif what == "query":
                    _, l, pair, part = step
                    pe.wait_ge(sems["xT_lo"], ordinal[("xT", l, 2 * pair + 1)] + 1)
                    free_small(step)
                    to = split3(small_of(step), 2)
                    for i in range(2):
                        a = QC + 128 * (2 * part + i)
                        row = (bias_rows(l, a, a + 128), ones[32 * l:32 * l + 2, 0:256]) if l in (0, 3) else None
                        last = product(to[:, i, :], cut(att[l], a, a + 128), turned["xT"][pair % 2], row)
                    last.then_inc(sems["query"], 1)
                elif what == "key":
                    _, l, s, n = step
                    if s == 0 and n == 0:
                        pe.wait_ge(sems["weights_split"], split_count(("attention", l)))
                    free_small(step)
                    a = KC + 128 * s
                    product(small_of(step), cut(att[l], a, a + 128), cut(ctx, 512 * n, 512 * n + 512),
                            (bias_rows(l, a, a + 128),
                             ones[32 * l:32 * l + 2, 0:256].unsqueeze(1).to_broadcast([2, 2, 256]))).then_inc(sems["key"], 1)
                elif what == "value":
                    _, l, b = step
                    free_small(step)
                    product(small_of(step)[:, 0:128], cut(ctx, S * b, S * b + S), cut(att[l], VC, VC + 128),
                            token_row(l, VC, VC + 128) if l != 1 else None).then_inc(sems["value"], 1)
                elif what in ("scores0", "scores1"):
                    _, l, b = step
                    half = int(what[-1])
                    q, k = queries(l, b), key_stack[:, :, S * b:S * b + S]
                    pe.wait_ge(sems["query_split"], 2 * (l * (B // 2) + b // 2 + 1))
                    pe.wait_ge(sems["key_split"], 8 * l + 4 * (b // 4) + 4)
                    if l == 1 and b == 0:
                        pe.wait_ge(sems["masks"], 1)
                    free_unit(step)
                    to = unit_of(step).rearrange("p (j s k) -> p j s k", j=2, s=4)
                    if l < 3:
                        for jj in range(2):
                            pe.matmul(to[:, jj], ident16, mask_of(l, b).unsqueeze(1).to_broadcast([128, 4, 128]),
                                      start=True, stop=False, skip_group_check=True)
                    for s in range(4):
                        for jj in range(2):
                            r = rows(l, 2 * half + jj)
                            last = pe.matmul(to[:, jj, s, :], q[r, s, :], k[r, s, :], start=(l == 3), stop=True,
                                             skip_group_check=True)
                    last.then_inc(sems["scores"], 1)
                elif what == "maxT":
                    _, l, b = step
                    k = attn_ordinal(l, b)
                    pe.wait_ge(sems["max_split"], k + 1)
                    free_small(step)
                    to, parts_ = split3(small_of(step), 4), split3(max_parts[k % 2], 4)
                    for s in range(4):
                        last = pe.matmul(to[:, s, :], parts_[:, s, :], ident_r, start=True, stop=True)
                    last.then_inc(sems["maxT"], 1)
                elif what in ("expscores0", "expscores1"):
                    _, l, b = step
                    half = int(what[-1])
                    q, k = query_max[par(l, b)], key_stack[:, :, S * b:S * b + S]
                    pe.wait_ge(sems["max_merge"], attn_ordinal(l, b) + 1)
                    free_unit(step)
                    to = unit_of(step).rearrange("p (j s q) -> p j s q", j=2, s=4)
                    if l < 3:
                        for jj in range(2):
                            pe.matmul(to[:, jj], mask_of(l, b), ident16.unsqueeze(1).to_broadcast([128, 4, 128]),
                                      start=True, stop=False, skip_group_check=True)
                    for s in range(4):
                        for jj in range(2):
                            r = rows(l, 2 * half + jj)
                            last = pe.matmul(to[:, jj, s, :], k[r, s, :], q[r, s, :], start=(l == 3), stop=True,
                                             skip_group_check=True)
                    last.then_inc(sems["expscores"], 1)
                elif what == "mix":
                    _, l, b = step
                    k = attn_ordinal(l, b)
                    d = HEAD_DIM[l]
                    heads = 128 // d
                    pe.wait_ge(sems["exp"], n_attn(l) + (b + 1) * (1 if l == 3 else 2))
                    pe.wait_ge(sems["value_copy"], k + 1)
                    free_small(step)
                    p = split3(probs[k % 2], 16)
                    v = split3((values3 if l == 3 else values)[k % 2], heads)
                    for h in range(heads):
                        j, s = divmod(h, 4)
                        last = pe.matmul(small_of(step)[32 * j:32 * j + 32, 128 * s:128 * s + 128], v[:, h, :],
                                         p[:, h, :], start=True, stop=True, skip_group_check=True)
                    last.then_inc(sems["mix"], 1)
                elif what == "mixT":
                    _, l, b = step
                    pe.wait_ge(sems["mix_copy"], attn_ordinal(l, b) + 1)
                    free_small(step)
                    r = 128 if l < 3 else 64
                    for s in range(4):
                        last = pe.transpose(small_of(step)[:, r * s:r * s + r],
                                            mix_rows[0:r, 128 * s:128 * s + 128], ident[0:r, 0:r])
                    last.then_inc(sems["mixT"], 1)
                elif what == "out":
                    _, l, b = step
                    k = ordinal[("oT", l, b)]
                    pe.wait_ge(sems["oT_lo"], k + 1)
                    free_small(step)
                    product(small_of(step)[:, 0:128], turned["oT"][k % 2], cut(att[l], OC, OC + 128),
                            token_row(l, OC, OC + 128)).then_inc(sems["out"], 1)
                elif what == "self_qkv":
                    _, l, b = step
                    pe.wait_ge(sems["tT_lo"], b + 1)
                    free_small(step)
                    product(small_of(step)[:, 0:384], turned["tT"][b % 2], cut(att[3], QKVC, QKVC + 384),
                            token_row(3, QKVC, QKVC + 384)).then_inc(sems["self_qkv"], 1)
                elif what == "self_out":
                    _, l, b = step
                    pe.wait_ge(sems["vT_lo"], b + 1)
                    free_small(step)
                    product(small_of(step)[:, 0:128], turned["vT"][b % 2], cut(att[3], SOC, SOC + 128),
                            token_row(3, SOC, SOC + 128)).then_inc(sems["self_out"], 1)
                elif what == "logits":
                    _, l, b = step
                    pe.wait_ge(sems["fT_lo"], B * l + b + 1)
                    free_small(step)
                    product(small_of(step)[:, 0:8], cut(ffn_in, S * b, S * b + S), cut(att[l], RC, RC + 8),
                            token_row(l, RC, RC + 8)).then_inc(sems["logits"], 1)
                elif what == "shareT":
                    k = ordinal[step]
                    pe.wait_ge(sems["share_parts"], k + 1)
                    free_small(step)
                    pe.matmul(small_of(step)[:, 0:128], share_parts.rearrange("p b r -> p (b r)"), ident_r,
                              start=True, stop=True).then_inc(sems["shareT"], 1)
                elif what == "weigh":
                    _, kind, e, n = step
                    pe.wait_ge(sems["share_rows"], ordinal[("shareT", kind)] + 1)
                    free_small(step)
                    pe.matmul(small_of(step), pick[:, e:e + 1].to_broadcast([128, 128]), share_rows[:, 512 * n:512 * n + 512],
                              start=True, stop=True).then_inc(sems["weigh"], 1)
                elif what == "merge":
                    _, kind, n = step
                    if kind == DENSE:
                        pe.wait_ge(sems["add_expert"], ordinal[("down", DENSE, 0, n)] + 1)
                    else:
                        pe.wait_ge(sems["summed"], sum_count(("add_expert", kind, EXPERTS - 1, n)))
                    free_small(step)
                    to = split3(small_of(step), 4)
                    for i in range(4):
                        a = 512 * n + 128 * i
                        last = pe.transpose(to[:, i, :], expert_sum[:, a:a + 128], ident)
                    last.then_inc(sems["merge"], 1)
                elif what == "up":
                    _, kind, e, n, c = step
                    k, j = ordinal[step], local_chunk(kind, e, n, c)
                    hi, lo = exp_w[EXPERT_LIST.index((kind, e)) % 2]
                    if n == 0 and c == 0:
                        item = ("expert", EXPERT_LIST.index((kind, e)))
                        pe.wait_ge(sems["weights_split"], split_count(item, up_parts(item) - 1))
                    if e == 0 and c == 0:
                        if kind == DENSE:
                            pe.wait_ge(sems["yT_lo"], 4 * n + 4)
                        else:
                            pe.wait_ge(sems["fT_lo"], B * kind + 4 * n + 4)
                    if j == 0:
                        if kind != 3:
                            l = 3 if kind == DENSE else kind
                            pe.wait_ge(sems["exp"], n_attn(l) + B * (1 if l == 3 else 2))
                    tokens = cut(ffn_in, 512 * n, 512 * n + 512)
                    width = 128 * CHUNKS[kind]
                    if GATED[kind]:
                        if j >= 2:
                            pe.wait_ge(sems["activated"], k - 1)
                        product(bank(2 * j % 4), cut((hi, lo), 128 * c, 128 * c + 128), tokens).then_inc(
                            sems["gate_up"], 1)
                        if j >= 2:
                            pe.wait_ge(sems["hidden"], k - 1)
                        product(bank((2 * j + 1) % 4), cut((hi, lo), width + 128 * c, width + 128 * c + 128),
                                tokens).then_inc(sems["plain_up"], 1)
                    else:
                        if j >= 4:
                            pe.wait_ge(sems["activated"], k - 3)
                        product(bank(j % 4), cut((hi, lo), 128 * c, 128 * c + 128), tokens).then_inc(
                            sems["gate_up"], 1)
                elif what in ("down", "down_part"):
                    kind, e, n = step[1:4]
                    c = step[4] if what == "down_part" else CHUNKS[kind] - 1
                    whole = ("down", kind, e, n)
                    y = ordinal[whole]
                    hi, lo = exp_w[EXPERT_LIST.index((kind, e)) % 2]
                    base = 128 * CHUNKS[kind] * (2 if GATED[kind] else 1)
                    pe.wait_ge(sems["hidden_lo"], chunk_ordinal(kind, e, n, c) + 1)
                    if n == 0 and c == 0:
                        pe.wait_ge(sems["weights_split"], split_count(("expert", EXPERT_LIST.index((kind, e)))))
                    if c == 0:
                        free_small(whole)
                    w = cut((hi, lo), base + 128 * c, base + 128 * c + 128)
                    h = cut((hid_hi[y % 2], hid_lo[y % 2]), 512 * c, 512 * c + 512)
                    last = product(small_of(whole), w, h, start=(c == 0), stop=(what == "down"))
                    if what == "down":
                        last.then_inc(sems["down"], 1)


def _stack_columns(w, d):
    j = 32 // d
    w = w.reshape(*w.shape[:-1], j, 4, d)
    w = np.moveaxis(w, -2, -3)
    out = np.zeros((*w.shape[:-1], 4, d), np.float32)
    out[..., 0:3, :] = w[..., None, :]
    return out.reshape(*w.shape[:-3], 512)


def _constants():
    const = np.zeros((128, CONST_COLS), np.float32)
    const[:, IDENT:IDENT + 128] = np.eye(128)
    r = np.arange(128)
    const[:, LAM + LAM_Q] = np.where((r // 8) % 4 == 2, -1.0, 0.0)
    const[:, LAM + LAM_K] = np.where((r // 8) % 4 == 1, -1.0, 0.0)
    const[:, LAM + LAM_Q3] = np.where((r // 16) % 4 == 2, -1.0, 0.0)
    const[:, LAM + LAM_K3] = np.where((r // 16) % 4 == 1, -1.0, 0.0)
    const[:, LAM + LAM_ROW] = np.where(r % 32 == 1, -1.0, 0.0)
    const[:, IOTA:IOTA + 8] = np.arange(8)
    const[:, PICK:PICK + 8] = r[:, None] % 8 == np.arange(8)
    const[:, TILE:TILE + 8] = r[:, None] // 16 == np.arange(8)
    q, k = r[:, None], r[None, :]
    const[:, MASKS:MASKS + 128] = np.where(k <= q, 0, MASKED)
    strict = k < q
    strict[0, 0] = True
    const[:, MASKS + 128:MASKS + 256] = np.where(strict, 0, MASKED)
    return const


def _down_rows(w):
    return w.reshape(-1, 128, 128).transpose(1, 0, 2).reshape(128, -1)


def kernel(**inputs):
    import concourse.bacc as _bacc
    from concourse.bass_utils import run_bass_kernel_spmd as _run

    g = {k: np.asarray(v) for k, v in inputs.items()}
    x = g["x"].transpose(1, 0, 2).reshape(128, B * D)
    ctx = g["ctx_1024"].transpose(2, 0, 1).reshape(128, B * S)
    mask = g["mask_Bx1xSxS2_ik1"][:, 0].transpose(1, 0, 2).reshape(128, B * S)

    def diagonal(w):
        out = np.zeros((128, 128), np.float32)
        for h in range(16):
            out[8 * h:8 * h + 8, 8 * h:8 * h + 8] = w.T
        return out

    def router(w):
        out = np.zeros((128, 8), np.float32)
        out[:, :w.shape[1]] = w
        return out

    wq3, wk3, wv3 = np.split(g["L3_xattn_in_proj_w"], 3, axis=0)
    bq3, bk3, bv3 = np.split(g["L3_xattn_in_proj_b"], 3)
    att_parts = [
        [(g["L0_xattn_w_q"]), (g["L0_xattn_w_k"]), g["L0_xattn_w_v"], g["L0_xattn_w_o"], router(g["L0_ffn_wr"].T)],
        [diagonal(g["L1_xattn_Wq"]), diagonal(g["L1_xattn_Wk"]), diagonal(g["L1_xattn_Wv"]), g["L1_xattn_Wo"].T,
         router(g["L1_ffn_Wr"])],
        [g["L2_xattn_Wq"].T, g["L2_xattn_Wk"].T, g["L2_xattn_Wv"].T, g["L2_xattn_Wo"].T, router(g["L2_ffn_gate_w"])],
        [wq3.T, wk3.T, wv3.T, g["L3_xattn_mha_out_w"].T, router(g["L3_ffn_router_w"].T), g["L3_xattn_qkv_w"].T,
         g["L3_xattn_sa_out_w"].T],
    ]
    arrays = {}
    for l, p in enumerate(att_parts):
        p = [_stack_columns(p[0], HEAD_DIM[l]), _stack_columns(p[1], HEAD_DIM[l]), *p[2:]]
        arrays[f"att{l}"] = np.ascontiguousarray(np.concatenate(p, axis=1))
    bias = np.zeros((128, BIAS_COLS), np.float32)
    for r in range(2):
        bias[r, QC:QC + 512] = _stack_columns(g["L0_xattn_b_q"], 8)
        bias[r, KC:KC + 512] = _stack_columns(g["L0_xattn_b_k"], 8)
        bias[r, VC:VC + 128] = g["L0_xattn_b_v"]
        bias[r, OC:OC + 128] = g["L0_xattn_b_o"]
        bias[r, RC:RC + 7] = g["L0_ffn_rb"]
        bias[r, RC + 7] = MASKED
        bias[32 + r, OC:OC + 128] = g["L1_xattn_bo"]
        bias[64 + r, VC:VC + 128] = g["L2_xattn_bv"]
        bias[64 + r, OC:OC + 128] = g["L2_xattn_bo"]
        bias[64 + r, RC:RC + 8] = g["L2_ffn_gate_b"]
        bias[96 + r, QC:QC + 512] = _stack_columns(bq3, 16)
        bias[96 + r, KC:KC + 512] = _stack_columns(bk3, 16)
        bias[96 + r, VC:VC + 128] = bv3
        bias[96 + r, OC:OC + 128] = g["L3_xattn_mha_out_b"]
        bias[96 + r, QKVC:QKVC + 384] = g["L3_xattn_qkv_b"]
        bias[96 + r, SOC:SOC + 128] = g["L3_xattn_sa_out_b"]
    for l, d in enumerate(HEAD_DIM):
        ones = bias[32 * l:32 * l + 2, KC:KC + 512].reshape(2, 4, 32 // d, 4, d)
        ones[..., 3, 0:2] = 1
    hidden_bias = np.concatenate([g["L2_ffn_b1"].reshape(32, 128).T, g["L3_xattn_lin1_b"].reshape(4, 128).T,
                                  g["L2_ffn_b2"].T, g["L3_xattn_lin2_b"][:, None]], axis=1)
    norm = np.stack([g[f"L3_xattn_ln{i}_{p}"] for i in (1, 2, 3) for p in "gb"])
    norm = np.broadcast_to(norm[None], (128, 6, 128)).reshape(128, 768)

    def swiglu(gate, up, down):
        out = np.zeros((128, 3, 384), np.float32)
        out[:, 0, :gate.shape[0]] = gate.T
        out[:, 1, :up.shape[0]] = up.T
        rows = np.zeros((384, 128), np.float32)
        rows[:down.shape[1]] = down.T
        out[:, 2] = _down_rows(rows)
        return out.reshape(128, 1152)

    e0 = [swiglu(g["L0_ffn_rg"][e], g["L0_ffn_ru"][e], g["L0_ffn_rd"][e]) for e in range(7)]
    e0.append(swiglu(g["L0_ffn_sg"], g["L0_ffn_su"], g["L0_ffn_sd"]))
    arrays["exp0"] = np.stack(e0)
    arrays["exp1"] = np.stack([np.concatenate([g["L1_ffn_Wg"][e], g["L1_ffn_Wu"][e], _down_rows(g["L1_ffn_Wd"][e])],
                                              axis=1) for e in range(8)])
    arrays["exp2"] = np.stack([np.concatenate([g["L2_ffn_w1"][e], _down_rows(g["L2_ffn_w2"][e])], axis=1)
                               for e in range(8)])
    arrays["expdense"] = np.concatenate([g["L3_xattn_lin1_w"].T, _down_rows(g["L3_xattn_lin2_w"].T)], axis=1)[None]
    arrays["exp3"] = np.stack([np.concatenate([g["L3_ffn_w1"][e], _down_rows(g["L3_ffn_w2"][e])], axis=1)
                               for e in range(8)])
    const = _constants()
    arrays.update(x_in=x, ctx_in=ctx, mask_in=mask, bias_in=bias, hidden_bias_in=hidden_bias, norm_in=norm,
                  const_in=const)

    nc = _bacc.Bacc("TRN2", target_bir_lowering=False, num_devices=1)
    arrays = {k: np.ascontiguousarray(v) for k, v in arrays.items()}
    dram = {k: nc.dram_tensor(k, v.shape, mybir.dt.from_np(v.dtype), kind="ExternalInput").ap()
            for k, v in arrays.items()}
    out = nc.dram_tensor("x_out", (128, B * D), F32, kind="ExternalOutput").ap()
    fused_layers(nc, dram["x_in"], dram["ctx_in"], dram["mask_in"], [dram[f"att{l}"] for l in range(LAYERS)],
                 {k: dram[f"exp{k}"] for k in (0, 1, 2, DENSE, 3)}, dram["bias_in"], dram["hidden_bias_in"],
                 dram["norm_in"], dram["const_in"], out)
    r = _run(nc, [arrays], core_ids=[0])
    return np.ascontiguousarray(r.results[0]["x_out"].reshape(128, B, D).transpose(1, 0, 2))
```

```python
import concourse.bass as bass
from concourse import mybir
from contextlib import ExitStack
import numpy as np

F32 = mybir.dt.float32
F32R = mybir.dt.float32r
BF16 = mybir.dt.bfloat16
I32 = mybir.dt.int32
U32 = mybir.dt.uint32
ALU = mybir.AluOpType
ACT = mybir.ActivationFunctionType
AX = mybir.AxisListType

B, S, D = 8, 128, 128
LAYERS = 4
HEAD_DIM = [8, 8, 8, 16]
SCORE_SCALE = [1.0, 128.0 ** -0.5, 8.0 ** -0.5, 16.0 ** -0.5]
SELF_SCALE = 128.0 ** 0.5
MOE_SCALE = [1.0, 12.0 ** -0.5, 1.0, 1.0]
TOP_K = [2, 2, 1, 2]
EXPERTS = 8
DENSE = "dense"
CHUNKS = {0: 3, 1: 4, 2: 4, DENSE: 4, 3: 2}
GATED = {0: True, 1: True, 2: False, DENSE: False, 3: False}
FUNCTION = {0: ACT.Silu, 1: ACT.Silu, 2: ACT.Gelu, DENSE: ACT.Relu, 3: ACT.Gelu}
N_EXPERTS = {0: 8, 1: 8, 2: 8, DENSE: 1, 3: 8}
MASKED = -1e30
FILL = -1e20
EPS = 1e-5
ARENA_BYTES = 58368

QC, KC, VC, OC, RC = 0, 512, 1024, 1152, 1280
QKVC, SOC = 1288, 1672
ATT_COLS = [1288, 1288, 1288, 1800]
BIAS_COLS = 1800
RAW_COLS = 1800
WEIGHT_PARTS = 4
IDENT, MASKS, LAM, IOTA, PICK, TILE, CONST_COLS = 0, 128, 384, 389, 397, 405, 413
LAM_Q, LAM_K, LAM_Q3, LAM_K3, LAM_ROW = range(5)


def expert_cols(kind):
    return CHUNKS[kind] * 128 * (3 if GATED[kind] else 2)


def up_parts(item):
    return 3 if item[0] == "expert" and GATED[EXPERT_LIST[item[1]][0]] else 2


EXPERT_LIST = [(kind, e) for kind in (0, 1, 2, DENSE, 3) for e in range(N_EXPERTS[kind])]


def build_schedule():
    PERIOD = {0: 12, 1: 6.16, 2: 12, 3: 6.74}
    enter_0 = [(-34, "pre_stats"), (-32.5, "pre_norm"), (-29.26, "xT"), (-28.4, "xT_split")]
    heads_0 = [(-15.5, "key_block"), (-10, "scores0"), (-9.96, "max0"), (-9.99, "scores1"), (-7.8, "max1"),
             (-6.69, "max_split"), (-4.12, "maxT"), (-4, "max_merge"), (-3.2, "max_merge_rest"),
             (3.1, "expscores0"), (4, "exp0"), (4.2, "expscores1"), (5, "exp1"), (6.35, "value"), (6.8, "value_copy"), (11.9, "mix"), (14.17, "mix_copy"),
             (16.5, "mixT"), (16.7, "mix_norm")]
    enter = [(-34, "pre_stats"), (-32.5, "pre_norm"), (-29.26, "xT"), (-28.4, "xT_split")]
    heads = [(-15.5, "key_block"), (-10, "scores0"), (-9.96, "max0"), (-9.99, "scores1"), (-7.8, "max1"),
             (-6.69, "max_split"), (-4.6, "maxT"), (-4, "max_merge"), (-3.2, "max_merge_rest"),
             (3.1, "expscores0"), (4, "exp0"), (4.2, "expscores1"), (5, "exp1"), (6.35, "value"), (6.8, "value_copy"), (11.9, "mix"), (14.17, "mix_copy"),
             (16.5, "mixT"), (16.7, "mix_norm")]
    leave = [(20.6, "oT"), (21.6, "oT_split"), (23.72, "out"), (24.4, "residual")]
    last = [(24.68, "post_stats"), (26.18, "post_norm"), (29.75, "fT"), (28.61, "fT_split"), (31, "logits")]
    inner = [(-55.31, "pre_stats"), (-53.5, "pre_norm"), (-51.89, "tT"), (-51, "tT_split"),
             (-49, "self_qkv"), (-48.5, "self_copy"), (-47.8, "self_dot"), (-46.5, "self_exp"),
             (-45, "self_value"), (-43, "vT"), (-42, "vT_split"), (-40, "self_out"),
             (-41.1, "self_residual"), (-38.5, "mid_stats"), (-36, "mid_norm"), (-29.4, "xT"), (-28.4, "xT_split")]
    heads_3 = [(-15.5, "key_block"), (-10.09, "scores0"), (-9, "max0"), (-5.79, "max_split"),
               (-4.6, "maxT"), (-4, "max_merge"), (-3.2, "max_merge_rest"), (3.1, "expscores0"), (4, "exp0"),
               (6.4, "value"), (5.14, "value_copy"), (14.93, "mix"), (15.04, "mix_copy"), (16.5, "mixT"),
               (17, "mix_norm")]
    leave_3 = [(20.6, "oT"), (21.53, "oT_split"), (23.6, "out"), (24.4, "residual"),
               (25, "cross_stats"), (26.6, "cross_norm"), (28.6, "yT"), (28.4, "yT_split")]
    tables = {0: enter_0 + heads_0 + [(14.93, "shuffle_store")],
              1: enter + heads + leave + last,
              2: enter + heads + leave + last,
              3: inner + heads_3 + leave_3}
    at, items = [], []

    def add(time, *step):
        at.append((time, step))

    def weights(time, item, spread=0.0, down_time=None):
        items.append(item)
        up = up_parts(item)
        for part in range(WEIGHT_PARTS):
            at_part = time if down_time is None or part < up else down_time
            add(at_part + part * (spread + 1e-4), "weights", len(items) - 1, part)

    def attention(l, keys, half_ready, all_ready, start, load=()):
        unit = PERIOD[l] / 10
        before = start - 1.5
        if l == 3:
            startup = {kind: 0.5 * (t - inner[0][0]) for t, kind in inner}
            start = max(start, half_ready + startup["xT_split"] + 5.5)
        else:
            startup = {"pre_stats": 0, "pre_norm": 1.3, "xT": 2.2, "xT_split": 2.8}
        zero = start + 10 * unit
        for b in range(B):
            for t, kind in tables[l]:
                at_end = 10 * (B - 1) + 5
                t += 10 * b
                if b == B - 1 and t > at_end + 5:
                    t -= 5
                time = zero + unit * (min(t, at_end) + 0.6 * max(t - at_end, 0))
                ready = half_ready if b < B // 2 else all_ready
                if kind in startup:
                    time = max(time, ready + 0.1 + startup[kind] + (3.27 if l == 3 else 0.7) * (b % 4))
                if kind == "key_block" and b == 0:
                    time = start + -2.66
                add(time, kind, l, b)
        for pair in range(B // 2):
            for part in range(2):
                time = zero + unit * (20 * pair + -17.2 + 0.6 * part)
                time = max(time, start + -2.24 + 0.6 * part)
                add(time, "query", l, pair, part)
                add(time + 0.7, "query_split", l, pair, part)
        add(keys + 4.5, "clear_keys", l)
        add(before + -0.5, "clear_queries", l)
        for s in range(4):
            add(keys + 0.02 + 0.9 * s, "key", l, s, 0)
            add(keys + 0.02 + 0.9 * s + 0.85, "key_split", l, s, 0)
            second = zero + unit * (10 * s + -8) if l < 3 else before + 0.9 * s
            add(second, "key", l, s, 1)
            add(second + 1.2, "key_split", l, s, 1)
        for i, item in enumerate(load):
            weights(zero + 12.89 * i, item, 3)
        end = max(time for time, step in at if step[0] in ("logits", "fT_split", "yT_split", "shuffle_store"))
        scores_end = max(time for time, step in at if step[0] in ("expscores0", "expscores1"))
        return scores_end, end

    def leave_first(start):
        at_tile = [(0, "oT"), (1.41, "oT_split"), (3, "out"), (4, "residual"), (4.77, "post_stats"),
                   (6.5, "post_norm"), (8, "fT"), (9, "fT_split"), (11, "logits")]
        add(start, "shuffle_load", 0, 0)
        add(start + 0.1, "shuffle_load", 0, 1)
        for b in range(B):
            for t, kind in at_tile:
                add(start + 3 + 2 * b + t, kind, 0, b)
        return start + 3 + 2 * (B - 1) + 11

    def finish_tiles(start, n):
        for t, kind in [(0, "final_stats"), (0.37, "final_norm"), (5.5, "last_stats"), (8, "last_norm")]:
            add(start + t, kind, 3, n)
        table = [(8.72, "fT"), (9.3, "fT_split"), (10.9, "logits")]
        for i in range(4):
            for t, kind in table:
                add(start + t + 0.6 * i, kind, 3, 4 * n + i)
        return start + 12.9

    def feed_forward(kind, start, all_ready):
        units = [(e, n) for e in range(N_EXPERTS[kind]) for n in range(2)]
        if len(units) > 2:
            units[1], units[2] = units[2], units[1]
        up_time = 1.28 if GATED[kind] else 0.64
        before, t, merged = None, start, []

        def down(t, c, e, n):
            if c < CHUNKS[kind] - 1:
                add(t, "down_part", kind, e, n, c)
                return t + 0.64
            add(t, "down", kind, e, n)
            return t + 0.64

        def next_weights(t, e, n):
            x = EXPERT_LIST.index((kind, e)) + 2
            if n == 1 and x < len(EXPERT_LIST) and EXPERT_LIST[x][0] in ((kind,) if kind == 2 else (kind, 3)):
                unit_time = (up_time + 0.64) * CHUNKS[kind]
                weights(t + 0.01, ("expert", x), down_time=t + unit_time + 0.26)

        def finish(t, e, n):
            if kind != DENSE:
                add(t, "weigh", kind, e, n)
            add(t + 0.02, "add_expert", kind, e, n)
            if e == N_EXPERTS[kind] - 1:
                merge = t + (3.8 if kind != DENSE else 0.03)
                add(merge, "merge", kind, n)
                merged.append(merge + 0.02)
                if kind == 3:
                    add(merge + 0.01, "store", n)
            return t + (0.25 if kind != DENSE else 0)

        for i, (e, n) in enumerate(units):
            if i == (2 if kind != DENSE else 1):
                t = max(t, all_ready + 0.1)
                if kind != DENSE:
                    add(t, "route", kind)
            for c in range(CHUNKS[kind]):
                add(t, "up", kind, e, n, c)
                t += up_time
                if before is not None:
                    add(t + (-0.01 if GATED[kind] else -0.7), "hidden_split", kind, *before)
                before = (e, n, c)
                if c == (0 if i > 3 else CHUNKS[kind] - 1) and i >= 3:
                    t = finish(t, *units[i - 2])
                if i == 2 and c == 1:
                    add(t - 0.005, "shareT", kind)
                if (i, c) == ((2, 3) if CHUNKS[kind] > 3 else (3, 0)):
                    t = finish(t, *units[0])
                if i:
                    t = down(t, c, *units[i - 1])
            next_weights(t, e, n)
        add(t + 0.01, "hidden_split", kind, *before)
        keys = t = finish(t + 0.02, *units[-2])
        t += 4 if kind != DENSE else 0.2
        for c in range(CHUNKS[kind]):
            t = down(t, c, *units[-1])
        t = finish(t + 1.11, *units[-1])
        return keys, merged[0], t, merged[-1]

    weights(-100, ("attention", 0))
    add(40, "masks")
    _, end = attention(0, -10, -60, -60, 0, [("attention", 1), ("expert", 0), ("expert", 1)])
    end_first = leave_first(end + 0.1)
    keys, half, done, merged = feed_forward(0, end + 18.5, end_first)
    for l in (1, 2, 3):
        kind = DENSE if l == 3 else l
        first = EXPERT_LIST.index((kind, 0))
        loads = [("expert", first), ("expert", first + 1)]
        if l < 3:
            loads.insert(0, ("attention", l + 1))
        scores_end, end = attention(l, keys, half, merged, done + {1: 2.39, 2: 2.39, 3: 2.39}[l], loads)
        keys, half, done, merged = feed_forward(kind, scores_end + {1: 1, 2: 1, 3: 1}[l], end)
    middle = finish_tiles(half + 0.1, 0)
    end = finish_tiles(half + 5.2, 1)
    feed_forward(3, middle + 0.55, end)
    return [step for _, step in sorted(at, key=lambda s: s[0])], items


def fused_layers(nc, x_in, ctx_in, mask_in, att_w, expert_w, bias_in, hidden_bias_in, norm_in,
                 const_in, x_out):
    steps, items = build_schedule()
    ordinal, per_kind = {}, {}
    for step in steps:
        ordinal[step] = per_kind.get(step[0], 0)
        per_kind[step[0]] = ordinal[step] + 1

    TRANSPOSES = ("xT", "fT", "oT", "tT", "vT", "yT")
    SMALL = TRANSPOSES + ("query", "key", "value", "logits", "maxT", "mix", "mixT", "out", "self_qkv", "self_out",
                          "shareT", "weigh", "merge", "down")
    UNITS = ("scores0", "scores1", "expscores0", "expscores1")
    units = [s for s in steps if s[0] in UNITS]
    unit_at = {s: i for i, s in enumerate(units)}
    small_bank, small_before, held, turn, feeding = {}, {}, {}, [0, 0, 0], False
    rounded_turn, rounded_before = {}, {}
    for s in steps:
        feeding = s[0] == "up" or (feeding and not (s[0] == "add_expert" and s[2:] == (N_EXPERTS[s[1]] - 1, 1)))
        if s[0] in ("query", "key"):
            i = len(rounded_turn)
            rounded_turn[s] = i % 2
            rounded_before[s] = list(rounded_turn)[i - 2] if i >= 2 else None
        if s[0] in ("down", "down_part"):
            s = ("down", *s[1:4])
        if s[0] not in SMALL or s in small_bank:
            continue
        if s[0] == "down":
            bank_number = 2 + turn[0] % 2
            turn[0] += 1
        elif feeding:
            bank_number = turn[1] % 2
            turn[1] += 1
        else:
            bank_number = turn[2] % 4
            turn[2] += 1
        small_bank[s], small_before[s] = bank_number, held.get(bank_number)
        held[bank_number] = s
    READ = {"query": "query_split", "key": "key_split", "value": "value_copy", "maxT": "max_merge_rest",
            "mix": "mix_copy", "mixT": "mix_norm", "out": "residual", "self_qkv": "self_copy", "self_out": "self_residual",
            "logits": "logits_copy", "shareT": "share_rows", "weigh": "weigh_copy", "merge": "merged",
            "down": "add_expert", **{t: f"{t}_lo" for t in TRANSPOSES},
            "scores0": "max", "scores1": "max", "expscores0": "exp", "expscores1": "exp"}

    def read_count(step):
        kind = step[0]
        if kind in ("scores0", "scores1", "expscores0", "expscores1"):
            same = [u for u in units if u[0][:-1] == kind[:-1]]
            return same.index(step) + 1
        return ordinal[step] + 1

    dscratch = nc.dram_tensor("head_major_scratch", (16, B, S, 8), F32, kind="Internal").ap()

    with ExitStack() as stack:
        def sb(name, shape, dtype):
            return stack.enter_context(nc.sbuf_tensor(name, [shape[0], int(np.prod(shape[1:]))], dtype))[:, :]

        arena = {}

        def shared(name, shape, dtype, phase):
            at = arena.setdefault(phase, arena["base"])
            arena[phase] = at + 4 * shape[1]
            assert arena[phase] <= arena["base"] + ARENA_BYTES
            return nc.alloc_sbuf_tensor_at(name, shape, dtype, offset=at)[:, :]

        def split3(ap, a):
            return ap.rearrange("p (a c) -> p a c", a=a)

        sems = {}
        SEMAPHORES = (
            ["loads_x", "loads_ctx", "loads_const", "loads_mask", "loads_bias", "raw0", "raw1", "shuffled0",
             "shuffled1", "unshuffled0", "unshuffled1", "stored", "dve_own", "pool_own", "constants", "const_rows",
             "masks", "context_hi", "context_lo", "weights_split", "variance", "rstd", "pre_norm",
             "mid_norm", "cross_norm", "mid_plain", "cross_plain", "topped", "post_norm", "self_value", "self_copy", "self_dot", "self_exp",
             "self_residual", "query", "query_round", "query_split", "key", "key_round", "key_split",
             "value", "value_copy", "scores", "max", "max_split", "maxT", "max_merge", "max_merge_rest", "share_parts", "shareT",
             "share_rows", "weigh", "weigh_copy", "merge", "merged", "summed", "expscores",
             "key_block", "key_block_rest", "clear_keys", "clear_queries", "exp", "mix", "mix_copy", "mixT", "mix_norm", "out", "residual", "self_qkv", "self_out", "logits", "logits_copy",
             "route_diff", "route_exp", "gate_up", "plain_up", "activated", "hidden", "hidden_hi", "hidden_lo", "down",
             "add_expert", "final_sum"]
            + [f"{t}_{p}" for t in TRANSPOSES for p in ("ps", "hi", "lo")])
        for name in SEMAPHORES:
            sems[name] = stack.enter_context(nc.semaphore(name))

        arena["base"] = (nc.sbuf_base + 31) // 32 * 32
        sb("arena", [128, ARENA_BYTES // 4 + 8], F32)
        x = split3(sb("x", [128, B * D], F32), B)
        ctx = sb("ctx_hi", [128, B * S], F32R), sb("ctx_lo", [128, B * S], F32R)
        att_ring = [(sb(f"att_hi{i}", [128, ATT_COLS[2 + i]], F32R), sb(f"att_lo{i}", [128, ATT_COLS[2 + i]], F32R))
                    for i in range(2)]
        att = [att_ring[l % 2] for l in range(LAYERS)]
        bias = sb("bias_rows", [128, BIAS_COLS], F32R)
        raw = [sb(f"raw{i}", [128, RAW_COLS], F32) for i in range(2)]
        exp_w = [(sb(f"expert_hi{i}", [128, 1536], F32R), sb(f"expert_lo{i}", [128, 1536], F32R))
                 for i in range(2)]
        const = sb("const", [128, CONST_COLS], F32)
        const16 = sb("const16", [128, 384], BF16)
        ident_r = sb("ident_r", [128, 128], F32R)
        pick = sb("pick", [128, 8], F32R)
        ones = sb("ones", [128, 256], F32R)
        minus_half = sb("minus_half", [128, 4], F32)
        hidden_bias = sb("hidden_bias", [128, 36 + 9], F32)
        out_bias = hidden_bias[:, 36:45]
        norms = split3(sb("norms", [128, 6 * D], F32), 6)
        mask1_at = (nc.sbuf_base + 31) // 32 * 32
        mask1 = split3(sb("mask1", [128, B * S], BF16), B)
        stats = [split3(sb(f"stats{i}", [128, 24], F32), 4) for i in range(4)]
        moments = [split3(sb(f"moments{i}", [128, 8], F32), 4) for i in range(4)]
        var_eps = [sb(f"var_eps{i}", [128, 4], F32) for i in range(4)]
        rstd = [sb(f"rstd{i}", [128, 4], F32) for i in range(4)]
        norm_x = [sb(f"norm_x{i}", [128, D], F32) for i in range(2)]
        norm_f = [sb(f"norm_f{i}", [128, D], F32) for i in range(4)]
        turned = {t: [(sb(f"{t}_hi{i}", [128, 128], F32R), sb(f"{t}_lo{i}", [128, 128], F32R))
                      for i in range(2)] for t in ("oT", "tT", "vT")}
        turned["xT"] = [(sb(f"xT_hi{i}", [128, 256], F32R), sb(f"xT_lo{i}", [128, 256], F32R)) for i in range(2)]
        ffn_in = sb("ffn_in_hi", [128, B * S], F32R), sb("ffn_in_lo", [128, B * S], F32R)
        key_stack = split3(shared("key_stack", [128, 4 * B * S], F32R, "attention"), 4)
        key_blocks = shared("key_blocks", [128, 2048], F32R, "attention")
        query_blocks = shared("query_blocks", [128, 2048], F32R, "attention")
        query_stack = [split3(shared(f"query_stack{i}", [128, 1024], F32R, "attention"), 4) for i in range(2)]
        rounded = [sb(f"rounded{i}", [128, 512], F32R) for i in range(2)]
        values = [sb(f"values{i}", [128, 16 * 32], F32) for i in range(2)]
        values3 = [nc.alloc_sbuf_tensor_at(f"values_wide{i}", [128, 8 * 32], F32, offset=mask1_at + 1024 * i)[:, :]
                   for i in range(2)]
        mix_rows = sb("mix_rows", [128, 512], F32)
        neg_max = [sb(f"neg_max{i}", [128, 16], F32) for i in range(2)]
        max_parts = [sb(f"max_parts{i}", [128, 512], F32R) for i in range(2)]
        recip = [sb(f"recip{i}", [128, 16], F32) for i in range(2)]
        mixed = [sb(f"mixed{i}", [128, D], F32) for i in range(2)]
        hid_hi, hid_lo = [[], []]
        hid_hi.append(shared("hidden_hi0", [128, 2048], F32R, "ffn"))
        hid_lo.append(shared("hidden_lo0", [128, 2048], F32R, "ffn"))
        hid = [shared(f"hidden{i}", [128, 512], F32, "ffn") for i in range(3)]
        gate = [shared(f"gate{i}", [128, 512], F32, "ffn") for i in range(3)]
        hid_hi.append(shared("hidden_hi1", [128, 2048], F32R, "ffn"))
        hid_lo.append(shared("hidden_lo1", [128, 2048], F32R, "ffn"))
        probs = [shared(f"probs{i}", [128, 2048], F32, "attention") for i in range(2)]
        weight = [shared(f"weight{i}", [128, 512], F32, "ffn") for i in range(2)]
        weighed = [shared(f"weighed{i}", [128, 512], F32, "ffn") for i in range(2)]
        share_rows = shared("share_rows_x", [128, B * 128], F32R, "ffn")
        expert_sum = sb("expert_sum", [128, B * 128], F32)
        tgt = split3(sb("tgt", [128, B * D], F32), B)
        x1 = split3(sb("x1", [128, B * D], F32), B)
        mask_raw = x1.rearrange("p b d -> p (b d)").bitcast(I32)
        unshuffled = tgt
        x2 = tgt
        mid_sum = [sb(f"mid_sum{i}", [128, D], F32) for i in range(2)]
        cross_sum = [sb(f"cross_sum{i}", [128, D], F32) for i in range(2)]
        final_sum = x1
        self_qkv = [sb(f"self_qkv_x{i}", [128, 384], F32) for i in range(2)]
        self_prod = sb("self_prod", [128, D], F32)
        self_s = [sb(f"self_s{i}", [128, 8], F32) for i in range(2)]
        self_v = [sb(f"self_v{i}", [128, D], F32) for i in range(2)]
        logits = split3(sb("logits_x", [128, B * EXPERTS], F32), B)
        top = split3(sb("top", [128, B * 8], F32), B)
        top_at = split3(sb("top_at", [128, B * 8], U32), B)
        top_atf = split3(sb("top_atf", [128, B * 8], F32), B)
        route_diff = split3(sb("route_diff_x", [128, B * 8], F32), B)
        route_exp = split3(sb("route_exp_x", [128, B * 8], F32), B)
        route_sum = sb("route_sum", [128, B], F32)
        route_r = sb("route_r", [128, B], F32)
        hot = sb("hot", [128, B * 16], F32).rearrange("p (b i r) -> p b i r", b=B, i=2)
        share = split3(sb("share", [128, B * 8], F32), B)
        share_parts = split3(sb("share_parts_x", [128, B * 16], F32R), B)

        ident = const[:, IDENT:IDENT + 128]
        ident16 = const16[:, 0:128]
        mask0, mask2 = const16[:, 128:256], const16[:, 256:384]
        iota = const[:, IOTA:IOTA + 8]

        def lam(i):
            return const[:, LAM + i:LAM + i + 1]

        psum = [stack.enter_context(nc.psum_tensor(f"pair{i}", [128, 1024], F32))[:, :] for i in range(2)]
        small = [stack.enter_context(nc.psum_tensor(f"small{i}", [128, 512], F32))[:, :] for i in range(4)]

        def small_of(step):
            return small[small_bank[step]]

        def unit_of(step):
            return psum[unit_at[step] % 2]

        def bank(i):
            return psum[i // 2][:, 512 * (i % 2):512 * (i % 2) + 512]

        def queries(l, b):
            return query_stack[(l * (B // 2) + b // 2) % 2][:, :, S * (b % 2):S * (b % 2) + S]

        def blocks(buffer, l):
            heads = 4 if l < 3 else 2
            return buffer[:, 0:512 * heads].rearrange("p (s j q) -> p s j q", s=4, j=heads)

        def rows(l, j):
            size = 32 if l < 3 else 64
            return slice(size * j, size * j + size)

        def first_heads(l):
            return (0, 1) if l < 3 else (0,)

        def other_heads(l):
            return (2, 3) if l < 3 else (1,)

        def attn_ordinal(l, b):
            return l * B + b

        def par(l, b):
            return (l * B + b) % 2

        summed = [s for s in steps if s[0] == "add_expert" and s[1] != DENSE and s[2] > 0]

        def sum_count(step):
            return summed.index(step) + 1

        weighs = [s for s in steps if s[0] == "weigh"]

        def n_attn(l):
            return sum(B * (1 if m == 3 else 2) for m in range(l))

        def source(t, l, b):
            k = ordinal[(t, l, b)]
            if t == "xT":
                if l < 3:
                    return norm_x[k % 2], "pre_norm", ordinal[("pre_norm", l, b)] + 1
                return x1[:, b, :], "mid_norm", b + 1
            if t == "tT":
                return tgt[:, b, :], "pre_norm", ordinal[("pre_norm", l, b)] + 1
            if t == "vT":
                return self_v[b % 2], "self_value", b + 1
            if t == "oT":
                if l == 0:
                    return unshuffled[:, b, :], f"unshuffled{b // 4}", 16
                return mixed[par(l, b)], "mix_norm", ordinal[("mix_norm", l, b)] + 1
            if t == "yT":
                return x2[:, b, :], "cross_norm", b + 1
            return norm_f[k % 4], "post_norm", k + 1

        def target(t, l, b):
            if t in ("fT", "yT"):
                return tuple(a[:, S * b:S * b + S] for a in ffn_in)
            if t == "xT":
                return tuple(a[:, S * (b % 2):S * (b % 2) + S] for a in turned["xT"][b // 2 % 2])
            return turned[t][ordinal[(t, l, b)] % 2]

        def chunk_ordinal(kind, e, n, c):
            return ordinal[("up", kind, e, n, c)]

        def plain_before(kind):
            order = (0, 1, 2, DENSE, 3)
            return sum(CHUNKS[m] * N_EXPERTS[m] * 2 for m in order[:order.index(kind)])

        def local_chunk(kind, e, n, c):
            return chunk_ordinal(kind, e, n, c) - plain_before(kind)

        def columns(item):
            return ATT_COLS[item[1]] if item[0] == "attention" else expert_cols(EXPERT_LIST[item[1]][0])

        def part_of(item, part):
            cols = columns(item)
            if item[0] == "attention":
                edge = [(cols * i // WEIGHT_PARTS + 7) // 8 * 8 for i in range(WEIGHT_PARTS)] + [cols]
            else:
                n, width = up_parts(item), 128 * CHUNKS[EXPERT_LIST[item[1]][0]]
                up, down = cols - width, WEIGHT_PARTS - n
                edge = [up * i // n for i in range(n)] + [up + width * i // down for i in range(down)] + [cols]
            return edge[part], edge[part + 1]

        def parts(item):
            return att[item[1]] if item[0] == "attention" else exp_w[item[1] % 2]

        def first_down(x):
            kind = EXPERT_LIST[x][0]
            return expert_cols(kind) - 128 * CHUNKS[kind]

        weight_steps = [s for s in steps if s[0] == "weights"]

        def split_count(item, part=WEIGHT_PARTS - 1):
            return max(weight_steps.index(("weights", items.index(item), p)) for p in range(part + 1)) + 1

        def last_mix(kind, e, n):
            y, l = ordinal[("down", kind, e, n)], 3 if kind == DENSE else kind
            first = [ordinal[s] for s in steps if s[0] == "down" and s[1] == kind][1]
            return B * (l + 1) if y == first and kind != 3 else None

        def on_act(step):
            return GATED[step[1]] or step[4] % 2 == 1

        act_highs = [s for s in steps if s[0] == "hidden_split" and on_act(s)]

        block = stack.enter_context(nc.Block())

        @block.sync
        def _(sp):
            def load_item(i):
                kind, which = items[i]
                cols = columns(items[i])
                if i >= 2:
                    sp.wait_ge(sems["weights_split"], split_count(items[i - 2]))
                if kind == "attention":
                    src = att_w[which]
                else:
                    k, e = EXPERT_LIST[which]
                    src = expert_w[k][e]
                sp.dma_start(raw[i % 2][:, 0:cols], src).then_inc(sems[f"raw{i % 2}"], 16)

            sp.dma_start(const, const_in).then_inc(sems["loads_const"], 16)
            sp.dma_start(x.rearrange("p b d -> p (b d)"), x_in).then_inc(sems["loads_x"], 16)
            load_item(0)
            sp.dma_start(probs[1][:, 0:B * S], ctx_in).then_inc(sems["loads_ctx"], 16)
            sp.wait_ge(sems["loads_ctx"], 16)
            load_item(1)
            sp.dma_start(mask_raw, mask_in).then_inc(sems["loads_mask"], 16)
            sp.dma_start(hidden_bias, hidden_bias_in).then_inc(sems["loads_mask"], 16)
            sp.dma_start(norms.rearrange("p a c -> p (a c)"), norm_in).then_inc(sems["loads_mask"], 16)
            for step in steps:
                what = step[0]
                if what == "weights" and step[2] == WEIGHT_PARTS - 1 and step[1] + 2 < len(items):
                    load_item(step[1] + 2)
                if what == "shuffle_store":
                    _, l, b = step
                    sp.wait_ge(sems["mix_norm"], b + 1)
                    sp.dma_start(dscratch[:, b, :, :].rearrange("h q d -> q h d"),
                                 split3(mixed[b % 2], 16)).then_inc(sems[f"shuffled{b % 2}"], 16)
                if what == "shuffle_load":
                    n = step[2]
                    if n == 0:
                        sp.wait_ge(sems["shuffled0"], 16 * (B // 2))
                        sp.wait_ge(sems["shuffled1"], 16 * (B // 2))
                    flat = dscratch.rearrange("h b q d -> (h b q d)").rearrange("(t s c) -> s t c", s=S, c=D)
                    sp.dma_start(unshuffled[:, 4 * n:4 * n + 4, :], flat[:, 4 * n:4 * n + 4, :]).then_inc(
                        sems[f"unshuffled{n}"], 16)
                if what == "store":
                    n = step[1]
                    sp.wait_ge(sems["merged"], ordinal[("merge", 3, n)] + 1)
                    sp.dma_start(x_out[:, 512 * n:512 * n + 512],
                                 x[:, 4 * n:4 * n + 4, :].rearrange("p b d -> p (b d)")).then_inc(sems["stored"], 16)
            sp.wait_ge(sems["stored"], 32)

        @block.gpsimd
        def _(pool):
            own = [0]

            def chain(instruction):
                own[0] += 1
                instruction.then_inc(sems["pool_own"], 1)
                pool.wait_ge(sems["pool_own"], own[0])

            pool.dma_start(probs[0][:, 0:BIAS_COLS], bias_in).then_inc(sems["loads_bias"], 16)
            pool.memset(minus_half, -0.5).then_inc(sems["pool_own"], 1)
            own[0] += 1
            count = 0
            for step in steps:
                what = step[0]
                if what == "weights":
                    _, i, part = step
                    item = items[i]
                    hi, lo = parts(item)
                    a, z = part_of(item, part)
                    if part == 0:
                        pool.wait_ge(sems[f"raw{i % 2}"], 16 * (i // 2 + 1))
                        if item[0] == "attention" and item[1] >= 2:
                            pool.wait_ge(sems["logits"], B * (item[1] - 1))
                        if item[0] == "expert" and item[1] >= 2:
                            kind, e = EXPERT_LIST[item[1] - 2]
                            last_up = ordinal[("up", kind, e, 1, CHUNKS[kind] - 1)] + 1
                            pool.wait_ge(sems["gate_up"], last_up)
                            if GATED[kind]:
                                pool.wait_ge(sems["plain_up"], last_up)
                    if item[0] == "expert" and item[1] >= 2 and z > first_down(item[1] - 2):
                        pool.wait_ge(sems["down"], ordinal[("down", *EXPERT_LIST[item[1] - 2], 1)] + 1)
                    w = raw[i % 2][:, a:z]
                    chain(pool.tensor_scalar(hi[:, a:z], w, 1.0, 1.0, ALU.mult, ALU.mult))
                    pool.tensor_tensor(lo[:, a:z], w, hi[:, a:z].bitcast(F32), ALU.subtract).then_inc(
                        sems["weights_split"], 1)
                if what == "masks":
                    pool.wait_ge(sems["loads_mask"], 48)
                    pool.tensor_scalar(mask1.rearrange("p b k -> p (b k)"), mask_raw, 0.0, FILL,
                                       ALU.is_equal, ALU.mult).then_inc(sems["masks"], 1)
                if what == "clear_keys":
                    l = step[1]
                    if l:
                        pool.wait_ge(sems["hidden_lo"], plain_before(l) if l < 3 else plain_before(DENSE))
                    pool.memset(key_blocks[:, 0:2048 if l < 3 else 1024].bitcast(F32), 0.0).then_inc(
                        sems["clear_keys"], 1)
                if what == "clear_queries":
                    l = step[1]
                    if l:
                        pool.wait_ge(sems["down"], ordinal[("down", l - 1, EXPERTS - 1, 1)] + 1)
                    pool.memset(query_blocks[:, 0:2048 if l < 3 else 1024].bitcast(F32), 0.0).then_inc(
                        sems["clear_queries"], 1)
                if what == "key_block":
                    _, l, b = step
                    pool.wait_ge(sems["key_split"], 8 * l + 4 * (b // 4) + 4)
                    if b == 0:
                        pool.wait_ge(sems["clear_keys"], l + 1)
                    else:
                        pool.wait_ge(sems["scores"], n_attn(l) + b * (1 if l == 3 else 2))
                    before = steps[:steps.index(step)]
                    for kind, signal in (("masks", "masks"), ("clear_keys", "clear_keys"),
                                         ("clear_queries", "clear_queries"), ("weights", "weights_split"), ("stats", "rstd"),
                                         ("mid_norm", "mid_norm"), ("cross_norm", "cross_norm"),
                                         ("summed", "summed")):
                        done = sum(s in summed if kind == "summed" else s[0].endswith(kind) for s in before)
                        if done:
                            pool.wait_ge(sems[signal], done)
                    for j in other_heads(l):
                        r = rows(l, j)
                        block = pool.tensor_scalar(blocks(key_blocks, l)[r, :, j, :],
                                                   key_stack[r, :, S * b:S * b + S].bitcast(F32), 1.0, 1.0,
                                                   ALU.mult, ALU.mult)
                        if j == other_heads(l)[-1]:
                            block.then_inc(sems["key_block_rest"], 1)
                            pool.wait_ge(sems["key_block_rest"], attn_ordinal(l, b) + 1)
                        else:
                            chain(block)
                if what in ("mid_norm", "cross_norm"):
                    b, name = step[2], what[:-5]
                    out = {"mid": x1[:, b, :], "cross": x2[:, b, :]}[name]
                    which = ("mid", "cross").index(name)
                    pool.wait_ge(sems[f"{name}_plain"], b + 1)
                    chain(pool.tensor_tensor(out, out, norms[:, 2 * which, :], ALU.mult))
                    pool.tensor_tensor(out, out, norms[:, 2 * which + 1, :], ALU.add).then_inc(sems[what], 1)
                if what == "add_expert" and step in summed:
                    _, kind, e, n = step
                    y = ordinal[step]
                    total = expert_sum[:, 512 * n:512 * n + 512]
                    pool.wait_ge(sems["add_expert"], y + 1)
                    if sum_count(step) > 2:
                        pool.wait_ge(sems["summed"], sum_count(step) - 2)
                    pool.tensor_tensor(total, total, weighed[sum_count(step) % 2], ALU.add).then_inc(sems["summed"], 1)
                if what.endswith("_stats"):
                    i = count % 4
                    count += 1
                    pool.wait_ge(sems["variance"], count)
                    if count == 1:
                        pool.wait_ge(sems["pool_own"], 1)
                    tiles = 4 if what in ("final_stats", "last_stats") else 1
                    pool.tensor_tensor(rstd[i][:, 0:tiles], var_eps[i][:, 0:tiles], minus_half[:, 0:tiles],
                                       ALU.pow).then_inc(sems["rstd"], 1)

        @block.scalar
        def _(act):
            act.wait_ge(sems["loads_ctx"], 16)
            act.activation(ctx[0], probs[1][:, 0:B * S], ACT.Copy).then_inc(sems["context_hi"], 1)
            act.wait_ge(sems["loads_bias"], 16)
            act.activation(bias, probs[0][:, 0:BIAS_COLS], ACT.Copy).then_inc(sems["const_rows"], 1)
            for step in steps:
                what = step[0]
                if what.endswith("_split") and what[:-6] in TRANSPOSES:
                    t, l, b = what[:-6], step[1], step[2]
                    k = ordinal[(t, l, b)]
                    hi, _ = target(t, l, b)
                    act.wait_ge(sems[f"{t}_ps"], k + 1)
                    if t == "xT" and (l, b) >= (0, 4):
                        act.wait_ge(sems["query"], 2 * (l * (B // 2) + b // 2 - 1))
                    if t in ("tT", "vT", "oT") and k >= 2:
                        user = {"tT": "self_qkv", "vT": "self_out", "oT": "out"}[t]
                        act.wait_ge(sems[user], k - 1)
                    act.activation(hi, small_of((t, l, b))[:, 0:128], ACT.Copy).then_inc(sems[f"{t}_hi"], 1)
                elif what in ("query_split", "key_split"):
                    w = what[:-6]
                    k = ordinal[(w, *step[1:])]
                    act.wait_ge(sems[w], k + 1)
                    before = rounded_before[(w, *step[1:])]
                    if before is not None:
                        act.wait_ge(sems[READ[before[0]]], read_count(before))
                    act.activation(rounded[rounded_turn[(w, *step[1:])]], small_of((w, *step[1:])), ACT.Copy).then_inc(
                        sems[f"{w}_round"], 1)
                elif what == "value_copy":
                    _, l, b = step
                    k = ordinal[step]
                    act.wait_ge(sems["value"], k + 1)
                    if b == 0:
                        act.wait_ge(sems["constants"], 3 if l == 3 else 1)
                    if k >= 2:
                        act.wait_ge(sems["mix"], k - 1)
                    d = HEAD_DIM[l]
                    to = split3((values3 if l == 3 else values)[par(l, b)], 128 // d)[:, :, 0:d]
                    act.activation(to, split3(small_of(("value", l, b))[:, 0:128], 128 // d),
                                   ACT.Copy).then_inc(sems["value_copy"], 1)
                elif what == "key_block":
                    _, l, b = step
                    act.wait_ge(sems["key_split"], 8 * l + 4 * (b // 4) + 4)
                    if b == 0:
                        act.wait_ge(sems["clear_keys"], l + 1)
                    else:
                        act.wait_ge(sems["scores"], n_attn(l) + b * (1 if l == 3 else 2))
                    for j in first_heads(l):
                        r = rows(l, j)
                        last = act.activation(blocks(key_blocks, l)[r, :, j, :], key_stack[r, :, S * b:S * b + S],
                                              ACT.Copy)
                    last.then_inc(sems["key_block"], 1)
                elif what == "max_merge_rest":
                    _, l, b = step
                    act.wait_ge(sems["max_merge"], attn_ordinal(l, b) + 1)
                    for j in other_heads(l):
                        r = rows(l, j)
                        last = act.activation(blocks(query_blocks, l)[r, :, j, :],
                                              split3(small_of(("maxT", l, b)), 4)[r, :, :], ACT.Copy)
                    last.then_inc(sems["max_merge_rest"], 1)
                elif what == "mix_copy":
                    _, l, b = step
                    k = attn_ordinal(l, b)
                    act.wait_ge(sems["mix"], k + 1)
                    if k:
                        act.wait_ge(sems["mixT"], k)
                    r = 128 if l < 3 else 64
                    act.activation(mix_rows[0:r, :], small_of(("mix", l, b))[0:r, :], ACT.Copy).then_inc(
                        sems["mix_copy"], 1)
                elif what in ("exp0", "exp1"):
                    _, l, b = step
                    half = int(what[-1])
                    unit = (f"expscores{half}", l, b)
                    act.wait_ge(sems["expscores"], read_count(unit))
                    k = attn_ordinal(l, b)
                    if k >= 2 and half == 0:
                        act.wait_ge(sems["mix"], k - 1)
                    act.activation(probs[k % 2][:, 1024 * half:1024 * half + 1024], unit_of(unit), ACT.Exp,
                                   scale=SCORE_SCALE[l]).then_inc(sems["exp"], 1)
                elif what == "self_copy":
                    _, l, b = step
                    act.wait_ge(sems["self_qkv"], b + 1)
                    if b >= 2:
                        act.wait_ge(sems["self_value"], b - 1)
                    act.activation(self_qkv[b % 2], small_of(("self_qkv", l, b))[:, 0:384], ACT.Copy).then_inc(
                        sems["self_copy"], 1)
                elif what == "self_exp":
                    _, l, b = step
                    act.wait_ge(sems["self_dot"], b + 1)
                    s = self_s[b % 2]
                    act.activation(s[:, 3:4], s[:, 1:2], ACT.Exp, bias=s[:, 2:3]).then_inc(sems["self_exp"], 1)
                elif what == "route":
                    k = ordinal[step]
                    act.wait_ge(sems["route_diff"], k + 1)
                    width = 8 if TOP_K[step[1]] == 1 else 2
                    act.activation(route_exp[:, :, 0:width], route_diff[:, :, 0:width], ACT.Exp).then_inc(
                        sems["route_exp"], 1)
                elif what == "weigh":
                    k = ordinal[step]
                    act.wait_ge(sems["weigh"], k + 1)
                    if k >= 2:
                        act.wait_ge(sems["add_expert"], ordinal[("down", *weighs[k - 2][1:])] + 1)
                    act.activation(weight[k % 2], small_of(step), ACT.Copy).then_inc(sems["weigh_copy"], 1)
                elif what == "up":
                    _, kind, e, n, c = step
                    k, j = ordinal[step], local_chunk(kind, e, n, c)
                    act.wait_ge(sems["gate_up"], k + 1)
                    if GATED[kind]:
                        if j >= 3:
                            act.wait_ge(sems["hidden"], k - 2)
                        act.activation(gate[j % 3], bank(2 * j % 4), FUNCTION[kind]).then_inc(sems["activated"], 1)
                    else:
                        if j >= 3:
                            act.wait_ge(sems["hidden_lo"], k - 2)
                        col = 4 * e + c if kind == 2 else 32 + c
                        extra = dict(bias=hidden_bias[:, col:col + 1]) if kind in (2, DENSE) else {}
                        act.activation(hid[j % 3], bank(j % 4), FUNCTION[kind], **extra).then_inc(
                            sems["activated"], 1)
                elif what == "hidden_split":
                    _, kind, e, n, c = step
                    k, j = chunk_ordinal(kind, e, n, c), local_chunk(kind, e, n, c)
                    if on_act(step):
                        y = ordinal[("down", kind, e, n)]
                        if GATED[kind]:
                            act.wait_ge(sems["hidden"], k + 1)
                        else:
                            act.wait_ge(sems["activated"], k + 1)
                        if y >= 2:
                            act.wait_ge(sems["down"], y - 1)
                        if last_mix(kind, e, n) is not None:
                            act.wait_ge(sems["mix"], last_mix(kind, e, n))
                        act.activation(hid_hi[y % 2][:, 512 * c:512 * c + 512], hid[j % 3], ACT.Copy).then_inc(
                            sems["hidden_hi"], 1)

        @block.vector
        def _(dve):
            own = [0]

            def chain(instruction):
                own[0] += 1
                instruction.then_inc(sems["dve_own"], 1)
                dve.wait_ge(sems["dve_own"], own[0])

            norm_count = [0]
            pending = {}

            def statistics(key, *tiles):
                i = norm_count[0] % 4
                norm_count[0] += 1
                pending[key] = i, norm_count[0]
                for j, tile in enumerate(tiles):
                    last = dve.bn_stats(stats[i][:, j, :], tile)
                chain(last)
                for j in range(len(tiles)):
                    last = dve.bn_aggr(moments[i][:, j, :], stats[i][:, j, :])
                chain(last)
                dve.tensor_scalar(var_eps[i][:, 0:len(tiles)].unsqueeze(2), moments[i][:, 0:len(tiles), 1:2], EPS,
                                  None, ALU.add).then_inc(sems["variance"], 1)

            def normalize(key, out, src, j=0):
                i, count = pending[key]
                if j == 0:
                    dve.wait_ge(sems["rstd"], count)
                return dve.tensor_scalar(out, src, moments[i][:, j, 0:1], rstd[i][:, j:j + 1], ALU.subtract,
                                         ALU.mult)

            def x_ready(l, b):
                if l == 0:
                    dve.wait_ge(sems["loads_x"], 16)
                else:
                    n = b // 4
                    dve.wait_ge(sems["merged"], ordinal[("merge", l - 1, n)] + 1)

            for i in range(2):
                dve.memset(max_parts[i].bitcast(F32), 0.0)
                chain(dve.memset(values[i], 0.0))
                last = dve.memset(split3(values[i], 16)[:, :, 8:9], 1.0)
            last.then_inc(sems["constants"], 1)
            dve.wait_ge(sems["loads_const"], 16)
            dve.tensor_copy(ident_r, ident)
            dve.tensor_copy(const16, const[:, IDENT:IDENT + 384])
            dve.tensor_copy(pick, const[:, PICK:PICK + 8])
            dve.memset(ones.bitcast(F32), 1.0).then_inc(sems["constants"], 1)
            dve.wait_ge(sems["context_hi"], 1)
            dve.tensor_tensor(ctx[1], probs[1][:, 0:B * S], ctx[0].bitcast(F32), ALU.subtract).then_inc(
                sems["context_lo"], 1)
            dve.wait_ge(sems["const_rows"], 1)
            dve.scalar_tensor_tensor(bias, bias.bitcast(F32), lam(LAM_ROW), probs[0][:, 0:BIAS_COLS],
                                     ALU.mult, ALU.add).then_inc(sems["const_rows"], 1)

            for step in steps:
                what = step[0]
                if what.endswith("_split") and what[:-6] in TRANSPOSES:
                    t, l, b = what[:-6], step[1], step[2]
                    k = ordinal[(t, l, b)]
                    hi, lo = target(t, l, b)
                    dve.wait_ge(sems[f"{t}_hi"], k + 1)
                    dve.tensor_tensor(lo, small_of((t, l, b))[:, 0:128], hi.bitcast(F32), ALU.subtract).then_inc(
                        sems[f"{t}_lo"], 1)
                elif what in ("query_split", "key_split"):
                    w, l, which, part = what[:-6], *step[1:]
                    k = ordinal[(w, *step[1:])]
                    dve.wait_ge(sems[f"{w}_round"], k + 1)
                    got, temp = small_of((w, *step[1:])), rounded[rounded_turn[(w, *step[1:])]]
                    column = lam((LAM_Q if w == "query" else LAM_K) + (2 if l == 3 else 0))
                    if w == "query":
                        pair = l * (B // 2) + which
                        if pair >= 2 and part == 0:
                            dve.wait_ge(sems["max_merge"], 2 * (pair - 1))
                            dve.wait_ge(sems["maxT"], 2 * (pair - 1))
                        to = query_stack[pair % 2][:, 2 * part:2 * part + 2, :]
                        got, temp = split3(got, 2), split3(temp, 2)
                    else:
                        to = key_stack[:, which, 512 * part:512 * part + 512]
                    dve.scalar_tensor_tensor(to, temp.bitcast(F32), column, got, ALU.mult, ALU.add).then_inc(
                        sems[what], 1)
                elif what == "pre_stats":
                    _, l, b = step
                    if l == 3 and b == 0:
                        for i in range(2):
                            chain(dve.memset(values3[i], 0.0))
                            last = dve.memset(split3(values3[i], 8)[:, :, 16:17], 1.0)
                        last.then_inc(sems["constants"], 1)
                    x_ready(l, b)
                    statistics(step[1:], x[:, b, :])
                elif what == "pre_norm":
                    _, l, b = step
                    k = ordinal[step]
                    if l == 3:
                        out = tgt[:, b, :]
                    else:
                        out = norm_x[k % 2]
                        if k >= 2:
                            dve.wait_ge(sems["xT_ps"], k - 1)
                    normalize(step[1:], out, x[:, b, :]).then_inc(sems["pre_norm"], 1)
                elif what in ("max0", "max1"):
                    _, l, b = step
                    half = int(what[-1])
                    unit = (f"scores{half}", l, b)
                    dve.wait_ge(sems["scores"], read_count(unit))
                    dve.tensor_reduce(neg_max[par(l, b)][:, 8 * half:8 * half + 8], split3(unit_of(unit), 8),
                                      AX.X, ALU.max, negate=True).then_inc(sems["max"], 1)
                elif what == "max_split":
                    _, l, b = step
                    k = attn_ordinal(l, b)
                    dve.wait_ge(sems["max"], n_attn(l) + (b + 1) * (1 if l == 3 else 2))
                    if k >= 2:
                        dve.wait_ge(sems["maxT"], k - 1)
                    heads = 128 // HEAD_DIM[l] // 4
                    m = split3(neg_max[k % 2][:, 0:4 * heads], 4)
                    to = max_parts[k % 2].rearrange("p (s j r) -> p s j r", s=4, j=heads)
                    r = 3 * (128 // heads) // 4
                    if l == 3 and b < 2:
                        chain(dve.memset(max_parts[k % 2].bitcast(F32), 0.0))
                    chain(dve.tensor_copy(to[:, :, :, r], m))
                    dve.tensor_tensor(to[:, :, :, r + 1], m, to[:, :, :, r].bitcast(F32), ALU.subtract).then_inc(
                        sems["max_split"], 1)
                elif what == "max_merge":
                    _, l, b = step
                    k = attn_ordinal(l, b)
                    dve.wait_ge(sems["maxT"], k + 1)
                    if b == 0:
                        dve.wait_ge(sems["clear_queries"], l + 1)
                    else:
                        dve.wait_ge(sems["expscores"], n_attn(l) + b * (1 if l == 3 else 2))
                    for j in first_heads(l):
                        r = rows(l, j)
                        last = dve.tensor_copy(blocks(query_blocks, l)[r, :, j, :],
                                               split3(small_of(("maxT", l, b)), 4)[r, :, :])
                    last.then_inc(sems["max_merge"], 1)
                elif what == "mix_norm":
                    _, l, b = step
                    k = attn_ordinal(l, b)
                    d = HEAD_DIM[l]
                    heads = 128 // d
                    got = small_of(("mixT", l, b))[:, 0:4 * 32 * (heads // 4)].rearrange(
                        "p (s j r) -> p j s r", s=4, r=32)
                    dve.wait_ge(sems["mixT"], k + 1)
                    if k >= 2:
                        dve.wait_ge(sems["mix_norm"], k - 1)
                    r4 = recip[k % 2][:, 0:heads].rearrange("p (j s) -> p j s", s=4)
                    chain(dve.reciprocal(r4, got[:, :, :, d]))
                    if l == 0 and b >= 2:
                        dve.wait_ge(sems[f"shuffled{b % 2}"], 16 * (b // 2))
                    elif l == 1 and b < 2:
                        dve.wait_ge(sems[f"shuffled{b % 2}"], 16 * (B // 2))
                    elif l > 0:
                        dve.wait_ge(sems["oT_ps"], k - 1)
                    dve.tensor_tensor(mixed[k % 2].rearrange("p (j s d) -> p j s d", s=4, d=d), got[:, :, :, 0:d],
                                      r4.unsqueeze(3).to_broadcast([128, heads // 4, 4, d]),
                                      ALU.mult).then_inc(sems["mix_norm"], 1)
                elif what == "residual":
                    _, l, b = step
                    k = ordinal[step]
                    dve.wait_ge(sems["out"], k + 1)
                    got = small_of(("out", l, b))[:, 0:128]
                    if l < 3:
                        dve.tensor_tensor(x[:, b, :], x[:, b, :], got, ALU.add).then_inc(sems["residual"], 1)
                    else:
                        dve.tensor_tensor(cross_sum[b % 2], x1[:, b, :], got, ALU.add).then_inc(sems["residual"], 1)
                elif what == "cross_stats":
                    _, l, b = step
                    dve.wait_ge(sems["residual"], ordinal[("residual", l, b)] + 1)
                    statistics(("cross", b), cross_sum[b % 2])
                elif what == "cross_norm":
                    _, l, b = step
                    normalize(("cross", b), x2[:, b, :], cross_sum[b % 2]).then_inc(sems["cross_plain"], 1)
                elif what == "self_dot":
                    _, l, b = step
                    s = self_s[b % 2]
                    dve.wait_ge(sems["self_copy"], b + 1)
                    qkv = self_qkv[b % 2]
                    chain(dve.tensor_tensor(self_prod, qkv[:, 0:128], qkv[:, 128:256], ALU.mult))
                    chain(dve.tensor_reduce(s[:, 0:1], self_prod, AX.X, ALU.add))
                    chain(dve.tensor_scalar(s[:, 1:2], s[:, 0:1], SELF_SCALE, None, ALU.mult))
                    dve.tensor_scalar(s[:, 2:3], s[:, 1:2], -1.0, None, ALU.mult).then_inc(sems["self_dot"], 1)
                elif what == "self_value":
                    _, l, b = step
                    s = self_s[b % 2]
                    dve.wait_ge(sems["self_exp"], b + 1)
                    chain(dve.reciprocal(s[:, 4:5], s[:, 3:4]))
                    if b >= 2:
                        dve.wait_ge(sems["vT_ps"], b - 1)
                    dve.tensor_scalar(self_v[b % 2], self_qkv[b % 2][:, 256:384], s[:, 3:4], s[:, 4:5],
                                      ALU.mult, ALU.mult).then_inc(sems["self_value"], 1)
                elif what == "mid_stats":
                    _, l, b = step
                    dve.wait_ge(sems["self_out"], b + 1)
                    dve.tensor_tensor(mid_sum[b % 2], tgt[:, b, :], small_of(("self_out", l, b))[:, 0:128],
                                      ALU.add).then_inc(sems["self_residual"], 1)
                    dve.wait_ge(sems["self_residual"], b + 1)
                    statistics(("mid", b), mid_sum[b % 2])
                elif what == "mid_norm":
                    _, l, b = step
                    normalize(("mid", b), x1[:, b, :], mid_sum[b % 2]).then_inc(sems["mid_plain"], 1)
                elif what == "final_stats":
                    _, l, n = step
                    dve.wait_ge(sems["merged"], ordinal[("merge", DENSE, n)] + 1)
                    statistics(("final", n), *(final_sum[:, 4 * n + j, :] for j in range(4)))
                elif what == "final_norm":
                    _, l, n = step
                    four = final_sum[:, 4 * n:4 * n + 4, :]
                    for j in range(4):
                        last = normalize(("final", n), four[:, j, :], four[:, j, :], j)
                    chain(last)
                    gain, offset = (norms[:, p, :].unsqueeze(1).to_broadcast([128, 4, 128]) for p in (4, 5))
                    chain(dve.tensor_tensor(four, four, gain, ALU.mult))
                    chain(dve.tensor_tensor(four, four, offset, ALU.add))
                    tiles = x[:, 4 * n:4 * n + 4, :]
                    dve.tensor_tensor(tiles, tiles, four, ALU.add).then_inc(sems["final_sum"], 1)
                elif what == "last_stats":
                    _, l, n = step
                    dve.wait_ge(sems["final_sum"], n + 1)
                    statistics(("last", n), *(x[:, 4 * n + j, :] for j in range(4)))
                elif what == "last_norm":
                    _, l, n = step
                    first = ordinal[("fT", 3, 4 * n)]
                    dve.wait_ge(sems["fT_ps"], first)
                    for j in range(4):
                        normalize(("last", n), norm_f[(first + j) % 4], x[:, 4 * n + j, :], j).then_inc(
                            sems["post_norm"], 1)
                elif what == "post_stats":
                    _, l, b = step
                    dve.wait_ge(sems["residual"], ordinal[("residual", l, b)] + 1)
                    statistics(("post", l, b), x[:, b, :])
                elif what == "post_norm":
                    _, l, b = step
                    k = ordinal[step]
                    if k >= 4:
                        dve.wait_ge(sems["fT_ps"], k - 3)
                    normalize(("post", l, b), norm_f[k % 4], x[:, b, :]).then_inc(sems["post_norm"], 1)
                elif what == "logits":
                    _, l, b = step
                    dve.wait_ge(sems["logits"], ordinal[step] + 1)
                    if l and b == 0:
                        dve.wait_ge(sems["share_parts"], l)
                    dve.tensor_copy(logits[:, b, :], small_of(step)[:, 0:8]).then_inc(sems["logits_copy"], 1)
                    dve.wait_ge(sems["logits_copy"], ordinal[step] + 1)
                    chain(dve.max(top[:, b, :], logits[:, b, :]))
                    dve.max_index(top_at[:, b, :], top[:, b, :], logits[:, b, :]).then_inc(sems["topped"], 1)
                elif what == "route":
                    l = step[1]
                    k = ordinal[step]
                    dve.wait_ge(sems["topped"], B * (k + 1))
                    width = 8 if TOP_K[l] == 1 else 2
                    scores = logits if width == 8 else top
                    dve.tensor_tensor(route_diff[:, :, 0:width], scores[:, :, 0:width],
                                      top[:, :, 0:1].to_broadcast([128, B, width]), ALU.subtract).then_inc(
                        sems["route_diff"], 1)
                    chain(dve.tensor_copy(top_atf[:, :, 0:2], top_at[:, :, 0:2]))
                    chain(dve.tensor_tensor(hot, iota.unsqueeze(1).unsqueeze(1).to_broadcast([128, B, 2, 8]),
                                            top_atf[:, :, 0:2].unsqueeze(3).to_broadcast([128, B, 2, 8]),
                                            ALU.is_equal))
                    dve.wait_ge(sems["route_exp"], k + 1)
                    chain(dve.tensor_reduce(route_sum, route_exp[:, :, 0:width], AX.X, ALU.add))
                    if MOE_SCALE[l] != 1.0:
                        chain(dve.tensor_scalar(route_sum, route_sum, 1.0 / MOE_SCALE[l], None, ALU.mult))
                    chain(dve.reciprocal(route_r, route_sum))
                    if TOP_K[l] == 1:
                        chain(dve.tensor_tensor(share, hot[:, :, 0, :], route_r.unsqueeze(2).to_broadcast([128, B, 8]),
                                                ALU.mult))
                    else:
                        chain(dve.tensor_tensor(hot, hot,
                                                route_exp[:, :, 0:2].unsqueeze(3).to_broadcast([128, B, 2, 8]),
                                                ALU.mult))
                        for i in range(2):
                            last = dve.tensor_tensor(hot[:, :, i, :], hot[:, :, i, :],
                                                     route_r.unsqueeze(2).to_broadcast([128, B, 8]), ALU.mult)
                        chain(last)
                        chain(dve.tensor_tensor(share, hot[:, :, 0, :], hot[:, :, 1, :], ALU.add))
                    if l == 0:
                        chain(dve.memset(share[:, :, 7:8], 1.0))
                    if k:
                        dve.wait_ge(sems["shareT"], k)
                    chain(dve.tensor_copy(share_parts[:, :, 0:8], share))
                    dve.tensor_tensor(share_parts[:, :, 8:16], share, share_parts[:, :, 0:8].bitcast(F32),
                                      ALU.subtract).then_inc(sems["share_parts"], 1)
                elif what == "shareT":
                    k = ordinal[step]
                    dve.wait_ge(sems["shareT"], k + 1)
                    dve.tensor_tensor(split3(share_rows, B),
                                      small_of(step)[:, 0:128].unsqueeze(1).to_broadcast([128, B, 128]),
                                      const[:, TILE:TILE + 8].unsqueeze(2).to_broadcast([128, B, 128]),
                                      ALU.mult).then_inc(sems["share_rows"], 1)
                elif what == "up":
                    _, kind, e, n, c = step
                    k, j = ordinal[step], local_chunk(kind, e, n, c)
                    if GATED[kind]:
                        dve.wait_ge(sems["plain_up"], k + 1)
                        dve.wait_ge(sems["activated"], k + 1)
                        if j >= 3:
                            dve.wait_ge(sems["hidden_lo"], k - 2)
                        dve.tensor_tensor(hid[j % 3], gate[j % 3], bank((2 * j + 1) % 4), ALU.mult).then_inc(
                            sems["hidden"], 1)
                elif what == "hidden_split":
                    _, kind, e, n, c = step
                    k, j = chunk_ordinal(kind, e, n, c), local_chunk(kind, e, n, c)
                    y = ordinal[("down", kind, e, n)]
                    hi = hid_hi[y % 2][:, 512 * c:512 * c + 512]
                    if y >= 2:
                        dve.wait_ge(sems["down"], y - 1)
                    if last_mix(kind, e, n) is not None:
                        dve.wait_ge(sems["mix"], last_mix(kind, e, n))
                    if on_act(step):
                        dve.wait_ge(sems["hidden_hi"], act_highs.index(step) + 1)
                    else:
                        dve.wait_ge(sems["activated"], k + 1)
                        chain(dve.tensor_copy(hi, hid[j % 3]))
                    dve.tensor_tensor(hid_lo[y % 2][:, 512 * c:512 * c + 512], hid[j % 3], hi.bitcast(F32),
                                      ALU.subtract).then_inc(sems["hidden_lo"], 1)
                elif what == "add_expert":
                    _, kind, e, n = step
                    y = ordinal[step]
                    dve.wait_ge(sems["down"], y + 1)
                    got = small_of(("down", *step[1:]))
                    total = expert_sum[:, 512 * n:512 * n + 512]
                    if e == 0 and (kind != 0):
                        order = (0, 1, 2, DENSE, 3)
                        dve.wait_ge(sems["merge"], ordinal[("merge", order[order.index(kind) - 1], n)] + 1)
                    if kind == DENSE:
                        dve.tensor_scalar(total, got, out_bias[:, 8:9], None, ALU.add).then_inc(
                            sems["add_expert"], 1)
                        continue
                    k = ordinal[("weigh", *step[1:])]
                    dve.wait_ge(sems["weigh_copy"], k + 1)
                    if e == 0:
                        to = total
                    else:
                        to = weighed[sum_count(step) % 2]
                        if sum_count(step) > 2:
                            dve.wait_ge(sems["summed"], sum_count(step) - 2)
                    if kind == 2:
                        dve.scalar_tensor_tensor(to, got, out_bias[:, e:e + 1], weight[k % 2], ALU.add,
                                                 ALU.mult).then_inc(sems["add_expert"], 1)
                    else:
                        dve.tensor_tensor(to, weight[k % 2], got, ALU.mult).then_inc(sems["add_expert"], 1)
                elif what == "merge":
                    _, kind, n = step
                    dve.wait_ge(sems["merge"], ordinal[step] + 1)
                    got = split3(small_of(step), 4)
                    if kind == DENSE:
                        dve.tensor_tensor(final_sum[:, 4 * n:4 * n + 4, :], x2[:, 4 * n:4 * n + 4, :], got, ALU.add).then_inc(
                            sems["merged"], 1)
                    else:
                        tiles = x[:, 4 * n:4 * n + 4, :]
                        dve.tensor_tensor(tiles, tiles, got, ALU.add).then_inc(sems["merged"], 1)

        @block.tensor
        def _(pe):
            def product(out, left, right, row=None, start=True, stop=True):
                (lh, ll), (rh, rl) = left, right
                if row is not None:
                    pe.matmul(out, *row, start=start, stop=False, skip_group_check=True)
                    start = False
                pe.matmul(out, lh, rh, start=start, stop=False, skip_group_check=True)
                pe.matmul(out, lh, rl, start=False, stop=False, skip_group_check=True)
                return pe.matmul(out, ll, rh, start=False, stop=stop, skip_group_check=True)

            def cut(pair, a, z):
                return pair[0][:, a:z], pair[1][:, a:z]

            def free_small(step):
                before = small_before[step]
                if before is not None:
                    pe.wait_ge(sems[READ[before[0]]], read_count(before))

            def free_unit(step):
                i = unit_at[step]
                if i >= 2:
                    before = units[i - 2]
                    pe.wait_ge(sems[READ[before[0]]], read_count(before))

            def bias_rows(l, a, z):
                return bias[32 * l:32 * l + 2, a:z]

            def ones_rows(l):
                return ones[32 * l:32 * l + 2, 0:128]

            def token_row(l, a, z):
                return ones_rows(l), bias_rows(l, a, z)

            def mask_of(l, b):
                return {0: mask0, 1: mask1[:, b, :], 2: mask2}[l]

            pe.wait_ge(sems["constants"], 2)
            pe.wait_ge(sems["context_lo"], 1)
            pe.wait_ge(sems["const_rows"], 2)
            pe.wait_ge(sems["loads_const"], 16)
            for step in steps:
                what = step[0]
                if what in TRANSPOSES:
                    _, l, b = step
                    src, sem, value = source(*step)
                    pe.wait_ge(sems[sem], value)
                    free_small(step)
                    pe.transpose(small_of(step)[:, 0:128], src, ident).then_inc(sems[f"{what}_ps"], 1)
                elif what == "query":
                    _, l, pair, part = step
                    pe.wait_ge(sems["xT_lo"], ordinal[("xT", l, 2 * pair + 1)] + 1)
                    free_small(step)
                    to = split3(small_of(step), 2)
                    for i in range(2):
                        a = QC + 128 * (2 * part + i)
                        row = (bias_rows(l, a, a + 128), ones[32 * l:32 * l + 2, 0:256]) if l in (0, 3) else None
                        last = product(to[:, i, :], cut(att[l], a, a + 128), turned["xT"][pair % 2], row)
                    last.then_inc(sems["query"], 1)
                elif what == "key":
                    _, l, s, n = step
                    if l == 1 and s == 0 and n == 0:
                        pe.wait_ge(sems["loads_mask"], 48)
                    if s == 0 and n == 0:
                        pe.wait_ge(sems["weights_split"], split_count(("attention", l)))
                    free_small(step)
                    a = KC + 128 * s
                    product(small_of(step), cut(att[l], a, a + 128), cut(ctx, 512 * n, 512 * n + 512),
                            (bias_rows(l, a, a + 128),
                             ones[32 * l:32 * l + 2, 0:256].unsqueeze(1).to_broadcast([2, 2, 256]))).then_inc(sems["key"], 1)
                elif what == "value":
                    _, l, b = step
                    free_small(step)
                    product(small_of(step)[:, 0:128], cut(ctx, S * b, S * b + S), cut(att[l], VC, VC + 128),
                            token_row(l, VC, VC + 128) if l != 1 else None).then_inc(sems["value"], 1)
                elif what in ("scores0", "scores1"):
                    _, l, b = step
                    half = int(what[-1])
                    pe.wait_ge(sems["query_split"], 2 * (l * (B // 2) + b // 2 + 1))
                    pe.wait_ge(sems["key_block"], attn_ordinal(l, b) + 1)
                    pe.wait_ge(sems["key_block_rest"], attn_ordinal(l, b) + 1)
                    if l == 1 and b == 0:
                        pe.wait_ge(sems["masks"], 1)
                    free_unit(step)
                    q, k = queries(l, b), blocks(key_blocks, l)
                    slots = range(2 * half, 2 * half + 2) if l < 3 else range(4)
                    to = split3(unit_of(step), len(slots))
                    for i, s in enumerate(slots):
                        if l < 3:
                            pe.matmul(to[:, i], ident16, mask_of(l, b).unsqueeze(1).to_broadcast([128, 4, 128]),
                                      start=True, stop=False, skip_group_check=True)
                        last = pe.matmul(to[:, i], q[:, s, :], k[:, s, :, :], start=(l == 3), stop=True,
                                         skip_group_check=True)
                    last.then_inc(sems["scores"], 1)
                elif what == "maxT":
                    _, l, b = step
                    k = attn_ordinal(l, b)
                    pe.wait_ge(sems["max_split"], k + 1)
                    free_small(step)
                    to, parts_ = split3(small_of(step), 4), split3(max_parts[k % 2], 4)
                    pe.matmul(to, ident_r, queries(l, b), start=True, stop=False, skip_group_check=True)
                    for s in range(4):
                        last = pe.matmul(to[:, s, :], parts_[:, s, :], ident_r, start=False, stop=True,
                                         skip_group_check=True)
                    last.then_inc(sems["maxT"], 1)
                elif what in ("expscores0", "expscores1"):
                    _, l, b = step
                    half = int(what[-1])
                    pe.wait_ge(sems["max_merge_rest"], attn_ordinal(l, b) + 1)
                    free_unit(step)
                    q, k = blocks(query_blocks, l), key_stack[:, :, S * b:S * b + S]
                    slots = range(2 * half, 2 * half + 2) if l < 3 else range(4)
                    to = split3(unit_of(step), len(slots))
                    for i, s in enumerate(slots):
                        if l < 3:
                            pe.matmul(to[:, i], mask_of(l, b), ident16.unsqueeze(1).to_broadcast([128, 4, 128]),
                                      start=True, stop=False, skip_group_check=True)
                        last = pe.matmul(to[:, i], k[:, s, :], q[:, s, :, :], start=(l == 3), stop=True,
                                         skip_group_check=True)
                    last.then_inc(sems["expscores"], 1)
                elif what == "mix":
                    _, l, b = step
                    k = attn_ordinal(l, b)
                    d = HEAD_DIM[l]
                    heads = 128 // d
                    pe.wait_ge(sems["exp"], n_attn(l) + (b + 1) * (1 if l == 3 else 2))
                    pe.wait_ge(sems["value_copy"], k + 1)
                    free_small(step)
                    p = split3(probs[k % 2], 16)
                    v = split3((values3 if l == 3 else values)[k % 2], heads)
                    for h in range(heads):
                        j, s = divmod(h, 4)
                        last = pe.matmul(small_of(step)[32 * j:32 * j + 32, 128 * s:128 * s + 128], v[:, h, :],
                                         p[:, heads // 4 * s + j, :], start=True, stop=True, skip_group_check=True)
                    last.then_inc(sems["mix"], 1)
                elif what == "mixT":
                    _, l, b = step
                    pe.wait_ge(sems["mix_copy"], attn_ordinal(l, b) + 1)
                    free_small(step)
                    r = 128 if l < 3 else 64
                    for s in range(4):
                        last = pe.transpose(small_of(step)[:, r * s:r * s + r],
                                            mix_rows[0:r, 128 * s:128 * s + 128], ident[0:r, 0:r])
                    last.then_inc(sems["mixT"], 1)
                elif what == "out":
                    _, l, b = step
                    k = ordinal[("oT", l, b)]
                    pe.wait_ge(sems["oT_lo"], k + 1)
                    free_small(step)
                    product(small_of(step)[:, 0:128], turned["oT"][k % 2], cut(att[l], OC, OC + 128),
                            token_row(l, OC, OC + 128)).then_inc(sems["out"], 1)
                elif what == "self_qkv":
                    _, l, b = step
                    pe.wait_ge(sems["tT_lo"], b + 1)
                    free_small(step)
                    product(small_of(step)[:, 0:384], turned["tT"][b % 2], cut(att[3], QKVC, QKVC + 384),
                            token_row(3, QKVC, QKVC + 384)).then_inc(sems["self_qkv"], 1)
                elif what == "self_out":
                    _, l, b = step
                    pe.wait_ge(sems["vT_lo"], b + 1)
                    free_small(step)
                    product(small_of(step)[:, 0:128], turned["vT"][b % 2], cut(att[3], SOC, SOC + 128),
                            token_row(3, SOC, SOC + 128)).then_inc(sems["self_out"], 1)
                elif what == "logits":
                    _, l, b = step
                    pe.wait_ge(sems["fT_lo"], B * l + b + 1)
                    free_small(step)
                    product(small_of(step)[:, 0:8], cut(ffn_in, S * b, S * b + S), cut(att[l], RC, RC + 8),
                            token_row(l, RC, RC + 8)).then_inc(sems["logits"], 1)
                elif what == "shareT":
                    k = ordinal[step]
                    pe.wait_ge(sems["share_parts"], k + 1)
                    free_small(step)
                    pe.matmul(small_of(step)[:, 0:128], share_parts.rearrange("p b r -> p (b r)"), ident_r,
                              start=True, stop=True).then_inc(sems["shareT"], 1)
                elif what == "weigh":
                    _, kind, e, n = step
                    pe.wait_ge(sems["share_rows"], ordinal[("shareT", kind)] + 1)
                    free_small(step)
                    pe.matmul(small_of(step), pick[:, e:e + 1].to_broadcast([128, 128]), share_rows[:, 512 * n:512 * n + 512],
                              start=True, stop=True).then_inc(sems["weigh"], 1)
                elif what == "merge":
                    _, kind, n = step
                    if kind == DENSE:
                        pe.wait_ge(sems["add_expert"], ordinal[("down", DENSE, 0, n)] + 1)
                    else:
                        pe.wait_ge(sems["summed"], sum_count(("add_expert", kind, EXPERTS - 1, n)))
                    free_small(step)
                    to = split3(small_of(step), 4)
                    for i in range(4):
                        a = 512 * n + 128 * i
                        last = pe.transpose(to[:, i, :], expert_sum[:, a:a + 128], ident)
                    last.then_inc(sems["merge"], 1)
                elif what == "up":
                    _, kind, e, n, c = step
                    k, j = ordinal[step], local_chunk(kind, e, n, c)
                    hi, lo = exp_w[EXPERT_LIST.index((kind, e)) % 2]
                    if n == 0 and c == 0:
                        item = ("expert", EXPERT_LIST.index((kind, e)))
                        pe.wait_ge(sems["weights_split"], split_count(item, up_parts(item) - 1))
                    if e == 0 and c == 0:
                        if kind == DENSE:
                            pe.wait_ge(sems["yT_lo"], 4 * n + 4)
                        else:
                            pe.wait_ge(sems["fT_lo"], B * kind + 4 * n + 4)
                    if j == 0:
                        if kind != 3:
                            l = 3 if kind == DENSE else kind
                            pe.wait_ge(sems["exp"], n_attn(l) + B * (1 if l == 3 else 2))
                    tokens = cut(ffn_in, 512 * n, 512 * n + 512)
                    width = 128 * CHUNKS[kind]
                    if GATED[kind]:
                        if j >= 2:
                            pe.wait_ge(sems["activated"], k - 1)
                        product(bank(2 * j % 4), cut((hi, lo), 128 * c, 128 * c + 128), tokens).then_inc(
                            sems["gate_up"], 1)
                        if j >= 2:
                            pe.wait_ge(sems["hidden"], k - 1)
                        product(bank((2 * j + 1) % 4), cut((hi, lo), width + 128 * c, width + 128 * c + 128),
                                tokens).then_inc(sems["plain_up"], 1)
                    else:
                        if j >= 4:
                            pe.wait_ge(sems["activated"], k - 3)
                        product(bank(j % 4), cut((hi, lo), 128 * c, 128 * c + 128), tokens).then_inc(
                            sems["gate_up"], 1)
                elif what in ("down", "down_part"):
                    kind, e, n = step[1:4]
                    c = step[4] if what == "down_part" else CHUNKS[kind] - 1
                    whole = ("down", kind, e, n)
                    y = ordinal[whole]
                    hi, lo = exp_w[EXPERT_LIST.index((kind, e)) % 2]
                    base = 128 * CHUNKS[kind] * (2 if GATED[kind] else 1)
                    pe.wait_ge(sems["hidden_lo"], chunk_ordinal(kind, e, n, c) + 1)
                    if n == 0 and c == 0:
                        pe.wait_ge(sems["weights_split"], split_count(("expert", EXPERT_LIST.index((kind, e)))))
                    if c == 0:
                        free_small(whole)
                    w = cut((hi, lo), base + 128 * c, base + 128 * c + 128)
                    h = cut((hid_hi[y % 2], hid_lo[y % 2]), 512 * c, 512 * c + 512)
                    last = product(small_of(whole), w, h, start=(c == 0), stop=(what == "down"))
                    if what == "down":
                        last.then_inc(sems["down"], 1)


def _stack_columns(w, d):
    j = 32 // d
    w = w.reshape(*w.shape[:-1], j, 4, d)
    w = np.moveaxis(w, -2, -3)
    out = np.zeros((*w.shape[:-1], 4, d), np.float32)
    out[..., 0:3, :] = w[..., None, :]
    return out.reshape(*w.shape[:-3], 512)


def _constants():
    const = np.zeros((128, CONST_COLS), np.float32)
    const[:, IDENT:IDENT + 128] = np.eye(128)
    r = np.arange(128)
    const[:, LAM + LAM_Q] = np.where((r // 8) % 4 == 2, -1.0, 0.0)
    const[:, LAM + LAM_K] = np.where((r // 8) % 4 == 1, -1.0, 0.0)
    const[:, LAM + LAM_Q3] = np.where((r // 16) % 4 == 2, -1.0, 0.0)
    const[:, LAM + LAM_K3] = np.where((r // 16) % 4 == 1, -1.0, 0.0)
    const[:, LAM + LAM_ROW] = np.where(r % 32 == 1, -1.0, 0.0)
    const[:, IOTA:IOTA + 8] = np.arange(8)
    const[:, PICK:PICK + 8] = r[:, None] % 8 == np.arange(8)
    const[:, TILE:TILE + 8] = r[:, None] // 16 == np.arange(8)
    q, k = r[:, None], r[None, :]
    const[:, MASKS:MASKS + 128] = np.where(k <= q, 0, MASKED)
    strict = k < q
    strict[0, 0] = True
    const[:, MASKS + 128:MASKS + 256] = np.where(strict, 0, MASKED)
    return const


def _down_rows(w):
    return w.reshape(-1, 128, 128).transpose(1, 0, 2).reshape(128, -1)


def kernel(**inputs):
    import concourse.bacc as _bacc
    from concourse.bass_utils import run_bass_kernel_spmd as _run

    g = {k: np.asarray(v) for k, v in inputs.items()}
    x = g["x"].transpose(1, 0, 2).reshape(128, B * D)
    ctx = g["ctx_1024"].transpose(2, 0, 1).reshape(128, B * S)
    mask = g["mask_Bx1xSxS2_ik1"][:, 0].transpose(1, 0, 2).reshape(128, B * S)

    def diagonal(w):
        out = np.zeros((128, 128), np.float32)
        for h in range(16):
            out[8 * h:8 * h + 8, 8 * h:8 * h + 8] = w.T
        return out

    def router(w):
        out = np.zeros((128, 8), np.float32)
        out[:, :w.shape[1]] = w
        return out

    wq3, wk3, wv3 = np.split(g["L3_xattn_in_proj_w"], 3, axis=0)
    bq3, bk3, bv3 = np.split(g["L3_xattn_in_proj_b"], 3)
    att_parts = [
        [(g["L0_xattn_w_q"]), (g["L0_xattn_w_k"]), g["L0_xattn_w_v"], g["L0_xattn_w_o"], router(g["L0_ffn_wr"].T)],
        [diagonal(g["L1_xattn_Wq"]), diagonal(g["L1_xattn_Wk"]), diagonal(g["L1_xattn_Wv"]), g["L1_xattn_Wo"].T,
         router(g["L1_ffn_Wr"])],
        [g["L2_xattn_Wq"].T, g["L2_xattn_Wk"].T, g["L2_xattn_Wv"].T, g["L2_xattn_Wo"].T, router(g["L2_ffn_gate_w"])],
        [wq3.T, wk3.T, wv3.T, g["L3_xattn_mha_out_w"].T, router(g["L3_ffn_router_w"].T), g["L3_xattn_qkv_w"].T,
         g["L3_xattn_sa_out_w"].T],
    ]
    arrays = {}
    for l, p in enumerate(att_parts):
        p = [_stack_columns(p[0], HEAD_DIM[l]), _stack_columns(p[1], HEAD_DIM[l]), *p[2:]]
        arrays[f"att{l}"] = np.ascontiguousarray(np.concatenate(p, axis=1))
    bias = np.zeros((128, BIAS_COLS), np.float32)
    for r in range(2):
        bias[r, QC:QC + 512] = _stack_columns(g["L0_xattn_b_q"], 8)
        bias[r, KC:KC + 512] = _stack_columns(g["L0_xattn_b_k"], 8)
        bias[r, VC:VC + 128] = g["L0_xattn_b_v"]
        bias[r, OC:OC + 128] = g["L0_xattn_b_o"]
        bias[r, RC:RC + 7] = g["L0_ffn_rb"]
        bias[r, RC + 7] = MASKED
        bias[32 + r, OC:OC + 128] = g["L1_xattn_bo"]
        bias[64 + r, VC:VC + 128] = g["L2_xattn_bv"]
        bias[64 + r, OC:OC + 128] = g["L2_xattn_bo"]
        bias[64 + r, RC:RC + 8] = g["L2_ffn_gate_b"]
        bias[96 + r, QC:QC + 512] = _stack_columns(bq3, 16)
        bias[96 + r, KC:KC + 512] = _stack_columns(bk3, 16)
        bias[96 + r, VC:VC + 128] = bv3
        bias[96 + r, OC:OC + 128] = g["L3_xattn_mha_out_b"]
        bias[96 + r, QKVC:QKVC + 384] = g["L3_xattn_qkv_b"]
        bias[96 + r, SOC:SOC + 128] = g["L3_xattn_sa_out_b"]
    for l, d in enumerate(HEAD_DIM):
        ones = bias[32 * l:32 * l + 2, KC:KC + 512].reshape(2, 4, 32 // d, 4, d)
        ones[..., 3, 0:2] = 1
    hidden_bias = np.concatenate([g["L2_ffn_b1"].reshape(32, 128).T, g["L3_xattn_lin1_b"].reshape(4, 128).T,
                                  g["L2_ffn_b2"].T, g["L3_xattn_lin2_b"][:, None]], axis=1)
    norm = np.stack([g[f"L3_xattn_ln{i}_{p}"] for i in (1, 2, 3) for p in "gb"])
    norm = np.broadcast_to(norm[None], (128, 6, 128)).reshape(128, 768)

    def swiglu(gate, up, down):
        out = np.zeros((128, 3, 384), np.float32)
        out[:, 0, :gate.shape[0]] = gate.T
        out[:, 1, :up.shape[0]] = up.T
        rows = np.zeros((384, 128), np.float32)
        rows[:down.shape[1]] = down.T
        out[:, 2] = _down_rows(rows)
        return out.reshape(128, 1152)

    e0 = [swiglu(g["L0_ffn_rg"][e], g["L0_ffn_ru"][e], g["L0_ffn_rd"][e]) for e in range(7)]
    e0.append(swiglu(g["L0_ffn_sg"], g["L0_ffn_su"], g["L0_ffn_sd"]))
    arrays["exp0"] = np.stack(e0)
    arrays["exp1"] = np.stack([np.concatenate([g["L1_ffn_Wg"][e], g["L1_ffn_Wu"][e], _down_rows(g["L1_ffn_Wd"][e])],
                                              axis=1) for e in range(8)])
    arrays["exp2"] = np.stack([np.concatenate([g["L2_ffn_w1"][e], _down_rows(g["L2_ffn_w2"][e])], axis=1)
                               for e in range(8)])
    arrays["expdense"] = np.concatenate([g["L3_xattn_lin1_w"].T, _down_rows(g["L3_xattn_lin2_w"].T)], axis=1)[None]
    arrays["exp3"] = np.stack([np.concatenate([g["L3_ffn_w1"][e], _down_rows(g["L3_ffn_w2"][e])], axis=1)
                               for e in range(8)])
    const = _constants()
    arrays.update(x_in=x, ctx_in=ctx, mask_in=mask, bias_in=bias, hidden_bias_in=hidden_bias, norm_in=norm,
                  const_in=const)

    nc = _bacc.Bacc("TRN2", target_bir_lowering=False, num_devices=1)
    arrays = {k: np.ascontiguousarray(v) for k, v in arrays.items()}
    dram = {k: nc.dram_tensor(k, v.shape, mybir.dt.from_np(v.dtype), kind="ExternalInput").ap()
            for k, v in arrays.items()}
    out = nc.dram_tensor("x_out", (128, B * D), F32, kind="ExternalOutput").ap()
    fused_layers(nc, dram["x_in"], dram["ctx_in"], dram["mask_in"], [dram[f"att{l}"] for l in range(LAYERS)],
                 {k: dram[f"exp{k}"] for k in (0, 1, 2, DENSE, 3)}, dram["bias_in"], dram["hidden_bias_in"],
                 dram["norm_in"], dram["const_in"], out)
    r = _run(nc, [arrays], core_ids=[0])
    return np.ascontiguousarray(r.results[0]["x_out"].reshape(128, B, D).transpose(1, 0, 2))
```
